# Optimizing a Trainium2 kernel written in Bass

```python
import numpy as np
import jax
import jax.numpy as jnp

def _softmax(x, axis=-1):
    return jax.nn.softmax(x, axis=axis)

def _gelu(x):
    return jax.nn.gelu(x, approximate=True)

def _silu(x):
    return jax.nn.silu(x)

def _sigmoid(x):
    return jax.nn.sigmoid(x)

def _layernorm(x, axis=-1, eps=1e-05):
    m = jnp.mean(x, axis=axis, keepdims=True)
    v = jnp.var(x, axis=axis, keepdims=True)
    return (x - m) / jnp.sqrt(v + eps)

def _scatter_add(tgt, idx, src, axis=0):
    return tgt.at[idx].add(src)

def _segment_sum(src, seg, n):
    return jax.ops.segment_sum(src, seg, n)
kernel_name = 'mk_flamingo_gated_d4_seqx_r8_5a6b1c'

def setup_inputs(seed: int=0):
    np.random.seed(seed)
    _w = jnp.asarray

    def _rec_inputs():
        import jax
        import jax.numpy as jnp
        _rk = jax.random.key(seed)
        x = -0.0003929 + 0.9999 * jax.random.normal(jax.random.fold_in(_rk, 1), (8, 56, 256), jnp.float32)
        _lenS = 56 - jax.random.randint(jax.random.fold_in(_rk, 7), (8,), 0, max(1, 56 // 4) + 1, jnp.int32)
        _lenS2 = 1500 - jax.random.randint(jax.random.fold_in(_rk, 8), (8,), 0, max(1, 1500 // 4) + 1, jnp.int32)
        _ctx_2048P = jax.random.normal(jax.random.fold_in(_rk, 11), (8, 16, 256), jnp.float32)
        _ctx_2048c = jax.random.dirichlet(jax.random.fold_in(_rk, 511), 0.3 * jnp.ones((16,), jnp.float32), (8, 1500))
        _ctx_2048t = jnp.einsum('bsk,bkd->bsd', _ctx_2048c, _ctx_2048P)
        _ctx_2048t = _ctx_2048t * jax.lax.rsqrt(jnp.mean(jnp.square(_ctx_2048t)) + 1e-12) * 0.953939
        ctx_2048 = -0.000514642 + 1.00011 * (_ctx_2048t + 0.3 * jax.random.normal(jax.random.fold_in(_rk, 611), (8, 1500, 256), jnp.float32))
        _validS = jnp.arange(56)[None, :] < _lenS[:, None]
        _validS2 = jnp.arange(1500)[None, :] < _lenS2[:, None]
        _causal = jnp.tril(jnp.ones((56, 56), dtype=bool))
        mask_BxS2_ik0 = jnp.where(jnp.broadcast_to(_validS2[:, :], (8, 1500)), 0, 1).astype(jnp.int32)
        mask_BxS2_bf1 = jnp.ones((8, 1500), dtype=bool)
        _g = jax.random.normal(jax.random.fold_in(_rk, 9001), (2, 4), jnp.float32)
        _g = jnp.sign(_g) * jnp.maximum(jnp.abs(_g), 1.0) + (_g == 0) * 1.0
        g_xattn = _g[0]
        g_ffn = _g[1]
        return (x, ctx_2048, mask_BxS2_ik0, mask_BxS2_bf1, g_xattn, g_ffn)
    x, ctx_2048, mask_BxS2_ik0, mask_BxS2_bf1, g_xattn, g_ffn = _rec_inputs()

    def _L0_xattn_setup():
        import jax, jax.numpy as jnp
        import numpy as np
        import math
        H = 256
        NH = 16
        HD = H // NH
        EPS_LN = 1e-05
        RES_SCALE_MAX = 0.3

        def _nan_clean(x, lim=10000.0):
            return jnp.nan_to_num(x, nan=0.0, posinf=lim, neginf=-lim)
        key = jax.random.key(seed)
        ks = jax.random.split(key, 12)
        B, S, T = (4, 256, 32)
        std = 1.0 / math.sqrt(H)
        return {'hidden_states': jax.random.normal(ks[0], (B, S, H), jnp.float32), 'audio_tokens': jax.random.normal(ks[1], (B, T, H), jnp.float32), 'attention_mask': jax.random.randint(ks[2], (B, T), 0, 2, jnp.int32), 'Wq': jax.random.normal(ks[3], (H, H), jnp.float32) * std, 'bq': jnp.zeros((H,), jnp.float32), 'Wk': jax.random.normal(ks[4], (H, H), jnp.float32) * std, 'bk': jnp.zeros((H,), jnp.float32), 'Wv': jax.random.normal(ks[5], (H, H), jnp.float32) * std, 'bv': jnp.zeros((H,), jnp.float32), 'Wo': jax.random.normal(ks[6], (H, H), jnp.float32) * std, 'bo': jnp.zeros((H,), jnp.float32), 'ln_gamma': jnp.ones((H,), jnp.float32), 'ln_beta': jnp.zeros((H,), jnp.float32), 'residual_scale': jnp.float32(0.05)}
    _L0_xattn_all = _L0_xattn_setup()
    _L0_xattn_in = {k: v for k, v in _L0_xattn_all.items() if k in ('Wq', 'bq', 'Wk', 'bk', 'Wv', 'bv', 'Wo', 'bo', 'ln_gamma', 'ln_beta', 'residual_scale')}
    del _L0_xattn_all

    def _L0_ffn_setup():
        import jax, jax.numpy as jnp
        import numpy as np
        TOP_K = 2

        def moe_forward(x, w_gate_router, w_gate_proj, w_up_proj, w_down_proj):
            E = w_gate_router.shape[0]
            scores = jnp.einsum('bsd,ed->bse', x, w_gate_router)
            topk_scores, topk_idx = jax.lax.top_k(scores, TOP_K)
            topk_probs = jax.nn.softmax(topk_scores, axis=-1)
            weights = jnp.sum(topk_probs[..., None] * jax.nn.one_hot(topk_idx, E, dtype=x.dtype), axis=-2)
            gate = jnp.einsum('bsd,efd->bsef', x, w_gate_proj)
            up = jnp.einsum('bsd,efd->bsef', x, w_up_proj)
            hidden = jax.nn.silu(gate) * up
            out = jnp.einsum('bsef,edf,bse->bsd', hidden, w_down_proj, weights)
            return out
        key = jax.random.key(seed)
        k1, k2, k3, k4, k5 = jax.random.split(key, 5)
        B, S, D, E, F = (2, 128, 256, 8, 96)
        scale_in = 1.0 / np.sqrt(D)
        scale_ff = 1.0 / np.sqrt(F)
        return {'x': jax.random.normal(k1, (B, S, D), dtype=jnp.float32), 'w_gate_router': jax.random.normal(k2, (E, D), dtype=jnp.float32) * scale_in, 'w_gate_proj': jax.random.normal(k3, (E, F, D), dtype=jnp.float32) * scale_in, 'w_up_proj': jax.random.normal(k4, (E, F, D), dtype=jnp.float32) * scale_in, 'w_down_proj': jax.random.normal(k5, (E, D, F), dtype=jnp.float32) * scale_ff}
    _L0_ffn_all = _L0_ffn_setup()
    _L0_ffn_in = {k: v for k, v in _L0_ffn_all.items() if k in ('w_gate_router', 'w_gate_proj', 'w_up_proj', 'w_down_proj')}
    del _L0_ffn_all

    def _L1_xattn_setup():
        import jax, jax.numpy as jnp
        import numpy as np
        import math
        D_MODEL = 256
        N_Q_HEADS = 16
        N_KV_HEADS = 4
        HEAD_DIM = D_MODEL // N_Q_HEADS
        B = 4
        S = 128

        def _alibi_slopes(num_heads):
            n = 2 ** int(math.floor(math.log2(num_heads)))
            m0 = 2.0 ** (-8.0 / n)
            return m0 ** jnp.arange(1, n + 1, dtype=jnp.float32)
        key = jax.random.key(seed)
        ks = jax.random.split(key, 8)
        xavier = lambda k, fi, fo: jax.random.normal(k, (fi, fo), jnp.float32) * math.sqrt(2.0 / (fi + fo))
        return {'query': jax.random.normal(ks[0], (B, S, D_MODEL), jnp.float32), 'key': jax.random.normal(ks[1], (B, S, D_MODEL), jnp.float32), 'value': jax.random.normal(ks[2], (B, S, D_MODEL), jnp.float32), 'mask': jnp.ones((B, S), dtype=bool), 'Wq': xavier(ks[3], D_MODEL, N_Q_HEADS * HEAD_DIM), 'Wk': xavier(ks[4], D_MODEL, N_KV_HEADS * HEAD_DIM), 'Wv': xavier(ks[5], D_MODEL, N_KV_HEADS * HEAD_DIM), 'Wo': xavier(ks[6], D_MODEL, D_MODEL)}
    _L1_xattn_all = _L1_xattn_setup()
    _L1_xattn_in = {k: v for k, v in _L1_xattn_all.items() if k in ('Wq', 'Wk', 'Wv', 'Wo')}
    del _L1_xattn_all

    def _L1_ffn_setup():
        import jax, jax.numpy as jnp
        import numpy as np
        E, TOP_K, H, I = (32, 8, 256, 96)
        B, S = (1, 256)
        key = jax.random.key(seed)
        ks = jax.random.split(key, 5)
        scale = 0.02
        return {'hidden_states': jax.random.normal(ks[0], (B, S, H), dtype=jnp.float32), 'gate_w': jax.random.normal(ks[1], (E, H), dtype=jnp.float32) * scale, 'Wg': jax.random.normal(ks[2], (E, I, H), dtype=jnp.float32) * scale, 'Wu': jax.random.normal(ks[3], (E, I, H), dtype=jnp.float32) * scale, 'Wd': jax.random.normal(ks[4], (E, H, I), dtype=jnp.float32) * scale}
    _L1_ffn_all = _L1_ffn_setup()
    _L1_ffn_in = {k: v for k, v in _L1_ffn_all.items() if k in ('gate_w', 'Wg', 'Wu', 'Wd')}
    del _L1_ffn_all

    def _L2_xattn_setup():
        import jax, jax.numpy as jnp
        import numpy as np
        EPS = 1e-06
        NUM_HEADS = 16

        def _feature_map(x):
            return jnp.where(x > 0, x + 1.0, jnp.exp(x))
        key = jax.random.key(seed)
        ks = jax.random.split(key, 7)
        B, L, S, D = (4, 512, 512, 256)
        sc = 1.0 / np.sqrt(D)
        return {'query': jax.random.normal(ks[0], (B, L, D), jnp.float32), 'kv': jax.random.normal(ks[1], (B, S, D), jnp.float32), 'Wq': jax.random.normal(ks[2], (D, D), jnp.float32) * sc, 'Wg': jax.random.normal(ks[3], (D, D), jnp.float32) * sc, 'bg': jnp.ones((D,), jnp.float32), 'Wkv': jax.random.normal(ks[4], (2 * D, D), jnp.float32) * sc, 'Wo': jax.random.normal(ks[5], (D, D), jnp.float32) * sc}
    _L2_xattn_all = _L2_xattn_setup()
    _L2_xattn_in = {k: v for k, v in _L2_xattn_all.items() if k in ('Wq', 'Wg', 'bg', 'Wkv', 'Wo')}
    del _L2_xattn_all

    def _L2_ffn_setup():
        import jax, jax.numpy as jnp
        import numpy as np
        E = 8
        TOP_K = 2
        D = 256
        DE = 176
        DS = 352
        B, S = (2, 256)
        key = jax.random.key(seed)
        ks = jax.random.split(key, 8)
        std = 0.02
        return {'x': jax.random.normal(ks[0], (B, S, D), jnp.float32), 'W_router': jax.random.normal(ks[1], (D, E), jnp.float32) * std, 'We_gate': jax.random.normal(ks[2], (E, D, DE), jnp.float32) * std, 'We_up': jax.random.normal(ks[3], (E, D, DE), jnp.float32) * std, 'We_down': jax.random.normal(ks[4], (E, DE, D), jnp.float32) * std, 'Ws_gate': jax.random.normal(ks[5], (D, DS), jnp.float32) * std, 'Ws_up': jax.random.normal(ks[6], (D, DS), jnp.float32) * std, 'Ws_down': jax.random.normal(ks[7], (DS, D), jnp.float32) * std}
    _L2_ffn_all = _L2_ffn_setup()
    _L2_ffn_in = {k: v for k, v in _L2_ffn_all.items() if k in ('W_router', 'We_gate', 'We_up', 'We_down', 'Ws_gate', 'Ws_up', 'Ws_down')}
    del _L2_ffn_all

    def _L3_xattn_setup():
        import jax, jax.numpy as jnp
        import numpy as np
        D_MODEL = 256
        NUM_HEADS = 16
        HEAD_DIM = D_MODEL // NUM_HEADS

        def _fq_sym(x, axis):
            s = jnp.max(jnp.abs(x), axis=axis, keepdims=True) / 127.0
            s = jnp.maximum(s, 1e-08)
            q = jnp.clip(jnp.round(x / s), -127.0, 127.0) * s
            return x + jax.lax.stop_gradient(q - x)

        def _fq_unsigned(x, axis):
            s = jnp.max(x, axis=axis, keepdims=True) / 255.0
            s = jnp.maximum(s, 1e-08)
            q = jnp.clip(jnp.round(x / s), 0.0, 255.0) * s
            return x + jax.lax.stop_gradient(q - x)
        key = jax.random.key(seed)
        ks = jax.random.split(key, 8)
        B, N, M, C = (2, 256, 64, D_MODEL)
        return {'x': jax.random.normal(ks[0], (B, N, C), jnp.float32), 'cond': jax.random.normal(ks[1], (B, M, C), jnp.float32), 'Wq': jax.random.normal(ks[2], (C, C), jnp.float32) * 0.02, 'bq': jnp.zeros((C,), jnp.float32), 'Wkv': jax.random.normal(ks[3], (C, 2 * C), jnp.float32) * 0.02, 'bkv': jnp.zeros((2 * C,), jnp.float32), 'Wp': jax.random.normal(ks[4], (C, C), jnp.float32) * 0.02, 'bp': jnp.zeros((C,), jnp.float32)}
    _L3_xattn_all = _L3_xattn_setup()
    _L3_xattn_in = {k: v for k, v in _L3_xattn_all.items() if k in ('Wq', 'bq', 'Wkv', 'bkv', 'Wp', 'bp')}
    del _L3_xattn_all

    def _L3_ffn_setup():
        import jax, jax.numpy as jnp
        import numpy as np
        B, S, D, F, E, SH, K = (2, 256, 256, 128, 16, 2, 2)

        def _experts_all(x, g, gb, w1, b1, w2, b2):
            y = jax.nn.gelu(jnp.einsum('bsd,edf->bsef', x, g) + gb, approximate=False)
            y = y * (jnp.einsum('bsd,edf->bsef', x, w1) + b1)
            return jnp.einsum('bsef,efd->bsed', y, w2) + b2
        key = jax.random.key(seed)
        ks = jax.random.split(key, 8)
        std = 0.02
        mk = lambda k, sh: jax.random.normal(k, sh, jnp.float32) * std
        return {'x': jax.random.normal(ks[0], (B, S, D), jnp.float32), 'wa': mk(ks[1], (D, E)), 'rg': mk(ks[2], (E, D, F)), 'rgb': jnp.zeros((E, F), jnp.float32), 'rw1': mk(ks[3], (E, D, F)), 'rb1': jnp.zeros((E, F), jnp.float32), 'rw2': mk(ks[4], (E, F, D)), 'rb2': jnp.zeros((E, D), jnp.float32), 'sg': mk(ks[5], (SH, D, F)), 'sgb': jnp.zeros((SH, F), jnp.float32), 'sw1': mk(ks[6], (SH, D, F)), 'sb1': jnp.zeros((SH, F), jnp.float32), 'sw2': mk(ks[7], (SH, F, D)), 'sb2': jnp.zeros((SH, D), jnp.float32)}
    _L3_ffn_all = _L3_ffn_setup()
    _L3_ffn_in = {k: v for k, v in _L3_ffn_all.items() if k in ('wa', 'rg', 'rgb', 'rw1', 'rb1', 'rw2', 'rb2', 'sg', 'sgb', 'sw1', 'sb1', 'sw2', 'sb2')}
    del _L3_ffn_all
    return {'x': x, 'ctx_2048': ctx_2048, 'mask_BxS2_ik0': mask_BxS2_ik0, 'mask_BxS2_bf1': mask_BxS2_bf1, 'g_xattn': g_xattn, 'g_ffn': g_ffn, 'L0_xattn_Wq': _L0_xattn_in['Wq'], 'L0_xattn_bq': _L0_xattn_in['bq'], 'L0_xattn_Wk': _L0_xattn_in['Wk'], 'L0_xattn_bk': _L0_xattn_in['bk'], 'L0_xattn_Wv': _L0_xattn_in['Wv'], 'L0_xattn_bv': _L0_xattn_in['bv'], 'L0_xattn_Wo': _L0_xattn_in['Wo'], 'L0_xattn_bo': _L0_xattn_in['bo'], 'L0_xattn_ln_gamma': _L0_xattn_in['ln_gamma'], 'L0_xattn_ln_beta': _L0_xattn_in['ln_beta'], 'L0_xattn_residual_scale': _L0_xattn_in['residual_scale'], 'L0_ffn_w_gate_router': _L0_ffn_in['w_gate_router'], 'L0_ffn_w_gate_proj': _L0_ffn_in['w_gate_proj'], 'L0_ffn_w_up_proj': _L0_ffn_in['w_up_proj'], 'L0_ffn_w_down_proj': _L0_ffn_in['w_down_proj'], 'L1_xattn_Wq': _L1_xattn_in['Wq'], 'L1_xattn_Wk': _L1_xattn_in['Wk'], 'L1_xattn_Wv': _L1_xattn_in['Wv'], 'L1_xattn_Wo': _L1_xattn_in['Wo'], 'L1_ffn_gate_w': _L1_ffn_in['gate_w'], 'L1_ffn_Wg': _L1_ffn_in['Wg'], 'L1_ffn_Wu': _L1_ffn_in['Wu'], 'L1_ffn_Wd': _L1_ffn_in['Wd'], 'L2_xattn_Wq': _L2_xattn_in['Wq'], 'L2_xattn_Wg': _L2_xattn_in['Wg'], 'L2_xattn_bg': _L2_xattn_in['bg'], 'L2_xattn_Wkv': _L2_xattn_in['Wkv'], 'L2_xattn_Wo': _L2_xattn_in['Wo'], 'L2_ffn_W_router': _L2_ffn_in['W_router'], 'L2_ffn_We_gate': _L2_ffn_in['We_gate'], 'L2_ffn_We_up': _L2_ffn_in['We_up'], 'L2_ffn_We_down': _L2_ffn_in['We_down'], 'L2_ffn_Ws_gate': _L2_ffn_in['Ws_gate'], 'L2_ffn_Ws_up': _L2_ffn_in['Ws_up'], 'L2_ffn_Ws_down': _L2_ffn_in['Ws_down'], 'L3_xattn_Wq': _L3_xattn_in['Wq'], 'L3_xattn_bq': _L3_xattn_in['bq'], 'L3_xattn_Wkv': _L3_xattn_in['Wkv'], 'L3_xattn_bkv': _L3_xattn_in['bkv'], 'L3_xattn_Wp': _L3_xattn_in['Wp'], 'L3_xattn_bp': _L3_xattn_in['bp'], 'L3_ffn_wa': _L3_ffn_in['wa'], 'L3_ffn_rg': _L3_ffn_in['rg'], 'L3_ffn_rgb': _L3_ffn_in['rgb'], 'L3_ffn_rw1': _L3_ffn_in['rw1'], 'L3_ffn_rb1': _L3_ffn_in['rb1'], 'L3_ffn_rw2': _L3_ffn_in['rw2'], 'L3_ffn_rb2': _L3_ffn_in['rb2'], 'L3_ffn_sg': _L3_ffn_in['sg'], 'L3_ffn_sgb': _L3_ffn_in['sgb'], 'L3_ffn_sw1': _L3_ffn_in['sw1'], 'L3_ffn_sb1': _L3_ffn_in['sb1'], 'L3_ffn_sw2': _L3_ffn_in['sw2'], 'L3_ffn_sb2': _L3_ffn_in['sb2']}

def reference(x, ctx_2048, mask_BxS2_ik0, mask_BxS2_bf1, g_xattn, g_ffn, L0_xattn_Wq, L0_xattn_bq, L0_xattn_Wk, L0_xattn_bk, L0_xattn_Wv, L0_xattn_bv, L0_xattn_Wo, L0_xattn_bo, L0_xattn_ln_gamma, L0_xattn_ln_beta, L0_xattn_residual_scale, L0_ffn_w_gate_router, L0_ffn_w_gate_proj, L0_ffn_w_up_proj, L0_ffn_w_down_proj, L1_xattn_Wq, L1_xattn_Wk, L1_xattn_Wv, L1_xattn_Wo, L1_ffn_gate_w, L1_ffn_Wg, L1_ffn_Wu, L1_ffn_Wd, L2_xattn_Wq, L2_xattn_Wg, L2_xattn_bg, L2_xattn_Wkv, L2_xattn_Wo, L2_ffn_W_router, L2_ffn_We_gate, L2_ffn_We_up, L2_ffn_We_down, L2_ffn_Ws_gate, L2_ffn_Ws_up, L2_ffn_Ws_down, L3_xattn_Wq, L3_xattn_bq, L3_xattn_Wkv, L3_xattn_bkv, L3_xattn_Wp, L3_xattn_bp, L3_ffn_wa, L3_ffn_rg, L3_ffn_rgb, L3_ffn_rw1, L3_ffn_rb1, L3_ffn_rw2, L3_ffn_rb2, L3_ffn_sg, L3_ffn_sgb, L3_ffn_sw1, L3_ffn_sb1, L3_ffn_sw2, L3_ffn_sb2):
    import jax
    import jax.numpy as jnp

    def _L0_xattn_ref(hidden_states, audio_tokens, attention_mask, Wq, bq, Wk, bk, Wv, bv, Wo, bo, ln_gamma, ln_beta, residual_scale):
        import jax, jax.numpy as jnp
        import numpy as np
        import math
        H = 256
        NH = 16
        HD = H // NH
        EPS_LN = 1e-05
        RES_SCALE_MAX = 0.3

        def _nan_clean(x, lim=10000.0):
            return jnp.nan_to_num(x, nan=0.0, posinf=lim, neginf=-lim)
        B, S, _ = hidden_states.shape
        T = audio_tokens.shape[1]
        hs = _nan_clean(hidden_states).astype(jnp.float32)
        at = _nan_clean(audio_tokens).astype(jnp.float32)

        def proj(x, W, b, L):
            y = x @ W.T + b
            return y.reshape(B, L, NH, HD).transpose(0, 2, 1, 3)
        q = _nan_clean(proj(hs, Wq, bq, S))
        k = _nan_clean(proj(at, Wk, bk, T))
        v = _nan_clean(proj(at, Wv, bv, T))
        scale = max(math.sqrt(HD), 1e-08)
        scores = jnp.einsum('bhsd,bhtd->bhst', q, k) / scale
        scores = jnp.clip(scores, -50.0, 50.0)
        scores = jnp.nan_to_num(scores, nan=0.0, posinf=50.0, neginf=-50.0)
        attend = (attention_mask.astype(jnp.float32) > 0.5)[:, None, None, :]
        scores = jnp.where(attend, scores, -10000.0)
        scores = jnp.clip(scores, -50.0, 50.0)
        probs = jax.nn.softmax(scores, axis=-1)
        probs = jnp.nan_to_num(probs, nan=0.0, posinf=1.0, neginf=0.0)
        probs = probs / (probs.sum(axis=-1, keepdims=True) + 1e-08)
        ctx = jnp.einsum('bhst,bhtd->bhsd', probs, v)
        ctx = ctx.transpose(0, 2, 1, 3).reshape(B, S, H)
        delta = _nan_clean(ctx @ Wo.T + bo)
        rs = jnp.clip(residual_scale, 0.0, RES_SCALE_MAX)
        delta = rs * delta
        mu = delta.mean(axis=-1, keepdims=True)
        var = jnp.mean((delta - mu) ** 2, axis=-1, keepdims=True)
        delta = (delta - mu) / jnp.sqrt(var + EPS_LN) * ln_gamma + ln_beta
        return delta

    def _L0_ffn_ref(x, w_gate_router, w_gate_proj, w_up_proj, w_down_proj):
        import jax, jax.numpy as jnp
        import numpy as np
        TOP_K = 2

        def moe_forward(x, w_gate_router, w_gate_proj, w_up_proj, w_down_proj):
            E = w_gate_router.shape[0]
            scores = jnp.einsum('bsd,ed->bse', x, w_gate_router)
            topk_scores, topk_idx = jax.lax.top_k(scores, TOP_K)
            topk_probs = jax.nn.softmax(topk_scores, axis=-1)
            weights = jnp.sum(topk_probs[..., None] * jax.nn.one_hot(topk_idx, E, dtype=x.dtype), axis=-2)
            gate = jnp.einsum('bsd,efd->bsef', x, w_gate_proj)
            up = jnp.einsum('bsd,efd->bsef', x, w_up_proj)
            hidden = jax.nn.silu(gate) * up
            out = jnp.einsum('bsef,edf,bse->bsd', hidden, w_down_proj, weights)
            return out
        return moe_forward(x, w_gate_router, w_gate_proj, w_up_proj, w_down_proj)

    def _L1_xattn_ref(query, key, value, mask, Wq, Wk, Wv, Wo):
        import jax, jax.numpy as jnp
        import numpy as np
        import math
        D_MODEL = 256
        N_Q_HEADS = 16
        N_KV_HEADS = 4
        HEAD_DIM = D_MODEL // N_Q_HEADS
        B = 4
        S = 128

        def _alibi_slopes(num_heads):
            n = 2 ** int(math.floor(math.log2(num_heads)))
            m0 = 2.0 ** (-8.0 / n)
            return m0 ** jnp.arange(1, n + 1, dtype=jnp.float32)
        b, q_len, d = query.shape
        kv_len = key.shape[1]
        G = N_KV_HEADS
        Hpg = N_Q_HEADS // G
        dh = HEAD_DIM
        Q = (query @ Wq).reshape(b, q_len, G, Hpg, dh)
        K = (key @ Wk).reshape(b, kv_len, G, dh)
        V = (value @ Wv).reshape(b, kv_len, G, dh)
        Q = Q / math.sqrt(dh)
        scores = jnp.einsum('bqghd,bkgd->bghqk', Q, K)
        rel = jnp.arange(kv_len, dtype=jnp.float32)[None, :] - jnp.arange(q_len, dtype=jnp.float32)[:, None]
        m = _alibi_slopes(N_Q_HEADS).reshape(1, G, Hpg, 1, 1)
        scores = scores + m * rel[None, None, None]
        neg = jnp.finfo(scores.dtype).min
        scores = jnp.where(mask[:, None, None, None, :], scores, neg)
        w = jax.nn.softmax(scores, axis=-1)
        out = jnp.einsum('bghqk,bkgd->bqghd', w, V)
        out = out.reshape(b, q_len, G * Hpg * dh)
        return out @ Wo

    def _L1_ffn_ref(hidden_states, gate_w, Wg, Wu, Wd):
        import jax, jax.numpy as jnp
        import numpy as np
        E, TOP_K, H, I = (32, 8, 256, 96)
        B, S = (1, 256)
        b, s, h = hidden_states.shape
        x = hidden_states.reshape(-1, h)
        T = x.shape[0]
        router_logits = x @ gate_w.T
        probs = jax.nn.softmax(router_logits.astype(jnp.float32), axis=-1)
        top_vals, top_idx = jax.lax.top_k(probs, TOP_K)
        top_vals = top_vals / jnp.sum(top_vals, axis=-1, keepdims=True)
        top_vals = top_vals.astype(hidden_states.dtype)
        routing_matrix = jnp.zeros_like(router_logits).at[jnp.arange(T)[:, None], top_idx].set(top_vals)
        g = jnp.einsum('th,eih->eti', x, Wg)
        u = jnp.einsum('th,eih->eti', x, Wu)
        expert_out = jnp.einsum('eti,ehi->eth', jax.nn.silu(g) * u, Wd)
        out = jnp.einsum('te,eth->th', routing_matrix, expert_out)
        return out.reshape(b, s, h)

    def _L2_xattn_ref(query, kv, Wq, Wg, bg, Wkv, Wo):
        import jax, jax.numpy as jnp
        import numpy as np
        EPS = 1e-06
        NUM_HEADS = 16

        def _feature_map(x):
            return jnp.where(x > 0, x + 1.0, jnp.exp(x))
        B, L, D = query.shape
        S = kv.shape[1]
        H = NUM_HEADS
        hd = D // H
        q = query @ Wq.T
        gate = jax.nn.sigmoid(query @ Wg.T + bg)
        kvp = kv @ Wkv.T
        k, v = jnp.split(kvp, 2, axis=-1)
        q = _feature_map(q.reshape(B, L, H, hd).transpose(0, 2, 1, 3))
        k = _feature_map(k.reshape(B, S, H, hd).transpose(0, 2, 1, 3))
        v = v.reshape(B, S, H, hd).transpose(0, 2, 1, 3)
        kv_summary = jnp.einsum('bhsd,bhse->bhde', k, v)
        k_sum = k.sum(axis=-2)
        z = 1.0 / (jnp.einsum('bhld,bhd->bhl', q, k_sum)[..., None] + EPS)
        attn = jnp.einsum('bhld,bhde->bhle', q, kv_summary) * z
        attn = attn.transpose(0, 2, 1, 3).reshape(B, L, D)
        out = attn * gate @ Wo.T
        return out

    def _L2_ffn_ref(x, W_router, We_gate, We_up, We_down, Ws_gate, Ws_up, Ws_down):
        import jax, jax.numpy as jnp
        import numpy as np
        E = 8
        TOP_K = 2
        D = 256
        DE = 176
        DS = 352
        B, S = (2, 256)
        b, s, d = x.shape
        shared = jax.nn.silu(x @ Ws_gate) * (x @ Ws_up) @ Ws_down
        scores = jax.nn.softmax(x @ W_router, axis=-1)
        topk_vals, topk_idx = jax.lax.top_k(scores, TOP_K)
        onehot = jax.nn.one_hot(topk_idx, E, dtype=x.dtype)
        combine = jnp.einsum('bsk,bske->bse', topk_vals, onehot)
        combine = combine.reshape(b * s, E)
        xf = x.reshape(b * s, d)
        h = jax.nn.silu(jnp.einsum('td,edh->eth', xf, We_gate)) * jnp.einsum('td,edh->eth', xf, We_up)
        y_all = jnp.einsum('eth,ehd->etd', h, We_down)
        routed = jnp.einsum('etd,te->td', y_all, combine)
        return routed.reshape(b, s, d) + shared

    def _L3_xattn_ref(x, cond, Wq, bq, Wkv, bkv, Wp, bp):
        import jax, jax.numpy as jnp
        import numpy as np
        D_MODEL = 256
        NUM_HEADS = 16
        HEAD_DIM = D_MODEL // NUM_HEADS

        def _fq_sym(x, axis):
            s = jnp.max(jnp.abs(x), axis=axis, keepdims=True) / 127.0
            s = jnp.maximum(s, 1e-08)
            q = jnp.clip(jnp.round(x / s), -127.0, 127.0) * s
            return x + jax.lax.stop_gradient(q - x)

        def _fq_unsigned(x, axis):
            s = jnp.max(x, axis=axis, keepdims=True) / 255.0
            s = jnp.maximum(s, 1e-08)
            q = jnp.clip(jnp.round(x / s), 0.0, 255.0) * s
            return x + jax.lax.stop_gradient(q - x)
        B, N, C = x.shape
        H, hd = (NUM_HEADS, HEAD_DIM)
        q = (x @ Wq + bq).reshape(1, B * N, H, hd)
        kv = (cond @ Wkv + bkv).reshape(1, -1, 2, H, hd)
        k, v = (kv[:, :, 0], kv[:, :, 1])
        scale = 1.0 / np.sqrt(hd).astype(np.float32)
        q = jnp.transpose(q * scale, (0, 2, 1, 3))
        k = jnp.transpose(k, (0, 2, 1, 3))
        v = jnp.transpose(v, (0, 2, 1, 3))
        q = _fq_sym(q, axis=-1)
        k = _fq_sym(k, axis=-1)
        v = _fq_sym(v, axis=2)
        attn = jnp.einsum('bhqd,bhkd->bhqk', q, k)
        attn = jax.nn.softmax(attn.astype(jnp.float32), axis=-1)
        attn = _fq_unsigned(attn, axis=-1)
        out = jnp.einsum('bhqk,bhkd->bhqd', attn, v)
        out = jnp.transpose(out, (0, 2, 1, 3)).reshape(B, N, C)
        return out @ Wp + bp

    def _L3_ffn_ref(x, wa, rg, rgb, rw1, rb1, rw2, rb2, sg, sgb, sw1, sb1, sw2, sb2):
        import jax, jax.numpy as jnp
        import numpy as np
        B, S, D, F, E, SH, K = (2, 256, 256, 128, 16, 2, 2)

        def _experts_all(x, g, gb, w1, b1, w2, b2):
            y = jax.nn.gelu(jnp.einsum('bsd,edf->bsef', x, g) + gb, approximate=False)
            y = y * (jnp.einsum('bsd,edf->bsef', x, w1) + b1)
            return jnp.einsum('bsef,efd->bsed', y, w2) + b2
        aff = jax.nn.sigmoid(jnp.einsum('bsd,de->bse', x, wa))
        topk_p, topk_i = jax.lax.top_k(aff, K)
        topk_p = topk_p / jnp.sum(topk_p, axis=-1, keepdims=True)
        combine = jnp.sum(jax.nn.one_hot(topk_i, E, dtype=x.dtype) * topk_p[..., None], axis=2)
        routed = jnp.einsum('bsed,bse->bsd', _experts_all(x, rg, rgb, rw1, rb1, rw2, rb2), combine)
        shared = jnp.sum(_experts_all(x, sg, sgb, sw1, sb1, sw2, sb2), axis=2)
        return x + shared + routed
    x = x + jnp.tanh(g_xattn[0]) * _L0_xattn_ref(_layernorm(x, axis=-1), ctx_2048, mask_BxS2_ik0, L0_xattn_Wq, L0_xattn_bq, L0_xattn_Wk, L0_xattn_bk, L0_xattn_Wv, L0_xattn_bv, L0_xattn_Wo, L0_xattn_bo, L0_xattn_ln_gamma, L0_xattn_ln_beta, L0_xattn_residual_scale)
    x = x + jnp.tanh(g_ffn[0]) * _L0_ffn_ref(_layernorm(x, axis=-1), L0_ffn_w_gate_router, L0_ffn_w_gate_proj, L0_ffn_w_up_proj, L0_ffn_w_down_proj)
    x = x + jnp.tanh(g_xattn[1]) * _L1_xattn_ref(_layernorm(x, axis=-1), ctx_2048, ctx_2048, mask_BxS2_bf1, L1_xattn_Wq, L1_xattn_Wk, L1_xattn_Wv, L1_xattn_Wo)
    x = x + jnp.tanh(g_ffn[1]) * _L1_ffn_ref(_layernorm(x, axis=-1), L1_ffn_gate_w, L1_ffn_Wg, L1_ffn_Wu, L1_ffn_Wd)
    x = x + jnp.tanh(g_xattn[2]) * _L2_xattn_ref(_layernorm(x, axis=-1), ctx_2048, L2_xattn_Wq, L2_xattn_Wg, L2_xattn_bg, L2_xattn_Wkv, L2_xattn_Wo)
    x = x + jnp.tanh(g_ffn[2]) * _L2_ffn_ref(_layernorm(x, axis=-1), L2_ffn_W_router, L2_ffn_We_gate, L2_ffn_We_up, L2_ffn_We_down, L2_ffn_Ws_gate, L2_ffn_Ws_up, L2_ffn_Ws_down)
    x = x + jnp.tanh(g_xattn[3]) * _L3_xattn_ref(_layernorm(x, axis=-1), ctx_2048, L3_xattn_Wq, L3_xattn_bq, L3_xattn_Wkv, L3_xattn_bkv, L3_xattn_Wp, L3_xattn_bp)
    x = x + jnp.tanh(g_ffn[3]) * _L3_ffn_ref(_layernorm(x, axis=-1), L3_ffn_wa, L3_ffn_rg, L3_ffn_rgb, L3_ffn_rw1, L3_ffn_rb1, L3_ffn_rw2, L3_ffn_rb2, L3_ffn_sg, L3_ffn_sgb, L3_ffn_sw1, L3_ffn_sb1, L3_ffn_sw2, L3_ffn_sb2)
    return x

_drawn_inputs = setup_inputs


def setup_inputs(seed=0):
    import zlib

    import numpy as np

    out = dict(_drawn_inputs(seed))
    spreads = {'L0_xattn_bq': (0.0, 0.1),
     'L0_xattn_bk': (0.0, 2.0),
     'L0_xattn_bv': (0.0, 0.1),
     'L0_xattn_bo': (0.0, 0.1),
     'L0_xattn_ln_gamma': (1.0, 0.2),
     'L0_xattn_ln_beta': (0.0, 0.1),
     'L2_xattn_bg': (1.0, 0.6),
     'L3_xattn_bq': (0.0, 0.8),
     'L3_xattn_bkv': (0.0, 0.56),
     'L3_xattn_bp': (0.0, 0.1),
     'L3_ffn_rgb': (0.0, 0.8),
     'L3_ffn_rb1': (0.0, 0.8),
     'L3_ffn_rb2': (0.0, 2.0),
     'L3_ffn_sgb': (0.0, 0.8),
     'L3_ffn_sb1': (0.0, 0.8),
     'L3_ffn_sb2': (0.0, 0.8)}
    factors = {'g_ffn': 29.92,
     'L1_ffn_gate_w': 8.0,
     'L1_ffn_Wg': 8.0,
     'L1_ffn_Wu': 8.0,
     'L1_ffn_Wd': 8.0,
     'L2_xattn_Wq': 7.749,
     'L2_ffn_W_router': 8.0,
     'L2_ffn_We_gate': 8.0,
     'L2_ffn_We_up': 8.0,
     'L2_ffn_We_down': 8.0,
     'L2_ffn_Ws_gate': 5.737,
     'L2_ffn_Ws_up': 5.517,
     'L2_ffn_Ws_down': 5.701,
     'L3_xattn_Wq': 8.0,
     'L3_xattn_Wkv': 6.921,
     'L3_xattn_Wp': 3.565,
     'L3_ffn_rg': 8.0,
     'L3_ffn_rw1': 8.0,
     'L3_ffn_rw2': 8.0,
     'L3_ffn_sg': 8.0,
     'L3_ffn_sw1': 8.0,
     'L3_ffn_sw2': 8.0}
    for name, (base, spread) in spreads.items():
        noise = np.random.default_rng([zlib.crc32(name.encode()), seed]).standard_normal(out[name].shape)
        drawn = base * np.exp(spread * noise) if base else spread * noise
        out[name] = jnp.asarray(drawn.astype(out[name].dtype))
    for name, factor in factors.items():
        out[name] = (out[name] * factor).astype(out[name].dtype)
    return out
```

```python
import math
import numpy as np
import concourse.bass as bass
from concourse import mybir
from contextlib import ExitStack

FP32 = mybir.dt.float32
BF16 = mybir.dt.bfloat16
U32 = mybir.dt.uint32
I32 = mybir.dt.int32
U8 = mybir.dt.uint8
ALU = mybir.AluOpType
ACT = mybir.ActivationFunctionType
X_AXIS = mybir.AxisListType.X
XY_AXES = mybir.AxisListType.XY

B, S, D = 8, 56, 256
N_TOK = B * S
TT, NT = 112, 4
T = 1500
KP, KN = 125, 12
KC = 500
H, HD = 16, 16
KT = D // 128
EPS_LN = 1e-5


class Program:

    def __init__(self, nc, dram, out):
        self.nc, self.dram, self.out = nc, dram, out


class Stage:

    def __init__(self, nc, name):
        self.nc, self.name, self.stack, self.semaphores = nc, name, ExitStack(), []

    def sb(self, name, shape, dt=FP32):
        return self.stack.enter_context(self.nc.sbuf_tensor(f"{self.name}_{name}", shape, dt))

    def ps(self, name, shape, dt=FP32):
        return self.stack.enter_context(self.nc.psum_tensor(f"{self.name}_{name}_ps", shape, dt))

    def sem(self, name):
        self.semaphores.append(self.stack.enter_context(self.nc.semaphore(f"{self.name}_{name}")))
        return self.semaphores[-1]

    def sems(self, name, n):
        return [self.sem(f"{name}{k}") for k in range(n)]

    def start_at_one(self, *semaphores):
        flat = list(semaphores)
        while any(isinstance(x, list) for x in flat):
            flat = [y for x in flat for y in (x if isinstance(x, list) else [x])]
        for k, x in enumerate(flat):
            (self.nc.sync, self.nc.gpsimd, self.nc.scalar, self.nc.vector)[k % 4].sem_inc(x, 1)

    def block(self):
        self.programs = ExitStack()
        return self.programs.enter_context(self.nc.Block())

    def __enter__(self):
        return self

    def __exit__(self, *e):
        if self.semaphores:
            self.programs.close()
            numbers = sorted(s.num for s in self.semaphores)
            starts = [a for a in numbers if a - 1 not in numbers]
            ends = [a + 1 for a in numbers if a + 1 not in numbers]
            for start, end in zip(starts, ends):
                self.nc.gpsimd.sem_clear(range(start, end))
            self.nc.all_engine_barrier()
        return self.stack.__exit__(*e)


def in_order(engine, sem, start=0):
    count = [start]

    def link(instruction):
        count[0] += 1
        instruction.then_inc(sem, 1)
        engine.wait_ge(sem, count[0])
        return count[0]
    return link


def setup_stage(P):
    nc = P.nc
    with Stage(nc, "setup") as st:
        loaded, gates_raw_ready = st.sem("loaded"), st.sem("gates_raw_ready")
        raw = st.sb("raw", [128, 9])
        block = st.block()

        @block.sync
        def _(sp):
            sp.dma_start(P.x[:], P.dram["x"].rearrange("(j p) d -> p j d", p=TT)).then_inc(loaded, 16)
            sp.dma_start(P.ident[:], P.dram["ident"]).then_inc(loaded, 16)
            sp.dma_start(P.head_mask[:], P.dram["head_mask"]).then_inc(loaded, 16)
            sp.dma_start(P.iota[:], P.dram["iota"]).then_inc(loaded, 16)
            sp.dma_start(raw[:, 0:4], P.dram["g_xattn"]).then_inc(loaded, 16)
            sp.dma_start(raw[:, 4:8], P.dram["g_ffn"]).then_inc(loaded, 16)
            sp.dma_start(raw[:, 8:9], P.dram["rs"]).then_inc(loaded, 16)
            sp.wait_ge(loaded, 7 * 16)

        @block.scalar
        def _(act):
            act.wait_ge(loaded, 7 * 16)
            nc.scalar.activation(P.gates[:, 0:8], raw[:, 0:8], ACT.Tanh)

        @block.vector
        def _(dve):
            dve.wait_ge(loaded, 7 * 16)
            nc.vector.tensor_scalar(P.gates[:, 8:9], raw[:, 8:9], 0.0, 0.3, ALU.max, ALU.min)
            nc.vector.memset(P.ones[:], 1.0)


def norm_stage(P, k):
    nc = P.nc
    with Stage(nc, f"norm{k}") as st:
        stats = st.sb("stats", [TT, NT, 6])
        mean_var = st.sb("mean_var", [TT, NT, 2])
        var_eps = st.sb("var_eps", [TT, NT])
        std = st.sb("std", [TT, NT])
        rstd = st.sb("rstd", [TT, NT])
        turned = [st.ps(f"turned{c}", [128, 512]) for c in range(KT)]
        dve_step, var_ready, std_ready = st.sem("dve_step"), st.sem("var_ready"), st.sem("std_ready")
        xn_ready, turned_done = st.sem("xn_ready"), st.sems("turned_done", KT)
        block = st.block()

        @block.vector
        def _(dve):
            link = in_order(dve, dve_step)
            for j in range(NT):
                link(nc.vector.bn_stats(stats[:, j, :], P.x[:, j, :]))
            for j in range(NT):
                link(nc.vector.bn_aggr(mean_var[:, j, :], stats[:, j, :]))
            nc.vector.tensor_scalar(var_eps[:], mean_var[:, :, 1], EPS_LN, None, ALU.add).then_inc(var_ready, 1)
            dve.wait_ge(std_ready, 1)
            link(nc.vector.reciprocal(rstd[:], std[:]))
            for j in range(NT):
                nc.vector.tensor_scalar(P.xn[:, j, :], P.x[:, j, :], mean_var[:, j, 0:1], rstd[:, j:j + 1],
                                        ALU.subtract, ALU.mult).then_inc(xn_ready, 1)
            dve.wait_ge(turned_done[0], NT)
            nc.vector.tensor_copy(P.xnT[:, 0, :], turned[0][:, 0:N_TOK])

        @block.scalar
        def _(act):
            act.wait_ge(var_ready, 1)
            nc.scalar.activation(std[:], var_eps[:], ACT.Sqrt).then_inc(std_ready, 1)
            act.wait_ge(turned_done[1], NT)
            nc.scalar.activation(P.xnT[:, 1, :], turned[1][:, 0:N_TOK], ACT.Copy)

        @block.tensor
        def _(pe):
            for j in range(NT):
                pe.wait_ge(xn_ready, j + 1)
                for c in range(KT):
                    nc.tensor.transpose(turned[c][:, j * TT:(j + 1) * TT], P.xn[:, j, c * 128:(c + 1) * 128],
                                        P.ident[0:TT, 0:TT]).then_inc(turned_done[c], 1)


def ffn_stage(P, k, E, n, F, routing, weight_e, biased=False):
    nc, dram = P.nc, P.dram
    with Stage(nc, f"ffn{k}") as st:
        router_w = st.sb("router_w", [128, KT, E])
        n_in = KT * 2 * F + 2 * biased
        w_all = st.sb("w_all", [128, 2, n_in])
        w_in = w_all[:, :, 0:KT * 2 * F].rearrange("p s (c g f) -> p s c g f", c=KT, g=2)
        w_down = st.sb("w_down", [F, 2, D])
        act_g = st.sb("act_g", [F, 2, N_TOK])
        hT = st.sb("hT", [F, 2, N_TOK])
        acc = st.sb("acc", [TT, NT, D])
        logits = st.sb("logits", [TT, NT, E])
        probs = st.sb("probs", [TT, NT, E])
        top = st.sb("top", [TT, NT, 8])
        top_at = st.sb("top_at", [TT, NT, 8], U32)
        top_at_f = st.sb("top_at_f", [TT, NT, 8])
        share = st.sb("share", [TT, NT, 2])
        tmp = st.sb("tmp", [TT, NT, E])
        rowmax = st.sb("rowmax", [TT, NT])
        rowsum = st.sb("rowsum", [TT, NT])
        rowinv = st.sb("rowinv", [TT, NT])
        w_e = st.sb("w_e", [TT, NT, E])
        w_blk = st.sb("w_blk", [TT, NT, n])
        gate_ps = [st.ps(f"gate{s}", [128, 512]) for s in range(2)]
        up_ps = [st.ps(f"up{s}", [128, 512]) for s in range(2)]
        down_ps = [st.ps(f"down{s}", [128, NT, D]) for s in range(2)]
        if biased:
            b_gate, b_up = w_all[0:F, :, n_in - 2:n_in - 1], w_all[0:F, :, n_in - 1:n_in]
            b_down = st.sb("b_down", [n, D])
            w_blkT = st.sb("w_blkT", [n, N_TOK])
        small_loaded = st.sem("small_loaded")
        w_loaded, act_ready, gate_done = st.sems("w_loaded", 2), st.sems("act_ready", 2), st.sems("gate_done", 2)
        up_done, h_ready = st.sems("up_done", 2), st.sems("h_ready", 2)
        down_done, acc_done = st.sems("down_done", 2), st.sems("acc_done", 2)
        router_done, dve_step, logits_ready = st.sem("router_done"), st.sem("dve_step"), st.sem("logits_ready")
        exp_ready, weights_ready = st.sem("exp_ready"), st.sem("weights_ready")
        wT_done, wT_ready, bias_done, acc_ready = (st.sem("wT_done"), st.sem("wT_ready"), st.sem("bias_done"),
                                                   st.sem("acc_ready"))
        st.start_at_one(down_done, h_ready, acc_done)
        block = st.block()
        n_small = 1 + biased

        @block.sync
        def _(sp):
            sp.dma_start(router_w[:], dram[f"f{k}_router"].rearrange("(c p) e -> p c e", p=128)).then_inc(small_loaded, 16)
            if biased:
                sp.dma_start(b_down[:], dram[f"f{k}_b_down"]).then_inc(small_loaded, 16)
            with sp.Fori(0, n // 2) as i:
                for s in range(2):
                    sp.wait_ge(down_done[s], i + 1)
                    sp.dma_start(w_all[:, s, :], dram[f"f{k}_w_in"][bass.ds(2 * i + s, 1)].rearrange("o p m -> p (o m)"))\
                        .then_inc(w_loaded[s], 16)
                    sp.dma_start(w_down[:, s, :], dram[f"f{k}_w_down"][bass.ds(2 * i + s, 1)].rearrange("o f d -> f (o d)"))\
                        .then_inc(w_loaded[s], 16)

        @block.tensor
        def _(pe):
            pe.wait_ge(small_loaded, 16 * n_small)
            for j in range(NT):
                for c in range(KT):
                    last = nc.tensor.matmul(down_ps[0][0:TT, j, 0:E], P.xnT[:, c, j * TT:(j + 1) * TT], router_w[:, c, :],
                                            start=(c == 0), stop=(c == KT - 1))
            last.then_inc(router_done, 1)
            if biased:
                pe.wait_ge(weights_ready, 1)
                for j in range(NT):
                    last = nc.tensor.transpose(down_ps[1][0:n, j, 0:TT], w_blk[:, j, :], P.ident[0:TT, 0:TT])
                last.then_inc(wT_done, 1)
                pe.wait_ge(wT_ready, 1)
                for j in range(NT):
                    last = nc.tensor.matmul(down_ps[0][0:TT, j, :], w_blkT[:, j * TT:(j + 1) * TT], b_down[:],
                                            start=True, stop=True)
                last.then_inc(bias_done, 1)
            pe.wait_ge(acc_ready, 1)
            with pe.Fori(0, n // 2) as i:
                for s in range(2):
                    pe.wait_ge(w_loaded[s], 32 * i + 32)
                    pe.wait_ge(h_ready[s], i + 1)
                    for g, bank, done in ((0, gate_ps[s], gate_done[s]), (1, up_ps[s], up_done[s])):
                        for c in range(KT):
                            last = nc.tensor.matmul(bank[0:F, 0:N_TOK], w_in[:, s, c, g, :], P.xnT[:, c, :],
                                                    start=(c == 0), stop=(c == KT - 1))
                        last.then_inc(done, 1)
                for s in range(2):
                    pe.wait_ge(h_ready[s], i + 2)
                    pe.wait_ge(acc_done[s], i + 1)
                    for j in range(NT):
                        last = nc.tensor.matmul(down_ps[s][0:TT, j, :], hT[:, s, j * TT:(j + 1) * TT], w_down[:, s, :],
                                                start=True, stop=True)
                    last.then_inc(down_done[s], 1)

        @block.scalar
        def _(act):
            act.wait_ge(logits_ready, 1)
            if routing == "softmax_of_top":
                nc.scalar.activation(share[:, :, 1:2], share[:, :, 0:1], ACT.Exp).then_inc(exp_ready, 1)
            elif routing == "sigmoid":
                nc.scalar.activation(probs[:], logits[:], ACT.Sigmoid).then_inc(exp_ready, 1)
            else:
                nc.scalar.activation(probs[:], logits[:], ACT.Exp).then_inc(exp_ready, 1)
            act.wait_ge(small_loaded, 16 * n_small)
            with act.Fori(0, n // 2) as i:
                for s in range(2):
                    act.wait_ge(gate_done[s], i + 1)
                    act.wait_ge(h_ready[s], i + 1)
                    if biased:
                        nc.scalar.activation(act_g[:, s, :], gate_ps[s][0:F, 0:N_TOK], ACT.Gelu,
                                             bias=b_gate[:, s]).then_inc(act_ready[s], 1)
                    else:
                        nc.scalar.activation(act_g[:, s, :], gate_ps[s][0:F, 0:N_TOK], ACT.Silu).then_inc(act_ready[s], 1)

        @block.vector
        def _(dve):
            link = in_order(dve, dve_step)
            dve.wait_ge(router_done, 1)
            link(nc.vector.tensor_copy(logits[:], down_ps[0][0:TT, :, 0:E]))
            if routing == "softmax_of_top":
                ranked = logits
                for j in range(NT):
                    link(nc.vector.max(top[:, j, :], logits[:, j, :]))
                nc.vector.tensor_tensor(share[:, :, 0:1], top[:, :, 1:2], top[:, :, 0:1], ALU.subtract).then_inc(logits_ready, 1)
                dve.wait_ge(exp_ready, 1)
                link(nc.vector.tensor_scalar(rowsum[:], share[:, :, 1], 1.0, None, ALU.add))
                link(nc.vector.reciprocal(share[:, :, 0], rowsum[:]))
                link(nc.vector.tensor_tensor(share[:, :, 1], share[:, :, 1], share[:, :, 0], ALU.mult))
            else:
                ranked = probs
                if routing == "sigmoid":
                    nc.vector.tensor_copy(tmp[:, 0, 0:1], logits[:, 0, 0:1]).then_inc(logits_ready, 1)
                    dve.wait_ge(exp_ready, 1)
                else:
                    link(nc.vector.tensor_reduce(rowmax[:], logits[:], X_AXIS, ALU.max))
                    nc.vector.tensor_tensor(logits[:], logits[:], rowmax[:].unsqueeze(2).broadcast_to([TT, NT, E]),
                                            ALU.subtract).then_inc(logits_ready, 1)
                    dve.wait_ge(exp_ready, 1)
                    link(nc.vector.tensor_reduce(rowsum[:], probs[:], X_AXIS, ALU.add))
                    link(nc.vector.reciprocal(rowinv[:], rowsum[:]))
                    link(nc.vector.tensor_tensor(probs[:], probs[:], rowinv[:].unsqueeze(2).broadcast_to([TT, NT, E]), ALU.mult))
                for j in range(NT):
                    link(nc.vector.max(top[:, j, :], probs[:, j, :]))
                if routing == "softmax":
                    link(nc.vector.tensor_copy(share[:], top[:, :, 0:2]))
                elif routing == "sigmoid":
                    link(nc.vector.tensor_reduce(rowsum[:], top[:, :, 0:2], X_AXIS, ALU.add))
                    link(nc.vector.reciprocal(rowinv[:], rowsum[:]))
                    link(nc.vector.tensor_tensor(share[:], top[:, :, 0:2], rowinv[:].unsqueeze(2).broadcast_to([TT, NT, 2]), ALU.mult))
            if routing == "top8":
                link(nc.vector.tensor_reduce(rowsum[:], top[:], X_AXIS, ALU.add))
                link(nc.vector.reciprocal(rowinv[:], rowsum[:]))
                for j in range(NT):
                    link(nc.vector.match_replace(tmp[:, j, :], top[:, j, :], probs[:, j, :], -1.0))
                link(nc.vector.tensor_tensor(tmp[:], tmp[:], probs[:], ALU.not_equal))
                link(nc.vector.tensor_tensor(tmp[:], tmp[:], probs[:], ALU.mult))
                link(nc.vector.tensor_tensor(w_e[:], tmp[:], rowinv[:].unsqueeze(2).broadcast_to([TT, NT, E]), ALU.mult))
            else:
                for j in range(NT):
                    link(nc.vector.max_index(top_at[:, j, :], top[:, j, :], ranked[:, j, :]))
                link(nc.vector.tensor_copy(top_at_f[:], top_at[:]))
                for j in range(NT):
                    for r, to in ((0, w_e), (1, tmp)):
                        link(nc.vector.tensor_scalar(to[:, j, :], P.iota[0:TT, 0:E], top_at_f[:, j, r:r + 1],
                                                     share[:, j, r:r + 1], ALU.is_equal, ALU.mult))
                link(nc.vector.tensor_tensor(w_e[:], w_e[:], tmp[:], ALU.add))
            per = sum(e == 0 for e in weight_e)
            routed = per * E
            if routed < n:
                link(nc.vector.memset(w_blk[:, :, routed:n], 1.0))
            last = nc.vector.tensor_copy(w_blk[:, :, 0:routed].rearrange("p j (e r) -> p j e r", r=per),
                                         w_e[:].unsqueeze(3).broadcast_to([TT, NT, E, per]))
            last.then_inc(weights_ready, 1)
            dve.wait_ge(weights_ready, 1)
            if biased:
                dve.wait_ge(wT_done, 1)
                nc.vector.tensor_copy(w_blkT[:].rearrange("p (j t) -> p j t", t=TT), down_ps[1][0:n, :, 0:TT]).then_inc(wT_ready, 1)
                dve.wait_ge(bias_done, 1)
                nc.vector.tensor_tensor(acc[:], P.xn[:], down_ps[0][0:TT], ALU.add).then_inc(acc_ready, 1)
            else:
                nc.vector.memset(acc[:], 0.0).then_inc(acc_ready, 1)
            dve.wait_ge(acc_ready, 1)
            with dve.Fori(0, n // 2) as i:
                for s in range(2):
                    dve.wait_ge(act_ready[s], i + 1)
                    dve.wait_ge(up_done[s], i + 1)
                    dve.wait_ge(down_done[s], i + 1)
                    if biased:
                        nc.vector.scalar_tensor_tensor(hT[:, s, :], up_ps[s][0:F, 0:N_TOK], b_up[:, s],
                                                       act_g[:, s, :], ALU.add, ALU.mult).then_inc(h_ready[s], 1)
                    else:
                        nc.vector.tensor_tensor(hT[:, s, :], act_g[:, s, :], up_ps[s][0:F, 0:N_TOK], ALU.mult)\
                            .then_inc(h_ready[s], 1)
                for s in range(2):
                    dve.wait_ge(down_done[s], i + 2)
                    dve.wait_ge(acc_done[1 - s], i + s + 1)
                    for j in range(NT):
                        last = nc.vector.scalar_tensor_tensor(acc[:, j, :], down_ps[s][0:TT, j, :],
                                                              w_blk[:, j, bass.ds(2 * i + s, 1)],
                                                              acc[:, j, :], ALU.mult, ALU.add)
                    last.then_inc(acc_done[s], 1)
            dve.wait_ge(acc_done[1], n // 2 + 1)
            nc.vector.scalar_tensor_tensor(P.x[:], acc[:], P.gates[0:TT, 4 + k:5 + k], P.x[:], ALU.mult, ALU.add)


def load_wait(engine, sem, dmas):
    engine.wait_ge(sem, 16 * dmas)


def xattn0_stage(P):
    nc, dram = P.nc, P.dram
    HH = 8
    with Stage(nc, "xa0") as st:
        wq, wk, wv, wo = (st.sb(n, [128, KT, D]) for n in ("wq", "wk", "wv", "wo"))
        bq, bk = st.sb("bq", [128, 2]), st.sb("bk", [128, 2])
        bv, bo, gamma, beta = (st.sb(n, [128, D]) for n in ("bv", "bo", "gamma", "beta"))
        mask_i = st.sb("mask_i", [KP, B * KN], I32)
        keep = st.sb("keep", [KP, B * KN])
        zeros = st.sb("zeros", [KP, HH * S])
        escale, ebias = ([st.sb(f"{n}{s}", [KP, KN]) for s in range(2)] for n in ("escale", "ebias"))
        qT = st.sb("qT", [128, 2, N_TOK])
        oT = st.sb("oT", [128, 2, N_TOK])
        ctxT = [st.sb(f"ctxT{s}", [128, KT, T]) for s in range(2)]
        kT = [st.sb(f"kT{s}", [128, 2, T]) for s in range(2)]
        v = [st.sb(f"v{s}", [KP, KN, D]) for s in range(2)]
        qblk = [st.sb(f"qblk{s}", [128, 2, HH, S]) for s in range(2)]
        clipped = [st.sb(f"clipped{r}", [KP, HH * S]) for r in range(3)]
        probs = [st.sb(f"probs{r}", [KP, HH * S]) for r in range(3)]
        psum_acc = [st.sb(f"psum_acc{h}", [KP, HH * S]) for h in range(2)]
        num_m, den_m = st.sb("num_m", [128, HH, S]), st.sb("den_m", [128, HH, S])
        num, den, rden, unit = (st.sb(n, [128, S]) for n in ("num", "den", "rden", "unit"))
        delta = st.sb("delta", [TT, NT, D])
        stats, mean_var = st.sb("stats", [TT, NT, 6]), st.sb("mean_var", [TT, NT, 2])
        var_eps, std, rstd = st.sb("var_eps", [TT, NT]), st.sb("std", [TT, NT]), st.sb("rstd", [TT, NT])
        proj_ps = [st.ps(f"proj{r}", [128, 512]) for r in range(2)]
        score_ps = [st.ps(f"score{r}", [128, 512]) for r in range(3)]
        pv_ps = [st.ps(f"pv{r}", [128, 512]) for r in range(2)]
        den_ps = st.ps("den_ps", [128, 512])
        loaded, ctx_loaded = st.sem("loaded"), st.sems("ctx_loaded", 2)
        q_done, q_ready = st.sem("q_done"), st.sem("q_ready")
        proj_done, proj_free = st.sems("proj_done", 2), st.sems("proj_free", 2)
        qblk_ready, att_done = st.sems("qblk_ready", 2), st.sems("att_done", 2)
        score_done, clip_done = st.sems("score_done", 3), st.sems("clip_done", 3)
        exp_done, pv_done, acc_done = st.sems("exp_done", 3), st.sems("pv_done", 3), st.sems("acc_done", 3)
        den_done, taken = st.sem("den_done"), st.sems("taken", 2)
        dve_step, scale_ready = st.sem("dve_step"), st.sems("scale_ready", 2)
        o_done, var_ready, std_ready = st.sem("o_done"), st.sem("var_ready"), st.sem("std_ready")
        zeros_ready = st.sem("zeros_ready")
        st.start_at_one(att_done, proj_free, taken, clip_done, den_done, acc_done, pv_done, exp_done)
        block = st.block()
        N_LOADS = 11
        PER = 9
        M = 2 * KN
        RU = M // 3

        @block.sync
        def _(sp):
            for name, t in (("wq", wq), ("wk", wk), ("wv", wv), ("wo", wo)):
                sp.dma_start(t[:], dram[f"x0_{name}"].rearrange("(c p) n -> p c n", p=128)).then_inc(loaded, 16)
            for name, t in (("bq", bq), ("bk", bk), ("bv", bv), ("bo", bo), ("gamma", gamma), ("beta", beta)):
                sp.dma_start(t[:], dram[f"x0_{name}"]).then_inc(loaded, 16)
            sp.dma_start(mask_i[:], dram["mask0"]).then_inc(loaded, 16)
            with sp.Fori(0, B // 2) as i:
                for s in range(2):
                    sp.wait_ge(att_done[s], i + 1)
                    sp.dma_start(ctxT[s][:], dram["ctxT"][bass.ds(2 * i + s, 1)].rearrange("o (c p) t -> p (o c) t", p=128))\
                        .then_inc(ctx_loaded[s], 16)

        @block.tensor
        def _(pe):
            load_wait(pe, loaded, N_LOADS)
            for h in range(2):
                for c in range(KT):
                    last = nc.tensor.matmul(score_ps[h][:, 0:N_TOK], wq[:, c, h * 128:(h + 1) * 128], P.xnT[:, c, :],
                                            start=(c == 0), stop=(c == KT - 1))
                last.then_inc(q_done, 1)
            pe.wait_ge(q_ready, 2)
            with pe.Fori(0, B // 2) as i:
                for s in range(2):
                    b = 2 * i + s
                    pe.wait_ge(ctx_loaded[s], 16 * i + 16)
                    for u in range(6):
                        h, c3 = u // 3, u % 3
                        pe.wait_ge(proj_free[u % 2], PER * b + u // 2 + 1)
                        for c in range(KT):
                            last = nc.tensor.matmul(proj_ps[u % 2][:, 0:KC], wk[:, c, h * 128:(h + 1) * 128],
                                                    ctxT[s][:, c, c3 * KC:(c3 + 1) * KC], start=(c == 0), stop=(c == KT - 1))
                        last.then_inc(proj_done[u % 2], 1)
                    for n in range(KN):
                        pe.wait_ge(proj_free[n % 2], PER * b + 3 + n // 2 + 1)
                        for c in range(KT):
                            last = nc.tensor.matmul(proj_ps[n % 2][0:KP, 0:D], ctxT[s][:, c, n * KP:(n + 1) * KP], wv[:, c, :],
                                                    start=(c == 0), stop=(c == KT - 1))
                        last.then_inc(proj_done[n % 2], 1)
                    pe.wait_ge(qblk_ready[s], i + 1)

                    def weigh(m):
                        h, n = m // KN, m % KN
                        pe.wait_ge(exp_done[m % 3], RU * b + m // 3 + 2)
                        if n == 0:
                            pe.wait_ge(taken[h], b + 1)
                            pe.wait_ge(proj_free[0], PER * b + PER + 1)
                            pe.wait_ge(proj_free[1], PER * b + PER + 1)
                        nc.tensor.matmul(pv_ps[h][:, 0:HH * S], v[s][:, n, h * 128:(h + 1) * 128], probs[m % 3][:],
                                         start=(n == 0), stop=(n == KN - 1)).then_inc(pv_done[m % 3], 1)

                    def total(h):
                        pe.wait_ge(acc_done[(h * KN + KN - 1) % 3], RU * b + (h * KN + KN - 1) // 3 + 2)
                        if h == 0:
                            pe.wait_ge(taken[1], b + 1)
                        else:
                            pe.wait_ge(taken[0], b + 2)
                        nc.tensor.matmul(den_ps[:, 0:HH * S], P.ones[0:KP, :], psum_acc[h][:], start=True, stop=True)\
                            .then_inc(den_done if h == 0 else att_done[s], 1)

                    for m in range(M):
                        h, n = m // KN, m % KN
                        pe.wait_ge(clip_done[m % 3], RU * b + m // 3 + 1)
                        nc.tensor.matmul(score_ps[m % 3][0:KP, 0:HH * S], kT[s][:, h, n * KP:(n + 1) * KP],
                                         qblk[s][:, h].rearrange("p a q -> p (a q)"), start=True, stop=True)\
                            .then_inc(score_done[m % 3], 1)
                        if m >= 2:
                            weigh(m - 2)
                        if m == KN + 4:
                            total(0)
                    weigh(M - 2)
                    weigh(M - 1)
                    total(1)
            pe.wait_ge(taken[1], B + 1)
            for j in range(NT):
                for h in range(2):
                    last = nc.tensor.matmul(proj_ps[j // 2][0:TT, (j % 2) * D:(j % 2 + 1) * D], oT[:, h, j * TT:(j + 1) * TT],
                                            wo[:, h, :], start=(h == 0), stop=(h == 1))
            last.then_inc(o_done, 1)

        @block.gpsimd
        def _(pool):
            nc.gpsimd.memset(zeros[:], 0.0).then_inc(zeros_ready, 1)
            pool.wait_ge(zeros_ready, 1)
            with pool.Fori(0, B // 2) as i:
                for s in range(2):
                    b = 2 * i + s
                    pool.wait_ge(att_done[s], i + 1)
                    pool.wait_ge(q_ready, 2)
                    for h in range(2):
                        last = nc.gpsimd.tensor_tensor(qblk[s][:, h], qT[:, h, bass.ds(b * S, S)].unsqueeze(1).broadcast_to([128, HH, S]),
                                                       P.head_mask[:].unsqueeze(2).broadcast_to([128, HH, S]), ALU.mult)
                    last.then_inc(qblk_ready[s], 1)
                    for m in range(M):
                        h, n = m // KN, m % KN
                        pool.wait_ge(exp_done[m % 3], RU * b + m // 3 + 2)
                        if n == 0:
                            if h == 0:
                                pool.wait_ge(den_done, b + 1)
                            else:
                                pool.wait_ge(att_done[1 - s], i + s + 1)
                            pool.wait_ge(q_ready, 2)
                            nc.gpsimd.tensor_tensor(psum_acc[h][:], probs[m % 3][:], zeros[:], ALU.add).then_inc(acc_done[m % 3], 1)
                        else:
                            pool.wait_ge(acc_done[(m - 1) % 3], RU * b + (m - 1) // 3 + 2)
                            nc.gpsimd.tensor_tensor(psum_acc[h][:], psum_acc[h][:], probs[m % 3][:], ALU.add)\
                                .then_inc(acc_done[m % 3], 1)

        @block.scalar
        def _(act):
            load_wait(act, loaded, N_LOADS)
            for h in range(2):
                act.wait_ge(q_done, h + 1)
                nc.scalar.activation(qT[:, h, :], score_ps[h][:, 0:N_TOK], ACT.Identity, bias=bq[:, h:h + 1]).then_inc(q_ready, 1)
            with act.Fori(0, B // 2) as i:
                for s in range(2):
                    b = 2 * i + s
                    act.wait_ge(att_done[s], i + 1)
                    for u in range(6):
                        h, c3 = u // 3, u % 3
                        act.wait_ge(proj_done[u % 2], PER * b + u // 2 + 1)
                        nc.scalar.activation(kT[s][:, h, c3 * KC:(c3 + 1) * KC], proj_ps[u % 2][:, 0:KC], ACT.Identity,
                                             bias=bk[:, h:h + 1]).then_inc(proj_free[u % 2], 1)
                    for m in range(M):
                        at = m % KN
                        act.wait_ge(clip_done[m % 3], RU * b + m // 3 + 2)
                        act.wait_ge(pv_done[m % 3], RU * b + m // 3 + 1)
                        act.wait_ge(acc_done[m % 3], RU * b + m // 3 + 1)
                        if m == 0:
                            act.wait_ge(scale_ready[s], i + 1)
                        nc.scalar.activation(probs[m % 3][:], clipped[m % 3][:], ACT.Exp, bias=ebias[s][:, at:at + 1],
                                             scale=escale[s][:, at:at + 1]).then_inc(exp_done[m % 3], 1)
            act.wait_ge(var_ready, 1)
            nc.scalar.activation(std[:], var_eps[:], ACT.Sqrt).then_inc(std_ready, 1)

        @block.vector
        def _(dve):
            link = in_order(dve, dve_step)
            load_wait(dve, loaded, N_LOADS)
            link(nc.vector.tensor_copy(keep[:], mask_i[:]))
            link(nc.vector.tensor_scalar(keep[:], keep[:], 0.5, None, ALU.is_gt))
            with dve.Fori(0, B // 2) as i:
                for s in range(2):
                    b = 2 * i + s
                    dve.wait_ge(att_done[s], i + 1)
                    nc.vector.tensor_scalar(escale[s][:], keep[:, bass.ds(b * KN, KN)], 0.25, None, ALU.mult)
                    nc.vector.tensor_scalar(ebias[s][:], keep[:, bass.ds(b * KN, KN)], -1.0, 50.0, ALU.add, ALU.mult)\
                        .then_inc(scale_ready[s], 1)
                    for n in range(KN):
                        dve.wait_ge(proj_done[n % 2], PER * b + 4 + n // 2)
                        nc.vector.tensor_tensor(v[s][:, n, :], proj_ps[n % 2][0:KP, 0:D], bv[0:KP, :], ALU.add)\
                            .then_inc(proj_free[n % 2], 1)

                    def take(h):
                        E0 = 9 * (2 * b + h)
                        steps = [0]

                        def done(ins):
                            steps[0] += 1
                            ins.then_inc(dve_step, 1)
                            dve.wait_ge(dve_step, 2 + E0 + steps[0])
                        if h == 0:
                            dve.wait_ge(den_done, b + 2)
                        else:
                            dve.wait_ge(att_done[s], i + 2)
                        mask = P.head_mask[:].unsqueeze(2).broadcast_to([128, HH, S])
                        done(nc.vector.tensor_tensor(den_m[:], den_ps[:, 0:HH * S].rearrange("p (a q) -> p a q", q=S), mask, ALU.mult))
                        done(nc.vector.tensor_tensor(num_m[:], pv_ps[h][:, 0:HH * S].rearrange("p (a q) -> p a q", q=S), mask, ALU.mult))
                        done(nc.vector.tensor_reduce(den[:], den_m[:].rearrange("p a q -> p q a"), X_AXIS, ALU.add))
                        done(nc.vector.tensor_reduce(num[:], num_m[:].rearrange("p a q -> p q a"), X_AXIS, ALU.add))
                        done(nc.vector.reciprocal(rden[:], den[:]))
                        done(nc.vector.tensor_tensor(unit[:], den[:], rden[:], ALU.mult))
                        done(nc.vector.tensor_scalar(unit[:], unit[:], 1e-8, None, ALU.add))
                        done(nc.vector.reciprocal(unit[:], unit[:]))
                        done(nc.vector.tensor_tensor(num[:], num[:], rden[:], ALU.mult))
                        nc.vector.tensor_tensor(oT[:, h, bass.ds(b * S, S)], num[:], unit[:], ALU.mult).then_inc(taken[h], 1)

                    for m in range(M):
                        dve.wait_ge(score_done[m % 3], RU * b + m // 3 + 1)
                        dve.wait_ge(exp_done[m % 3], RU * b + m // 3 + 1)
                        nc.vector.tensor_scalar(clipped[m % 3][:], score_ps[m % 3][0:KP, 0:HH * S], -200.0, 200.0,
                                                ALU.max, ALU.min).then_inc(clip_done[m % 3], 1)
                        if m == KN + 5:
                            take(0)
                    take(1)
            link = in_order(dve, dve_step, 2 + 9 * 2 * B)
            dve.wait_ge(o_done, 1)
            for j in range(NT):
                link(nc.vector.tensor_tensor(delta[:, j, :], proj_ps[j // 2][0:TT, (j % 2) * D:(j % 2 + 1) * D], bo[0:TT, :], ALU.add))
            link(nc.vector.tensor_scalar(delta[:], delta[:], P.gates[0:TT, 8:9], None, ALU.mult))
            for j in range(NT):
                link(nc.vector.bn_stats(stats[:, j, :], delta[:, j, :]))
            for j in range(NT):
                link(nc.vector.bn_aggr(mean_var[:, j, :], stats[:, j, :]))
            nc.vector.tensor_scalar(var_eps[:], mean_var[:, :, 1], EPS_LN, None, ALU.add).then_inc(var_ready, 1)
            dve.wait_ge(std_ready, 1)
            link(nc.vector.reciprocal(rstd[:], std[:]))
            for j in range(NT):
                link(nc.vector.tensor_scalar(delta[:, j, :], delta[:, j, :], mean_var[:, j, 0:1], rstd[:, j:j + 1],
                                             ALU.subtract, ALU.mult))
            link(nc.vector.tensor_tensor(delta[:], delta[:], gamma[0:TT, :].unsqueeze(1).broadcast_to([TT, NT, D]), ALU.mult))
            link(nc.vector.tensor_tensor(delta[:], delta[:], beta[0:TT, :].unsqueeze(1).broadcast_to([TT, NT, D]), ALU.add))
            nc.vector.scalar_tensor_tensor(P.x[:], delta[:], P.gates[0:TT, 0:1], P.x[:], ALU.mult, ALU.add)


def xattn1_stage(P):
    nc, dram = P.nc, P.dram
    G, HG, GD = 4, 4, 64
    R, NR = 128, 7
    KA = GD + 3
    with Stage(nc, "xa1") as st:
        wq = st.sb("wq", [128, KT, HG, GD])
        wk, wv = st.sb("wk", [128, KT, GD]), st.sb("wv", [128, KT, GD])
        wo = st.sb("wo", [GD, HG, D])
        qT = st.sb("qT", [GD, HG, N_TOK])
        oT = st.sb("oT", [GD, HG, N_TOK])
        ctxT = [st.sb(f"ctxT{s}", [128, KT, T]) for s in range(2)]
        kA = [st.sb(f"kA{s}", [KA, T]) for s in range(2)]
        v = [st.sb(f"v{s}", [KP, KN, GD]) for s in range(2)]
        qA = [st.sb(f"qA{s}", [KA, G, HG, S]) for s in range(2)]
        keep = [st.sb(f"keep{s}", [GD + 1, T], U8) for s in range(2)]
        probs = [st.sb(f"probs{r}", [R, T]) for r in range(2)]
        probsT = [st.sb(f"probsT{r}", [KP, KN, R]) for r in range(2)]
        negmax, den, rden = st.sb("negmax", [R, NR]), st.sb("den", [R, NR]), st.sb("rden", [R, NR])
        num_m = st.sb("num_m", [GD, G, HG, S])
        score_ps = st.ps("score", [128, 3, 512])
        turn_ps = [st.ps(f"turn{r}", [128, 512]) for r in range(2)]
        pv_ps = st.ps("pv", [GD, 1024])
        proj_ps = st.ps("proj", [128, 512])
        loaded, ctx_loaded, keep_loaded = st.sem("loaded"), st.sems("ctx_loaded", 2), st.sems("keep_loaded", 2)
        q_done, q_ready = st.sem("q_done"), st.sem("q_ready")
        proj_done, proj_free = st.sem("proj_done"), st.sem("proj_free")
        qA_ready, mask_ready, pv_done = st.sems("qA_ready", 2), st.sems("mask_ready", 2), st.sems("pv_done", 2)
        score_done, max_done, exp_done, norm_done = (st.sem("score_done"), st.sem("max_done"), st.sem("exp_done"),
                                                     st.sem("norm_done"))
        turn_done, turn_free = st.sems("turn_done", 2), st.sems("turn_free", 2)
        rows_done, dve_step, taken, o_done = st.sem("rows_done"), st.sem("dve_step"), st.sem("taken"), st.sem("o_done")
        st.start_at_one(pv_done, proj_free, exp_done, turn_free, taken)
        block = st.block()
        N_LOADS = 8
        PER = 5
        QT = 3
        NTURN = NR * QT

        @block.sync
        def _(sp):
            sp.dma_start(wq[:], dram["x1_wq"].rearrange("(c p) (a n) -> p c a n", p=128, a=HG)).then_inc(loaded, 16)
            sp.dma_start(wk[:], dram["x1_wk"].rearrange("(c p) n -> p c n", p=128)).then_inc(loaded, 16)
            sp.dma_start(wv[:], dram["x1_wv"].rearrange("(c p) n -> p c n", p=128)).then_inc(loaded, 16)
            sp.dma_start(wo[:], dram["x1_wo"]).then_inc(loaded, 16)
            for s in range(2):
                sp.dma_start(kA[s][GD + 1:KA, :], dram["x1_k_rows"]).then_inc(loaded, 16)
                sp.dma_start(qA[s][GD + 1:KA].rearrange("p g a q -> p (g a q)"), dram["x1_q_rows"]).then_inc(loaded, 16)
            with sp.Fori(0, B // 2) as i:
                for s in range(2):
                    sp.wait_ge(pv_done[s], i + 1)
                    sp.dma_start(ctxT[s][:], dram["ctxT"][bass.ds(2 * i + s, 1)].rearrange("o (c p) t -> p (o c) t", p=128))\
                        .then_inc(ctx_loaded[s], 16)
                    sp.dma_start(keep[s][GD:GD + 1, :], dram["mask1"][bass.ds(2 * i + s, 1), :]).then_inc(keep_loaded[s], 16)

        @block.tensor
        def _(pe):
            load_wait(pe, loaded, N_LOADS)
            for a in range(HG):
                if a >= 2:
                    pe.wait_ge(q_ready, a - 1)
                for c in range(KT):
                    last = nc.tensor.matmul(turn_ps[a % 2][0:GD, 0:N_TOK], wq[:, c, a, :], P.xnT[:, c, :],
                                            start=(c == 0), stop=(c == KT - 1))
                last.then_inc(q_done, 1)
            pe.wait_ge(q_ready, HG)
            with pe.Fori(0, B // 2) as i:
                for s in range(2):
                    b = 2 * i + s
                    pe.wait_ge(ctx_loaded[s], 16 * i + 16)
                    for c3 in range(3):
                        pe.wait_ge(proj_free, PER * b + c3 + 1)
                        for c in range(KT):
                            last = nc.tensor.matmul(proj_ps[0:GD, 0:KC], wk[:, c, :], ctxT[s][:, c, c3 * KC:(c3 + 1) * KC],
                                                    start=(c == 0), stop=(c == KT - 1))
                        last.then_inc(proj_done, 1)
                    for half in range(2):
                        pe.wait_ge(proj_free, PER * b + 3 + half + 1)
                        for n in range(6):
                            t0 = (half * 6 + n) * KP
                            for c in range(KT):
                                last = nc.tensor.matmul(proj_ps[0:KP, n * GD:(n + 1) * GD], ctxT[s][:, c, t0:t0 + KP],
                                                        wv[:, c, :], start=(c == 0), stop=(c == KT - 1))
                        last.then_inc(proj_done, 1)
                    pe.wait_ge(proj_free, PER * b + PER + 1)
                    pe.wait_ge(qA_ready[s], i + 1)
                    pe.wait_ge(mask_ready[s], i + 1)

                    def scores(r):
                        pe.wait_ge(exp_done, NR * b + r + 1)
                        for c3 in range(3):
                            last = nc.tensor.matmul(score_ps[:, c3, 0:KC], qA[s][:].rearrange("p g a q -> p (g a q)")[:, r * R:(r + 1) * R],
                                                    kA[s][:, c3 * KC:(c3 + 1) * KC], start=True, stop=True)
                        last.then_inc(score_done, 1)

                    def turn_and_weigh(r):
                        pe.wait_ge(norm_done, NR * b + r + 1)
                        for q in range(QT):
                            k = (r * QT + q) % 2
                            use = (r * QT + q) // 2
                            per = (NTURN + 1 - k) // 2
                            pe.wait_ge(turn_free[k], per * b + use + 1)
                            for n in range(4):
                                t0 = (q * 4 + n) * KP
                                last = nc.tensor.transpose(turn_ps[k][0:KP, n * R:(n + 1) * R], probs[r % 2][:, t0:t0 + KP],
                                                           P.ident[:])
                            last.then_inc(turn_done[k], 1)
                        if r == 0:
                            pe.wait_ge(taken, b + 1)
                        for k in range(2):
                            n_to = sum((r * QT + q) % 2 == k for q in range(QT))
                            pe.wait_ge(turn_free[k], ((NTURN + 1 - k) // 2) * b + (r * QT + 1 - k) // 2 + n_to + 1)
                        for n in range(KN):
                            last = nc.tensor.matmul(pv_ps[:, r * R:(r + 1) * R], v[s][:, n, :], probsT[r % 2][:, n, :],
                                                    start=(n == 0), stop=(n == KN - 1))
                        last.then_inc(rows_done if r < NR - 1 else pv_done[s], 1)

                    for r in range(NR):
                        scores(r)
                        if r:
                            turn_and_weigh(r - 1)
                    turn_and_weigh(NR - 1)
            pe.wait_ge(taken, B + 1)
            for j in range(NT):
                for a in range(HG):
                    last = nc.tensor.matmul(turn_ps[j // 2][0:TT, (j % 2) * D:(j % 2 + 1) * D], oT[:, a, j * TT:(j + 1) * TT],
                                            wo[:, a, :], start=(a == 0), stop=(a == HG - 1))
            last.then_inc(o_done, 1)

        @block.gpsimd
        def _(pool):
            with pool.Fori(0, B // 2) as i:
                for s in range(2):
                    b = 2 * i + s
                    pool.wait_ge(pv_done[s], i + 1)
                    pool.wait_ge(q_ready, HG)
                    for g in range(G):
                        last = nc.gpsimd.tensor_tensor(qA[s][0:GD, g], qT[:, :, bass.ds(b * S, S)],
                                                       P.head_mask[0:GD, g:g + 1].unsqueeze(2).broadcast_to([GD, HG, S]), ALU.mult)
                    last.then_inc(qA_ready[s], 1)

        @block.scalar
        def _(act):
            for a in range(HG):
                act.wait_ge(q_done, a + 1)
                nc.scalar.activation(qT[:, a, :], turn_ps[a % 2][0:GD, 0:N_TOK], ACT.Copy, scale=0.25).then_inc(q_ready, 1)
            with act.Fori(0, B // 2) as i:
                for s in range(2):
                    b = 2 * i + s
                    act.wait_ge(pv_done[s], i + 1)
                    for c3 in range(3):
                        act.wait_ge(proj_done, PER * b + c3 + 1)
                        nc.scalar.activation(kA[s][0:GD, c3 * KC:(c3 + 1) * KC], proj_ps[0:GD, 0:KC], ACT.Copy).then_inc(proj_free, 1)
                    for half in range(2):
                        act.wait_ge(proj_done, PER * b + 4 + half)
                        nc.scalar.activation(v[s][:, half * 6:(half + 1) * 6, :], proj_ps[0:KP, 0:6 * GD].rearrange("p (n d) -> p n d", d=GD),
                                             ACT.Copy).then_inc(proj_free, 1)

                    def copy_turned(r, q):
                        k, use = (r * QT + q) % 2, (r * QT + q) // 2
                        act.wait_ge(turn_done[k], ((NTURN + 1 - k) // 2) * b + use + 1)
                        nc.scalar.activation(probsT[r % 2][:, q * 4:(q + 1) * 4, :], turn_ps[k][0:KP, :].rearrange("p (n t) -> p n t", t=R),
                                             ACT.Copy).then_inc(turn_free[k], 1)

                    for r in range(NR):
                        act.wait_ge(max_done, NR * b + r + 1)
                        nc.scalar.activation(probs[r % 2][:], score_ps[:, :, 0:KC], ACT.Exp, bias=negmax[:, r:r + 1],
                                             accum_out=den[:, r:r + 1]).then_inc(exp_done, 1)
                        if r:
                            copy_turned(r - 1, 1)
                    copy_turned(NR - 1, 1)

        @block.vector
        def _(dve):
            def copy_turned(b, r, q):
                k, use = (r * QT + q) % 2, (r * QT + q) // 2
                dve.wait_ge(turn_done[k], ((NTURN + 1 - k) // 2) * b + use + 1)
                nc.vector.tensor_copy(probsT[r % 2][:, q * 4:(q + 1) * 4, :], turn_ps[k][0:KP, :].rearrange("p (n t) -> p n t", t=R))\
                    .then_inc(turn_free[k], 1)

            load_wait(dve, loaded, N_LOADS)
            for s in range(2):
                nc.vector.memset(qA[s][GD:GD + 1], 1.0)
            with dve.Fori(0, B // 2) as i:
                for s in range(2):
                    b = 2 * i + s
                    dve.wait_ge(keep_loaded[s], 16 * i + 16)
                    dve.wait_ge(pv_done[s], i + 1)
                    nc.vector.tensor_scalar(kA[s][GD:GD + 1, :], keep[s][GD:GD + 1, :], 1e30, -1e30, ALU.mult, ALU.add)\
                        .then_inc(mask_ready[s], 1)
                    for r in range(NR):
                        dve.wait_ge(score_done, NR * b + r + 1)
                        nc.vector.tensor_reduce(negmax[:, r:r + 1], score_ps[:, :, 0:KC], XY_AXES, ALU.max, negate=True)\
                            .then_inc(max_done, 1)
                        if r:
                            copy_turned(b, r - 1, 0)
                            copy_turned(b, r - 1, 2)
                        dve.wait_ge(exp_done, NR * b + r + 2)
                        nc.vector.reciprocal(rden[:, r:r + 1], den[:, r:r + 1]).then_inc(dve_step, 1)
                        dve.wait_ge(dve_step, NR * b + b + r + 1)
                        nc.vector.tensor_scalar(probs[r % 2][:], probs[r % 2][:], rden[:, r:r + 1], None, ALU.mult)\
                            .then_inc(norm_done, 1)
                    copy_turned(b, NR - 1, 0)
                    copy_turned(b, NR - 1, 2)
                    dve.wait_ge(pv_done[s], i + 2)
                    nc.vector.tensor_tensor(num_m[:].rearrange("p g a q -> p g (a q)"), pv_ps[:, 0:H * S].rearrange("p (g n) -> p g n", g=G),
                                            P.head_mask[0:GD, 0:G].unsqueeze(2).broadcast_to([GD, G, HG * S]), ALU.mult)\
                        .then_inc(dve_step, 1)
                    dve.wait_ge(dve_step, (NR + 1) * b + NR + 1)
                    nc.vector.tensor_reduce(oT[:, :, bass.ds(b * S, S)], num_m[:].rearrange("p g a q -> p a q g"), X_AXIS, ALU.add)\
                        .then_inc(taken, 1)
            dve.wait_ge(o_done, 1)
            for j in range(NT):
                nc.vector.scalar_tensor_tensor(P.x[:, j, :], turn_ps[j // 2][0:TT, (j % 2) * D:(j % 2 + 1) * D],
                                               P.gates[0:TT, 1:2], P.x[:, j, :], ALU.mult, ALU.add)


def xattn2_stage(P):
    nc, dram = P.nc, P.dram
    with Stage(nc, "xa2") as st:
        wq, wg, wo = (st.sb(n, [128, KT, D]) for n in ("wq", "wg", "wo"))
        wkv = st.sb("wkv", [128, KT, 2 * D])
        bg = st.sb("bg", [128, 2])
        block_mask = st.sb("block_mask", [128, 128])
        fq, lq, eq = (st.sb(n, [128, 2, N_TOK]) for n in ("fq", "lq", "eq"))
        gateT, oT = st.sb("gateT", [128, 2, N_TOK]), st.sb("oT", [128, 2, N_TOK])
        ctxT = [st.sb(f"ctxT{s}", [128, KT, T]) for s in range(2)]
        RING = 3
        pos, low, ek, fk = ([st.sb(f"{n}{r}", [KP, D]) for r in range(RING)] for n in ("pos", "low", "ek", "fk"))
        vx = [st.sb(f"vx{r}", [KP, 2, 129]) for r in range(RING)]
        summary, ksum_blk = st.sb("summary", [128, 2, 128]), st.sb("ksum_blk", [128, 2, 128])
        rden = st.sb("rden", [128, 2, S])
        kv_ps = [st.ps(f"kv{r}", [128, 512]) for r in range(RING)]
        sum_ps = [st.ps(f"sum{h}", [128, 512]) for h in range(2)]
        out_ps = st.ps("out", [128, 512])
        q_ps = [st.ps(f"q{h}", [128, 512]) for h in range(2)]
        loaded, ctx_loaded = st.sem("loaded"), st.sems("ctx_loaded", 2)
        q_done, q_low, q_exp, gate_done, gate_ready = (st.sem("q_done"), st.sem("q_low"), st.sem("q_exp"),
                                                       st.sem("gate_done"), st.sem("gate_ready"))
        kv_done, low_done, relu_done, exp_done = (st.sems(n, RING) for n in ("kv_done", "low_done", "relu_done", "exp_done"))
        fk_done, used = st.sems("fk_done", RING), st.sems("used", RING)
        v_done = st.sems("v_done", RING)
        sum_done, sum_read, out_done, out_read = st.sems("sum_done", 2), st.sem("sum_read"), st.sem("out_done"), st.sem("out_read")
        dve_step, o_done, dve_q = st.sem("dve_step"), st.sem("o_done"), st.sem("dve_q")
        st.start_at_one(sum_done, sum_read, v_done, relu_done, low_done, out_read, fk_done, exp_done, out_done)
        block = st.block()
        N_LOADS = 6
        RU = KN // RING

        @block.sync
        def _(sp):
            for name, t in (("wq", wq), ("wg", wg), ("wkv", wkv), ("wo", wo)):
                sp.dma_start(t[:], dram[f"x2_{name}"].rearrange("(c p) n -> p c n", p=128)).then_inc(loaded, 16)
            sp.dma_start(bg[:], dram["x2_bg"]).then_inc(loaded, 16)
            sp.dma_start(block_mask[:], dram["block_mask"]).then_inc(loaded, 16)
            with sp.Fori(0, B // 2) as i:
                for s in range(2):
                    sp.wait_ge(sum_done[s], i + 1)
                    sp.dma_start(ctxT[s][:], dram["ctxT"][bass.ds(2 * i + s, 1)].rearrange("o (c p) t -> p (o c) t", p=128))\
                        .then_inc(ctx_loaded[s], 16)

        @block.tensor
        def _(pe):
            load_wait(pe, loaded, N_LOADS)
            for w, done in ((wq, q_done), (wg, gate_done)):
                for h in range(2):
                    if w is wg:
                        pe.wait_ge(q_low, 2 * h + 2)
                    for c in range(KT):
                        last = nc.tensor.matmul(q_ps[h][:, 0:N_TOK], w[:, c, h * 128:(h + 1) * 128], P.xnT[:, c, :],
                                                start=(c == 0), stop=(c == KT - 1))
                    last.then_inc(done, 1)
            with pe.Fori(0, B // 2) as i:
                for s in range(2):
                    b = 2 * i + s
                    pe.wait_ge(ctx_loaded[s], 16 * i + 16)

                    def summarise(n):
                        r = n % RING
                        pe.wait_ge(fk_done[r], RU * b + n // RING + 2)
                        pe.wait_ge(v_done[r], RU * b + n // RING + 2)
                        if n == 0:
                            pe.wait_ge(sum_read, b + 1)
                        for h in range(2):
                            last = nc.tensor.matmul(sum_ps[h][:, 0:129], fk[r][:, h * 128:(h + 1) * 128], vx[r][:, h, :],
                                                    start=(n == 0), stop=(n == KN - 1))
                        last.then_inc(used[r] if n < KN - 1 else sum_done[s], 1)

                    for n in range(KN):
                        r = n % RING
                        pe.wait_ge(v_done[r], RU * b + n // RING + 1)
                        pe.wait_ge(relu_done[r], RU * b + n // RING + 1)
                        pe.wait_ge(low_done[r], RU * b + n // RING + 1)
                        for c in range(KT):
                            last = nc.tensor.matmul(kv_ps[r][0:KP, :], ctxT[s][:, c, n * KP:(n + 1) * KP], wkv[:, c, :],
                                                    start=(c == 0), stop=(c == KT - 1))
                        last.then_inc(kv_done[r], 1)
                        if n >= 2:
                            summarise(n - 2)
                    summarise(KN - 2)
                    summarise(KN - 1)
                    pe.wait_ge(sum_read, b + 2)
                    pe.wait_ge(out_read, b + 1)
                    pe.wait_ge(dve_q, 2)
                    for h in range(2):
                        for w, at in ((summary, 0), (ksum_blk, 1)):
                            last = nc.tensor.matmul(out_ps[:, (2 * h + at) * S:(2 * h + at + 1) * S], w[:, h, :],
                                                    fq[:, h, bass.ds(b * S, S)], start=True, stop=True)
                    last.then_inc(out_done, 1)
            pe.wait_ge(out_read, B + 1)
            for j in range(NT):
                for h in range(2):
                    last = nc.tensor.matmul(q_ps[j // 2][0:TT, (j % 2) * D:(j % 2 + 1) * D], oT[:, h, j * TT:(j + 1) * TT],
                                            wo[:, h, :], start=(h == 0), stop=(h == 1))
            last.then_inc(o_done, 1)

        @block.scalar
        def _(act):
            load_wait(act, loaded, N_LOADS)
            for h in range(2):
                act.wait_ge(q_low, 2 * h + 1)
                nc.scalar.activation(eq[:, h, :], lq[:, h, :], ACT.Exp).then_inc(q_exp, 1)
            for h in range(2):
                act.wait_ge(gate_done, h + 1)
                nc.scalar.activation(gateT[:, h, :], q_ps[h][:, 0:N_TOK], ACT.Sigmoid, bias=bg[:, h:h + 1]).then_inc(gate_ready, 1)
            with act.Fori(0, B // 2) as i:
                for s in range(2):
                    b = 2 * i + s
                    for n in range(KN):
                        r = n % RING
                        act.wait_ge(fk_done[r], RU * b + n // RING + 1)
                        act.wait_ge(v_done[r], RU * b + n // RING + 2)
                        nc.scalar.activation(pos[r][:], kv_ps[r][0:KP, 0:D], ACT.Relu).then_inc(relu_done[r], 1)
                        act.wait_ge(low_done[r], RU * b + n // RING + 2)
                        nc.scalar.activation(ek[r][:], low[r][:], ACT.Exp).then_inc(exp_done[r], 1)

        @block.vector
        def _(dve):
            for r in range(RING):
                nc.vector.memset(vx[r][:, :, 128:129], 1.0)
            for h in range(2):
                dve.wait_ge(q_done, h + 1)
                nc.vector.tensor_scalar(lq[:, h, :], q_ps[h][:, 0:N_TOK], 0.0, None, ALU.min).then_inc(q_low, 1)
                nc.vector.tensor_scalar(fq[:, h, :], q_ps[h][:, 0:N_TOK], 0.0, None, ALU.max).then_inc(q_low, 1)
            for h in range(2):
                dve.wait_ge(q_exp, h + 1)
                dve.wait_ge(q_low, 4)
                nc.vector.tensor_tensor(fq[:, h, :], fq[:, h, :], eq[:, h, :], ALU.add).then_inc(dve_q, 1)
            dve.wait_ge(loaded, 16 * N_LOADS)
            with dve.Fori(0, B // 2) as i:
                for s in range(2):
                    b = 2 * i + s
                    for n in range(KN):
                        r = n % RING
                        dve.wait_ge(kv_done[r], RU * b + n // RING + 1)
                        dve.wait_ge(exp_done[r], RU * b + n // RING + 1)
                        nc.vector.tensor_scalar(low[r][:], kv_ps[r][0:KP, 0:D], 0.0, None, ALU.min).then_inc(low_done[r], 1)
                        if n < RING:
                            dve.wait_ge(sum_done[1 - s], i + s + 1)
                        else:
                            dve.wait_ge(used[r], (RU - (r == RING - 1)) * b + n // RING)
                        nc.vector.tensor_copy(vx[r][:, :, 0:128], kv_ps[r][0:KP, D:2 * D].rearrange("p (h d) -> p h d", h=2))\
                            .then_inc(v_done[r], 1)
                        dve.wait_ge(relu_done[r], RU * b + n // RING + 2)
                        dve.wait_ge(exp_done[r], RU * b + n // RING + 2)
                        nc.vector.tensor_tensor(fk[r][:], pos[r][:], ek[r][:], ALU.add).then_inc(fk_done[r], 1)
                    dve.wait_ge(sum_done[s], i + 2)
                    dve.wait_ge(out_done, b + 1)
                    for h in range(2):
                        nc.vector.tensor_tensor(summary[:, h, :], sum_ps[h][:, 0:128], block_mask[:], ALU.mult)
                        last = nc.vector.tensor_scalar(ksum_blk[:, h, :], block_mask[:], sum_ps[h][:, 128:129], None, ALU.mult)
                    last.then_inc(sum_read, 1)
                    dve.wait_ge(out_done, b + 2)
                    view = out_ps[:, 0:4 * S].rearrange("p (h w q) -> p h w q", h=2, w=2)
                    nc.vector.tensor_scalar(rden[:], view[:, :, 1, :], 1e-6, None, ALU.add).then_inc(dve_step, 1)
                    dve.wait_ge(dve_step, 3 * b + 1)
                    nc.vector.reciprocal(rden[:], rden[:]).then_inc(dve_step, 1)
                    dve.wait_ge(dve_step, 3 * b + 2)
                    nc.vector.tensor_tensor(rden[:], view[:, :, 0, :], rden[:], ALU.mult).then_inc(dve_step, 1)
                    dve.wait_ge(dve_step, 3 * b + 3)
                    dve.wait_ge(gate_ready, 2)
                    nc.vector.tensor_tensor(oT[:, :, bass.ds(b * S, S)], rden[:], gateT[:, :, bass.ds(b * S, S)], ALU.mult)\
                        .then_inc(out_read, 1)
            dve.wait_ge(o_done, 1)
            for j in range(NT):
                nc.vector.scalar_tensor_tensor(P.x[:, j, :], q_ps[j // 2][0:TT, (j % 2) * D:(j % 2 + 1) * D],
                                               P.gates[0:TT, 2:3], P.x[:, j, :], ALU.mult, ALU.add)


ROUND = 12582912.0


def xattn3_stage(P):
    nc = P.nc
    P.kT_dram = nc.dram_tensor("k_parts", (3, D, B, T), BF16).ap()
    P.qT_dram = nc.dram_tensor("q_parts", (3, D, N_TOK), BF16).ap()
    with Stage(nc, "xa3") as keep:
        values = keep.sb("values", [128, B * KN * D])
        P.v32 = values[0:KP].rearrange("p (n d) -> p n d", d=D)
        halves = values[0:KP].bitcast(BF16).rearrange("p (a n) -> p a n", a=4)
        P.v8 = values[0:KP].bitcast(BF16)[:, 0:B * KN * D].rearrange("p (n d) -> p n d", d=D)
        P.vpad = [halves[:, 2 + s, :].rearrange("p (n d) -> p n d", d=128) for s in range(2)]
        P.v_scale = keep.sb("v_scale", [128, 2])
        P.oT = keep.sb("oT", [128, 2, N_TOK])
        P.rden = keep.sb("rden", [TT, NT, H])
        xattn3_keys(P)
        xattn3_values_queries(P)
        xattn3_attend(P)
        xattn3_out(P)


def xattn3_keys(P):
    nc, dram = P.nc, P.dram
    KE = KP + 1
    with Stage(nc, "xa3k") as st:
        wkv, bkv = st.sb("wkv", [128, KT, 2 * D]), st.sb("bkv", [128, 2 * D])
        ident16 = st.sb("ident16", [128, 128], BF16)
        ctxT = [st.sb(f"ctxT{s}", [128, KT, T]) for s in range(2)]
        kb = [st.sb(f"kb{s}", [KP, KN, D]) for s in range(2)]
        ints = st.sb("ints", [KP, KN, D])
        scale, inv = ([st.sb(f"{n}{s}", [KP, KN, H]) for s in range(2)] for n in ("scale", "inv"))
        part = [st.sb(f"part{x}", [KP, KN, D], BF16) for x in range(3)]
        turned = [st.sb(f"turned{r}", [128, T], BF16) for r in range(2)]
        RING = 3
        RU = KN // RING
        kv_ps = [st.ps(f"kv{r}", [128, 512]) for r in range(RING)]
        turn_ps = [st.ps(f"turn{r}", [128, 2, 1024], BF16) for r in range(2)]
        loaded, ctx_loaded, ident_ready = st.sem("loaded"), st.sems("ctx_loaded", 2), st.sem("ident_ready")
        kv_done, kv_read = st.sems("kv_done", RING), st.sems("kv_read", RING)
        dve_step = st.sem("dve_step")
        ints_ready, khat_done = st.sems("ints_ready", 2), st.sems("khat_done", 2)
        part_done = [st.sems(f"part{x}_done", 2) for x in range(3)]
        part_turned = [st.sems(f"part{x}_turned", 2) for x in range(3)]
        rest_done = [st.sems(f"rest{x}_done", 2) for x in range(2)]
        turn_done, copied, stored = st.sems("turn_done", 2), st.sems("copied", 2), st.sems("stored", 2)
        st.start_at_one(ints_ready, kv_read, copied, part_done, khat_done, rest_done, turn_done, stored)
        block = st.block()

        def by_head(t):
            return t.rearrange("p n (h e) -> p (n h) e", e=HD)

        def wide(t):
            return t.rearrange("p n h -> p (n h)").unsqueeze(2).broadcast_to([KP, KN * H, HD])

        @block.sync
        def _(sp):
            sp.dma_start(wkv[:], dram["x3_wkv"].rearrange("(c p) n -> p c n", p=128)).then_inc(loaded, 16)
            sp.dma_start(bkv[:], dram["x3_bkv"]).then_inc(loaded, 16)
            with sp.Fori(0, B // 2) as i:
                for s in range(2):
                    sp.wait_ge(ints_ready[s], i + 1)
                    sp.dma_start(ctxT[s][:], dram["ctxT"][bass.ds(2 * i + s, 1)].rearrange("o (c p) t -> p (o c) t", p=128))\
                        .then_inc(ctx_loaded[s], 16)

        @block.tensor
        def _(pe):
            load_wait(pe, loaded, 2)
            pe.wait_ge(ident_ready, 1)
            with pe.Fori(0, B // 2) as i:
                for s in range(2):
                    b = 2 * i + s
                    pe.wait_ge(ctx_loaded[s], 16 * i + 16)
                    for n in range(KN):
                        pe.wait_ge(kv_read[n % RING], RU * b + n // RING + 1)
                        for c in range(KT):
                            last = nc.tensor.matmul(kv_ps[n % RING][0:KP, :], ctxT[s][:, c, n * KP:(n + 1) * KP], wkv[:, c, :],
                                                    start=(c == 0), stop=(c == KT - 1))
                        last.then_inc(kv_done[n % RING], 1)
                for s in range(2):
                    b = 2 * i + s
                    for x in range(3):
                        pe.wait_ge(part_done[x][s], i + 2)
                        for h in range(2):
                            pe.wait_ge(copied[h], 3 * b + x + 1)
                            for n in range(KN):
                                last = nc.tensor.transpose(turn_ps[h][:, n // 6, (n % 6) * KE:(n % 6) * KE + KP],
                                                           part[x][:, n, h * 128:(h + 1) * 128], ident16[0:KP, 0:KP])
                            last.then_inc(turn_done[h], 1)

        @block.gpsimd
        def _(pool):
            with pool.Fori(0, B // 2) as i:
                for s in range(2):
                    pool.wait_ge(ints_ready[s], i + 2)
                    nc.gpsimd.tensor_tensor(by_head(kb[s][:]), by_head(ints[:]), wide(scale[s][:]), ALU.mult).then_inc(khat_done[s], 1)
                for s in range(2):
                    pool.wait_ge(part_done[1][s], i + 2)
                    nc.gpsimd.tensor_tensor(kb[s][:], kb[s][:], part[1][:], ALU.subtract).then_inc(rest_done[1][s], 1)

        @block.scalar
        def _(act):
            with act.Fori(0, B // 2) as i:
                for s in range(2):
                    b = 2 * i + s
                    for x, source in enumerate((khat_done, rest_done[0], rest_done[1])):
                        act.wait_ge(source[s], i + 2)
                        if x == 0:
                            act.wait_ge(turn_done[1], 3 * b + 1)
                        act.wait_ge(copied[1], 3 * b + 1)
                        nc.scalar.activation(part[x][:], kb[s][:], ACT.Copy).then_inc(part_done[x][s], 1)
                        for h in range(2):
                            act.wait_ge(turn_done[h], 3 * b + x + 2)
                            act.wait_ge(stored[h], 16 * (3 * b + x) + 1)
                            nc.scalar.activation(turned[h][:].rearrange("p (a n t) -> p a n t", a=2, n=6),
                                                 turn_ps[h][:, :, 0:6 * KE].rearrange("p a (n t) -> p a n t", t=KE)[:, :, :, 0:KP], ACT.Copy).then_inc(copied[h], 1)
                            act.wait_ge(copied[h], 3 * b + x + 2)
                            act.dma_start(P.kT_dram[x, h * 128:(h + 1) * 128, bass.ds(b, 1), :].rearrange("p o t -> p (o t)"), turned[h][:])\
                                .then_inc(stored[h], 16)
            for h in range(2):
                act.wait_ge(stored[h], 16 * 3 * B + 1)

        @block.vector
        def _(dve):
            dve.wait_ge(loaded, 32)
            nc.vector.tensor_copy(ident16[:], P.ident[:]).then_inc(ident_ready, 1)
            with dve.Fori(0, B // 2) as i:
                for s in range(2):
                    b = 2 * i + s
                    dve.wait_ge(part_done[2][s], i + 1)
                    for n in range(KN):
                        dve.wait_ge(kv_done[n % RING], RU * b + n // RING + 1)
                        nc.vector.tensor_tensor(kb[s][:, n, :], kv_ps[n % RING][0:KP, 0:D], bkv[0:KP, 0:D], ALU.add)
                        nc.vector.tensor_tensor(P.v32[:, bass.ds(b * KN + n, 1), :].rearrange("p o d -> p (o d)"),
                                                kv_ps[n % RING][0:KP, D:2 * D], bkv[0:KP, D:2 * D], ALU.add)\
                            .then_inc(kv_read[n % RING], 1)
                    dve.wait_ge(kv_read[2], RU * b + RU + 1)
                    steps = [0]

                    def done(ins):
                        steps[0] += 1
                        ins.then_inc(dve_step, 1)
                        dve.wait_ge(dve_step, 4 * b + steps[0])
                    done(nc.vector.tensor_reduce(scale[s][:].rearrange("p n h -> p (n h)"), by_head(kb[s][:]), X_AXIS, ALU.max,
                                                 apply_absolute_value=True))
                    done(nc.vector.tensor_scalar(scale[s][:], scale[s][:], 1.0 / 127.0, 1e-8, ALU.mult, ALU.max))
                    done(nc.vector.reciprocal(inv[s][:], scale[s][:]))
                    dve.wait_ge(khat_done[1 - s], i + s + 1)
                    done(nc.vector.tensor_tensor(by_head(ints[:]), by_head(kb[s][:]), wide(inv[s][:]), ALU.mult))
                    nc.vector.tensor_scalar(ints[:], ints[:], ROUND, -ROUND, ALU.add, ALU.add).then_inc(ints_ready[s], 1)
                for s in range(2):
                    dve.wait_ge(part_done[0][s], i + 2)
                    nc.vector.tensor_tensor(kb[s][:], kb[s][:], part[0][:], ALU.subtract).then_inc(rest_done[0][s], 1)


def xattn3_values_queries(P):
    nc, dram = P.nc, P.dram
    with Stage(nc, "xa3q") as st:
        wq, bq = st.sb("wq", [128, KT, D]), st.sb("bq", [128, D])
        vmax, vscaled = st.sb("vmax", [KP, D]), [st.sb(f"vscaled{r}", [KP, KN, D]) for r in range(1)]
        vinv, vdiag = st.sb("vinv", [128, 2]), st.sb("vdiag", [128, 2, 128])
        vinv_row = st.sb("vinv_row", [KP, D])
        q, qi, = st.sb("q", [TT, NT, D]), st.sb("qi", [TT, NT, D])
        scale, inv = st.sb("scale", [TT, NT, H]), st.sb("inv", [TT, NT, H])
        part = [st.sb(f"part{x}", [TT, NT, D], BF16) for x in range(3)]
        ident16 = st.sb("ident16", [128, 128], BF16)
        partT = st.sb("partT", [128, 3, 2, N_TOK], BF16)
        q_ps = st.ps("q_ps", [128, NT, D])
        vt_ps, row_ps = st.ps("vt", [128, 512]), st.ps("row", [128, 512])
        turn_ps = [st.ps(f"turn{r}", [128, 1024], BF16) for r in range(2)]
        loaded, q_done, vmax_done, vt_done = st.sem("loaded"), st.sem("q_done"), st.sem("vmax_done"), st.sem("vt_done")
        diag_done, row_done, dve_step = st.sem("diag_done"), st.sem("row_done"), st.sem("dve_step")
        parts_done, turn_done, copied, stored = st.sem("parts_done"), st.sem("turn_done"), st.sem("copied"), st.sem("stored")
        block = st.block()

        @block.sync
        def _(sp):
            sp.dma_start(wq[:], dram["x3_wq"].rearrange("(c p) n -> p c n", p=128)).then_inc(loaded, 16)
            sp.dma_start(bq[:], dram["x3_bq"]).then_inc(loaded, 16)
            for x in range(3):
                sp.wait_ge(copied, 2 * x + 2)
                sp.dma_start(P.qT_dram[x].rearrange("(h p) t -> p h t", p=128), partT[:, x]).then_inc(stored, 16)
            sp.wait_ge(stored, 48)

        @block.tensor
        def _(pe):
            load_wait(pe, loaded, 2)
            for j in range(NT):
                for c in range(KT):
                    last = nc.tensor.matmul(q_ps[0:TT, j, :], P.xnT[:, c, j * TT:(j + 1) * TT], wq[:, c, :],
                                            start=(c == 0), stop=(c == KT - 1))
            last.then_inc(q_done, 1)
            pe.wait_ge(parts_done, 1)
            for x in range(3):
                for h in range(2):
                    k = 2 * x + h
                    if k >= 2:
                        pe.wait_ge(copied, k - 1)
                    for j in range(NT):
                        last = nc.tensor.transpose(turn_ps[k % 2][:, j * TT:(j + 1) * TT], part[x][:, j, h * 128:(h + 1) * 128],
                                                   ident16[0:TT, 0:TT])
                    last.then_inc(turn_done, 1)
            pe.wait_ge(vmax_done, 1)
            for h in range(2):
                last = nc.tensor.transpose(vt_ps[:, h * KP:(h + 1) * KP], vmax[:, h * 128:(h + 1) * 128], P.ident[0:KP, 0:KP])
            last.then_inc(vt_done, 1)
            pe.wait_ge(diag_done, 1)
            for h in range(2):
                last = nc.tensor.matmul(row_ps[0:KP, h * 128:(h + 1) * 128], P.ones[:, 0:KP], vdiag[:, h, :], start=True, stop=True)
            last.then_inc(row_done, 1)

        @block.scalar
        def _(act):
            for k in range(6):
                act.wait_ge(turn_done, k + 1)
                nc.scalar.activation(partT[:, k // 2, k % 2, :], turn_ps[k % 2][:, 0:N_TOK], ACT.Copy).then_inc(copied, 1)

        @block.vector
        def _(dve):
            link = in_order(dve, dve_step)
            load_wait(dve, loaded, 2)
            nc.vector.tensor_copy(ident16[:], P.ident[:])
            dve.wait_ge(q_done, 1)
            link(nc.vector.tensor_tensor(q[:], q_ps[0:TT], bq[0:TT, :].unsqueeze(1).broadcast_to([TT, NT, D]), ALU.add))
            link(nc.vector.tensor_scalar(q[:], q[:], 0.25, None, ALU.mult))

            def groups(t):
                return t.rearrange("p j (h e) -> p (j h) e", e=HD)

            def wide(t):
                return t.rearrange("p j h -> p (j h)").unsqueeze(2).broadcast_to([TT, NT * H, HD])
            link(nc.vector.tensor_reduce(scale[:].rearrange("p j h -> p (j h)"), groups(q[:]), X_AXIS, ALU.max, apply_absolute_value=True))
            link(nc.vector.tensor_scalar(scale[:], scale[:], 1.0 / 127.0, 1e-8, ALU.mult, ALU.max))
            link(nc.vector.reciprocal(inv[:], scale[:]))
            link(nc.vector.tensor_tensor(groups(qi[:]), groups(q[:]), wide(inv[:]), ALU.mult))
            link(nc.vector.tensor_scalar(qi[:], qi[:], ROUND, -ROUND, ALU.add, ALU.add))
            link(nc.vector.tensor_tensor(groups(q[:]), groups(qi[:]), wide(scale[:]), ALU.mult))
            for x in range(2):
                link(nc.vector.tensor_copy(part[x][:], q[:]))
                link(nc.vector.tensor_tensor(q[:], q[:], part[x][:], ALU.subtract))
            nc.vector.tensor_copy(part[2][:], q[:]).then_inc(parts_done, 1)
            nc.vector.tensor_reduce(vmax[:], P.v32.rearrange("p n d -> p d n"), X_AXIS, ALU.max, apply_absolute_value=True)\
                .then_inc(vmax_done, 1)
            dve.wait_ge(vt_done, 1)
            link(nc.vector.tensor_reduce(P.v_scale[:], vt_ps[:, 0:2 * KP].rearrange("p (h t) -> p h t", h=2), X_AXIS, ALU.max))
            link(nc.vector.tensor_scalar(P.v_scale[:], P.v_scale[:], 1.0 / 127.0, 1e-8, ALU.mult, ALU.max))
            link(nc.vector.reciprocal(vinv[:], P.v_scale[:]))
            for h in range(2):
                last = nc.vector.tensor_scalar(vdiag[:, h, :], P.ident[:], vinv[:, h:h + 1], None, ALU.mult)
            last.then_inc(diag_done, 1)
            dve.wait_ge(row_done, 1)
            link(nc.vector.tensor_copy(vinv_row[:], row_ps[0:KP, 0:D]))
            for b in range(B):
                link(nc.vector.tensor_tensor(vscaled[0][:], P.v32[:, b * KN:(b + 1) * KN, :],
                                             vinv_row[:].unsqueeze(1).broadcast_to([KP, KN, D]), ALU.mult))
                link(nc.vector.tensor_scalar(P.v8[:, b * KN:(b + 1) * KN, :], vscaled[0][:], ROUND, -ROUND, ALU.add, ALU.add))


def xattn3_attend(P):
    nc, dram = P.nc, P.dram
    NK = B * KN
    CHUNK = 3 * KC
    NA, NC = NT * (B * T // CHUNK), B * T // CHUNK
    NG = NK // 3
    PER = (NA + NG) // 2
    QROWS, MROWS = 6 * HD, 3
    K_PART, Q_PART = (0, 0, 0, 1, 1, 2), (0, 1, 2, 0, 1, 0)
    with Stage(nc, "xa3a") as st:
        kS = [st.sb(f"kS{s}", [QROWS + MROWS, B * T], BF16) for s in range(2)]
        qS = [st.sb(f"qS{s}", [QROWS + MROWS, N_TOK], BF16) for s in range(2)]
        vpad = P.vpad
        zeros = st.sb("zeros", [KP, N_TOK], BF16)
        ident16 = st.sb("ident16", [128, 128], BF16)
        e = [st.sb(f"e{r}", [KP, 3, N_TOK]) for r in range(2)]
        r8 = [st.sb(f"r8{r}", [KP, 3, N_TOK], BF16) for r in range(2)]
        negmax, esum = st.sb("negmax", [TT, NT, NC]), st.sb("esum", [TT, NT, NC])
        diff, corr = st.sb("diff", [TT, NT, NC]), st.sb("corr", [TT, NT, NC])
        negm, m_rest = st.sb("negm", [TT, NT]), st.sb("m_rest", [TT, NT])
        m_parts = st.sb("m_parts", [TT, NT, MROWS], BF16)
        den, rden_h = st.sb("den", [TT, NT]), st.sb("rden_h", [TT, NT])
        ln255 = st.sb("ln255", [128, 1])
        ring = [st.ps(f"ring{p}", [128, 3, 512]) for p in range(2)]
        misc_ps = st.ps("misc", [128, 1024], BF16)
        out_ps = st.ps("out", [128, 512])
        prep, head_loaded, head_done, vpad_ready = st.sem("prep"), st.sems("head_loaded", 2), st.sems("head_done", 2), st.sems("vpad_ready", 2)
        mm_done, exp_done = st.sems("mm_done", 2), st.sems("exp_done", 2)
        max_done, split_done, mT_done, m_ready = st.sem("max_done"), st.sem("split_done"), st.sem("mT_done"), st.sem("m_ready")
        diff_done, corr_done, rden_done = st.sem("diff_done"), st.sem("corr_done"), st.sem("rden_done")
        round_done, pv_done = st.sems("round_done", 2), st.sems("pv_done", 2)
        dve_step, half_done, half_read = st.sem("dve_step"), st.sem("half_done"), st.sem("half_read")
        pool_step = st.sem("pool_step")
        st.start_at_one(head_done, exp_done, round_done, pv_done)
        block = st.block()

        @block.sync
        def _(sp):
            for half in range(2):
                with sp.Fori(0, 4) as i:
                    for s in range(2):
                        sp.wait_ge(head_done[s], 4 * half + i + 1)
                        row = (8 * half + 2 * i + s) * HD
                        for g in range(6):
                            sp.dma_start(qS[s][g * HD:(g + 1) * HD, :], P.qT_dram[Q_PART[g], bass.ds(row, HD), :]).then_inc(head_loaded[s], 16)
                            sp.dma_start(kS[s][g * HD:(g + 1) * HD, :].rearrange("p (b t) -> p b t", b=B),
                                         P.kT_dram[K_PART[g], bass.ds(row, HD), :, :]).then_inc(head_loaded[s], 16)

        @block.gpsimd
        def _(pool):
            link = in_order(pool, pool_step)
            for s in range(2):
                link(nc.gpsimd.memset(vpad[s], 0.0))
                link(nc.gpsimd.memset(kS[s][QROWS:QROWS + MROWS, :], 1.0))
            link(nc.gpsimd.memset(zeros[:], 0.0))
            nc.gpsimd.memset(ln255[:], math.log(255.0)).then_inc(prep, 1)

        @block.tensor
        def _(pe):
            pe.wait_ge(prep, 2)
            for half in range(2):
                if half:
                    pe.wait_ge(half_read, 1)
                nc.tensor.matmul(out_ps[:, 0:N_TOK], zeros[:, 0:128], zeros[:], start=True, stop=False, skip_group_check=True)
                with pe.Fori(0, 4) as i:
                    for s in range(2):
                        h = 8 * half + 2 * i + s
                        hs = 4 * half + i
                        pe.wait_ge(head_loaded[s], 192 * hs + 192)
                        for a in range(NA):
                            p, j, c = a % 2, a // NC, a % NC
                            pe.wait_ge(exp_done[p], PER * h + a // 2 + 1)
                            for k in range(3):
                                t0 = c * CHUNK + k * KC
                                last = nc.tensor.matmul(ring[p][0:TT, k, 0:KC], qS[s][0:QROWS, j * TT:(j + 1) * TT],
                                                        kS[s][0:QROWS, t0:t0 + KC], start=True, stop=True)
                            last.then_inc(mm_done[p], 1)
                        pe.wait_ge(split_done, h + 1)
                        for j in range(NT):
                            last = nc.tensor.transpose(misc_ps[QROWS:QROWS + MROWS, j * TT:(j + 1) * TT], m_parts[:, j, :],
                                                       ident16[0:TT, 0:TT])
                        last.then_inc(mT_done, 1)
                        pe.wait_ge(m_ready, h + 1)

                        def weigh(g):
                            pe.wait_ge(round_done[g % 2], NG // 2 * h + g // 2 + 2)
                            if g == 0:
                                pe.wait_ge(vpad_ready[s], hs + 1)
                            for k in range(3):
                                last = nc.tensor.matmul(out_ps[:, 0:N_TOK], vpad[s][:, 3 * g + k, :], r8[g % 2][:, k, :],
                                                        start=False, stop=False, skip_group_check=True)
                            last.then_inc(pv_done[g % 2] if g < NG - 1 else head_done[s], 1)

                        for g in range(NG):
                            p = g % 2
                            pe.wait_ge(exp_done[p], PER * h + NA // 2 + g // 2 + 1)
                            for k in range(3):
                                t0 = (3 * g + k) * KP
                                last = nc.tensor.matmul(ring[p][0:KP, k, 0:N_TOK], kS[s][:, t0:t0 + KP], qS[s][:], start=True, stop=True)
                            last.then_inc(mm_done[p], 1)
                            if g >= 2:
                                weigh(g - 2)
                        weigh(NG - 2)
                        weigh(NG - 1)
                nc.tensor.matmul(out_ps[:, 0:N_TOK], zeros[:, 0:128], zeros[:], start=False, stop=True, skip_group_check=True)\
                    .then_inc(half_done, 1)

        @block.scalar
        def _(act):
            act.wait_ge(prep, 2)
            for half in range(2):
                with act.Fori(0, 4) as i:
                    for s in range(2):
                        h = 8 * half + 2 * i + s
                        for a in range(NA):
                            p, j, c = a % 2, a // NC, a % NC
                            act.wait_ge(max_done, NA * h + a + 1)
                            nc.scalar.activation(ring[p][0:TT, :, 0:KC], ring[p][0:TT, :, 0:KC], ACT.Exp,
                                                 bias=negmax[:, j, c:c + 1], accum_out=esum[:, j, c:c + 1]).then_inc(exp_done[p], 1)
                        act.wait_ge(mT_done, h + 1)
                        nc.scalar.activation(qS[s][QROWS:QROWS + MROWS, :], misc_ps[QROWS:QROWS + MROWS, 0:N_TOK], ACT.Copy)\
                            .then_inc(m_ready, 1)
                        for g in range(NG):
                            p = g % 2
                            act.wait_ge(mm_done[p], PER * h + NA // 2 + g // 2 + 1)
                            act.wait_ge(round_done[p], NG // 2 * h + g // 2 + 1)
                            nc.scalar.activation(e[p][:], ring[p][0:KP, :, 0:N_TOK], ACT.Exp, bias=ln255[0:KP, :]).then_inc(exp_done[p], 1)
                            if g == 1:
                                act.wait_ge(diff_done, h + 1)
                                nc.scalar.activation(corr[:], diff[:], ACT.Exp).then_inc(corr_done, 1)
                act.wait_ge(half_done, half + 1)
                nc.scalar.activation(P.oT[:, half, :], out_ps[:, 0:N_TOK], ACT.Copy, scale=P.v_scale[:, half:half + 1]).then_inc(half_read, 1)

        @block.vector
        def _(dve):
            nc.vector.tensor_copy(ident16[:], P.ident[:]).then_inc(prep, 1)
            dve.wait_ge(prep, 2)
            for half in range(2):
                with dve.Fori(0, 4) as i:
                    for s in range(2):
                        h = 8 * half + 2 * i + s
                        hs = 4 * half + i
                        dve.wait_ge(head_done[s], hs + 1)
                        steps = [0]

                        def done(ins):
                            steps[0] += 1
                            ins.then_inc(dve_step, 1)
                            dve.wait_ge(dve_step, 9 * h + steps[0])
                        done(nc.vector.tensor_scalar(vpad[s][:, :, bass.ds((i + 3) % 4 * (2 * HD) + s * HD, HD)], P.v8[:, :, 0:HD], 0.0, None,
                                                     ALU.mult))
                        nc.vector.tensor_scalar(vpad[s][:, :, bass.ds((2 * i + s) * HD, HD)], P.v8[:, :, bass.ds(h * HD, HD)],
                                                1.0, None, ALU.mult).then_inc(vpad_ready[s], 1)
                        for a in range(NA):
                            p, j, c = a % 2, a // NC, a % NC
                            dve.wait_ge(mm_done[p], PER * h + a // 2 + 1)
                            nc.vector.tensor_reduce(negmax[:, j, c:c + 1], ring[p][0:TT, :, 0:KC], XY_AXES, ALU.max, negate=True)\
                                .then_inc(max_done, 1)
                        dve.wait_ge(max_done, NA * h + NA)
                        done(nc.vector.tensor_reduce(negm[:], negmax[:], X_AXIS, ALU.min))
                        done(nc.vector.tensor_copy(m_parts[:, :, 0], negm[:]))
                        done(nc.vector.tensor_tensor(m_rest[:], negm[:], m_parts[:, :, 0], ALU.subtract))
                        done(nc.vector.tensor_copy(m_parts[:, :, 1], m_rest[:]))
                        done(nc.vector.tensor_tensor(m_rest[:], m_rest[:], m_parts[:, :, 1], ALU.subtract))
                        nc.vector.tensor_copy(m_parts[:, :, 2], m_rest[:]).then_inc(split_done, 1)
                        nc.vector.tensor_tensor(diff[:], negm[:].unsqueeze(2).broadcast_to([TT, NT, NC]), negmax[:], ALU.subtract)\
                            .then_inc(diff_done, 1)
                        for g in range(NG):
                            p = g % 2
                            dve.wait_ge(exp_done[p], PER * h + NA // 2 + g // 2 + 2)
                            if g // 2:
                                dve.wait_ge(pv_done[p], (NG // 2 - p) * h + g // 2 + 1)
                            elif p == 0:
                                dve.wait_ge(pv_done[0], NG // 2 * h + 1)
                            else:
                                dve.wait_ge(head_done[1 - s], hs + s + 1)
                            nc.vector.tensor_scalar(r8[p][:], e[p][:], ROUND, -ROUND, ALU.add, ALU.add).then_inc(round_done[p], 1)
                            if g == 2:
                                dve.wait_ge(corr_done, h + 1)
                                done(nc.vector.tensor_tensor(corr[:], corr[:], esum[:], ALU.mult))
                                done(nc.vector.tensor_reduce(den[:], corr[:], X_AXIS, ALU.add))
                                done(nc.vector.reciprocal(rden_h[:], den[:]))
                                nc.vector.tensor_scalar(P.rden[:, :, bass.ds(h, 1)].rearrange("p j o -> p (j o)"), rden_h[:], 1.0 / 255.0, None,
                                                        ALU.mult)

def xattn3_out(P):
    nc, dram = P.nc, P.dram
    with Stage(nc, "xa3o") as st:
        wp, bp = st.sb("wp", [128, 2, D]), st.sb("bp", [128, D])
        wide = st.sb("wide", [TT, NT, D])
        delta = st.sb("delta", [TT, NT, D])
        turn_ps = [st.ps(f"turn{h}", [128, 512]) for h in range(2)]
        o_ps = st.ps("o", [128, NT, D])
        loaded, wide_done, turn_done, oT_ready, o_done = (
            st.sem(n) for n in ("loaded", "wide_done", "turn_done", "oT_ready", "o_done"))
        dve_step = st.sem("dve_step")
        block = st.block()

        @block.sync
        def _(sp):
            sp.dma_start(wp[:], dram["x3_wp"].rearrange("(c p) n -> p c n", p=128)).then_inc(loaded, 16)
            sp.dma_start(bp[:], dram["x3_bp"]).then_inc(loaded, 16)

        @block.tensor
        def _(pe):
            pe.wait_ge(wide_done, 1)
            for h in range(2):
                for j in range(NT):
                    last = nc.tensor.transpose(turn_ps[h][:, j * TT:(j + 1) * TT], wide[:, j, h * 128:(h + 1) * 128],
                                               P.ident[0:TT, 0:TT])
                last.then_inc(turn_done, 1)
            load_wait(pe, loaded, 2)
            pe.wait_ge(oT_ready, 2)
            for j in range(NT):
                for h in range(2):
                    last = nc.tensor.matmul(o_ps[0:TT, j, :], P.oT[:, h, j * TT:(j + 1) * TT], wp[:, h, :],
                                            start=(h == 0), stop=(h == 1))
            last.then_inc(o_done, 1)

        @block.vector
        def _(dve):
            link = in_order(dve, dve_step)
            nc.vector.tensor_copy(wide[:].rearrange("p j (h e) -> p (j h) e", e=HD),
                                  P.rden[:].rearrange("p j h -> p (j h)").unsqueeze(2).broadcast_to([TT, NT * H, HD])).then_inc(wide_done, 1)
            for h in range(2):
                dve.wait_ge(turn_done, h + 1)
                nc.vector.tensor_tensor(P.oT[:, h, :], P.oT[:, h, :], turn_ps[h][:, 0:N_TOK], ALU.mult).then_inc(oT_ready, 1)
            dve.wait_ge(o_done, 1)
            link(nc.vector.tensor_tensor(delta[:], o_ps[0:TT], bp[0:TT, :].unsqueeze(1).broadcast_to([TT, NT, D]), ALU.add))
            nc.vector.scalar_tensor_tensor(P.x[:], delta[:], P.gates[0:TT, 3:4], P.x[:], ALU.mult, ALU.add)


def finish_stage(P):
    with Stage(P.nc, "finish") as st:
        stored = st.sem("stored")
        block = st.block()

        @block.sync
        def _(sp):
            sp.dma_start(P.out.rearrange("(j p) d -> p j d", p=TT), P.x[:]).then_inc(stored, 16)
            sp.wait_ge(stored, 16)


def build_program(nc, dram, out):
    P = Program(nc, dram, out)
    with ExitStack() as stack:
        def sb(name, shape, dt=FP32):
            return stack.enter_context(nc.sbuf_tensor("s_" + name, shape, dt))
        P.x, P.xn = sb("x", [TT, NT, D]), sb("xn", [TT, NT, D])
        P.xnT = sb("xnT", [128, KT, N_TOK])
        P.ident, P.ones = sb("ident", [128, 128]), sb("ones", [128, 128])
        P.head_mask, P.iota = sb("head_mask", [128, 8]), sb("iota", [128, 32])
        P.gates = sb("gates", [128, 9])
        setup_stage(P)
        stages = [
            lambda: xattn0_stage(P),
            lambda: ffn_stage(P, 0, 8, 8, 96, "softmax_of_top", list(range(8))),
            lambda: xattn1_stage(P),
            lambda: ffn_stage(P, 1, 32, 32, 96, "top8", list(range(32))),
            lambda: xattn2_stage(P),
            lambda: ffn_stage(P, 2, 8, 20, 88, "softmax", [e for e in range(8) for _ in range(2)] + [None] * 4),
            lambda: xattn3_stage(P),
            lambda: ffn_stage(P, 3, 16, 18, 128, "sigmoid", list(range(16)) + [None] * 2, biased=True),
        ]
        for k, stage in enumerate(stages):
            if k not in STAGES:
                continue
            norm_stage(P, k)
            stage()
        finish_stage(P)


STAGES = range(8)


def laid_out(i):
    A = np.ascontiguousarray
    d = {}
    i = {k: np.asarray(v) for k, v in i.items()}

    def rows(a):
        return np.broadcast_to(a, (128, a.size))

    def halves(a):
        return a.reshape(2, 128).T
    p = np.arange(128)
    d["x"] = i["x"].reshape(N_TOK, D)
    d["ctxT"] = i["ctx_2048"].transpose(0, 2, 1)
    d["ident"] = np.eye(128, dtype=np.float32)
    d["head_mask"] = (p[:, None] // HD == np.arange(8)[None]).astype(np.float32)
    d["iota"] = np.broadcast_to(np.arange(32, dtype=np.float32), (128, 32))
    d["g_xattn"], d["g_ffn"] = rows(i["g_xattn"]), rows(i["g_ffn"])
    d["rs"] = rows(i["L0_xattn_residual_scale"].reshape(1))
    for n, s in (("wq", "Wq"), ("wk", "Wk"), ("wv", "Wv"), ("wo", "Wo")):
        d[f"x0_{n}"] = i[f"L0_xattn_{s}"].T
    d["x0_bq"], d["x0_bk"] = halves(i["L0_xattn_bq"]), halves(i["L0_xattn_bk"])
    for n, s in (("bv", "bv"), ("bo", "bo"), ("gamma", "ln_gamma"), ("beta", "ln_beta")):
        d[f"x0_{n}"] = rows(i[f"L0_xattn_{s}"])
    d["mask0"] = i["mask_BxS2_ik0"].reshape(B * KN, KP).T

    def gate_up(g, u):
        a = np.stack([g, u], 2)
        return a.reshape(a.shape[0], KT, 128, 2, a.shape[-1]).transpose(0, 2, 1, 3, 4).reshape(a.shape[0], 128, -1)

    def tr(a):
        return a.transpose(0, 2, 1)
    d["f0_router"] = i["L0_ffn_w_gate_router"].T
    d["f0_w_in"] = gate_up(tr(i["L0_ffn_w_gate_proj"]), tr(i["L0_ffn_w_up_proj"]))
    d["f0_w_down"] = tr(i["L0_ffn_w_down_proj"])
    d["f1_router"] = i["L1_ffn_gate_w"].T
    d["f1_w_in"] = gate_up(tr(i["L1_ffn_Wg"]), tr(i["L1_ffn_Wu"]))
    d["f1_w_down"] = tr(i["L1_ffn_Wd"])

    def blocks(a, f):
        e, dd, w = a.shape
        return a.reshape(e, dd, w // f, f).transpose(0, 2, 1, 3).reshape(e * w // f, dd, f)
    F = 88
    g = np.concatenate([blocks(i["L2_ffn_We_gate"], F), blocks(i["L2_ffn_Ws_gate"][None], F)])
    u = np.concatenate([blocks(i["L2_ffn_We_up"], F), blocks(i["L2_ffn_Ws_up"][None], F)])
    d["f2_router"] = i["L2_ffn_W_router"]
    d["f2_w_in"] = gate_up(g, u)
    d["f2_w_down"] = np.concatenate([i["L2_ffn_We_down"].reshape(-1, F, D), i["L2_ffn_Ws_down"].reshape(-1, F, D)])
    c3 = lambda r, s: np.concatenate([i[f"L3_ffn_{r}"], i[f"L3_ffn_{s}"]])
    d["f3_router"] = i["L3_ffn_wa"]
    d["f3_w_in"] = np.concatenate([gate_up(c3("rg", "sg"), c3("rw1", "sw1")), c3("rgb", "sgb")[:, :, None],
                                   c3("rb1", "sb1")[:, :, None]], 2)
    d["f3_w_down"] = c3("rw2", "sw2")
    d["f3_b_down"] = c3("rb2", "sb2")
    wq = i["L1_xattn_Wq"].reshape(D, 4, 4, HD).transpose(0, 2, 1, 3)
    d["x1_wq"] = wq.reshape(D, D)
    d["x1_wk"], d["x1_wv"] = i["L1_xattn_Wk"], i["L1_xattn_Wv"]
    d["x1_wo"] = i["L1_xattn_Wo"].reshape(4, 4, HD, D).transpose(0, 2, 1, 3).reshape(64, 4, D)
    d["mask1"] = i["mask_BxS2_bf1"].view(np.uint8)
    slope = (np.float32(2.0 ** -0.5) ** np.arange(1, H + 1, dtype=np.float32)).astype(np.float32)
    q_rows = np.zeros((2, 4, 4, S), np.float32)
    q_rows[0] = slope.reshape(4, 4, 1)
    q_rows[1] = -slope.reshape(4, 4, 1) * np.arange(S, dtype=np.float32)
    d["x1_q_rows"] = q_rows.reshape(2, H * S)
    d["x1_k_rows"] = np.stack([np.arange(T, dtype=np.float32), np.ones(T, np.float32)])
    d["x2_wq"], d["x2_wg"], d["x2_wkv"], d["x2_wo"] = (i[f"L2_xattn_{s}"].T for s in ("Wq", "Wg", "Wkv", "Wo"))
    d["x2_bg"] = halves(i["L2_xattn_bg"])
    d["block_mask"] = (p[:, None] // HD == p[None] // HD).astype(np.float32)
    d["x3_wq"], d["x3_wp"] = i["L3_xattn_Wq"], i["L3_xattn_Wp"]
    d["x3_wkv"] = i["L3_xattn_Wkv"]
    d["x3_bq"], d["x3_bp"], d["x3_bkv"] = rows(i["L3_xattn_bq"]), rows(i["L3_xattn_bp"]), rows(i["L3_xattn_bkv"])
    return {k: A(v) for k, v in d.items()}


def kernel(**inputs):
    import concourse.bacc as bacc
    from concourse.bass_utils import run_bass_kernel_spmd

    nc = bacc.Bacc("TRN2", target_bir_lowering=False, num_devices=1)
    arrays = laid_out(inputs)
    dram = {k: nc.dram_tensor("in_" + k, a.shape, mybir.dt.from_np(a.dtype), kind="ExternalInput").ap() for k, a in arrays.items()}
    out = nc.dram_tensor("out", (N_TOK, D), FP32, kind="ExternalOutput").ap()
    build_program(nc, dram, out)
    got = run_bass_kernel_spmd(nc, [{"in_" + k: a for k, a in arrays.items()}], core_ids=[0])
    return got.results[0]["out"].reshape(B, S, D)
```

```python
import math
import numpy as np
import concourse.bass as bass
from concourse import mybir
from contextlib import ExitStack

FP32 = mybir.dt.float32
BF16 = mybir.dt.bfloat16
U32 = mybir.dt.uint32
I32 = mybir.dt.int32
U8 = mybir.dt.uint8
ALU = mybir.AluOpType
ACT = mybir.ActivationFunctionType
X_AXIS = mybir.AxisListType.X
XY_AXES = mybir.AxisListType.XY

B, S, D = 8, 56, 256
N_TOK = B * S
TT, NT = 112, 4
T = 1500
KP, KN = 125, 12
KC = 500
H, HD = 16, 16
KT = D // 128
EPS_LN = 1e-5


class Program:

    def __init__(self, nc, dram, out):
        self.nc, self.dram, self.out = nc, dram, out


class Stage:

    def __init__(self, nc, name):
        self.nc, self.name, self.stack, self.semaphores = nc, name, ExitStack(), []

    def sb(self, name, shape, dt=FP32):
        return self.stack.enter_context(self.nc.sbuf_tensor(f"{self.name}_{name}", shape, dt))

    def ps(self, name, shape, dt=FP32):
        return self.stack.enter_context(self.nc.psum_tensor(f"{self.name}_{name}_ps", shape, dt))

    def sem(self, name):
        self.semaphores.append(self.stack.enter_context(self.nc.semaphore(f"{self.name}_{name}")))
        return self.semaphores[-1]

    def sems(self, name, n):
        return [self.sem(f"{name}{k}") for k in range(n)]

    def start_at_one(self, *semaphores):
        flat = list(semaphores)
        while any(isinstance(x, list) for x in flat):
            flat = [y for x in flat for y in (x if isinstance(x, list) else [x])]
        for k, x in enumerate(flat):
            (self.nc.sync, self.nc.gpsimd, self.nc.scalar, self.nc.vector)[k % 4].sem_inc(x, 1)

    def block(self):
        self.programs = ExitStack()
        return self.programs.enter_context(self.nc.Block())

    def __enter__(self):
        return self

    def __exit__(self, *e):
        if self.semaphores:
            self.programs.close()
            numbers = sorted(s.num for s in self.semaphores)
            starts = [a for a in numbers if a - 1 not in numbers]
            ends = [a + 1 for a in numbers if a + 1 not in numbers]
            for start, end in zip(starts, ends):
                self.nc.gpsimd.sem_clear(range(start, end))
            self.nc.all_engine_barrier()
        return self.stack.__exit__(*e)


def in_order(engine, sem, start=0):
    count = [start]

    def link(instruction):
        count[0] += 1
        instruction.then_inc(sem, 1)
        engine.wait_ge(sem, count[0])
        return count[0]
    return link


def setup_stage(P):
    nc = P.nc
    with Stage(nc, "setup") as st:
        loaded, gates_raw_ready = st.sem("loaded"), st.sem("gates_raw_ready")
        raw = st.sb("raw", [128, 9])
        block = st.block()

        @block.sync
        def _(sp):
            sp.dma_start(P.x[:], P.dram["x"].rearrange("(j p) d -> p j d", p=TT)).then_inc(loaded, 16)
            sp.dma_start(P.ident[:], P.dram["ident"]).then_inc(loaded, 16)
            sp.dma_start(P.head_mask[:], P.dram["head_mask"]).then_inc(loaded, 16)
            sp.dma_start(P.iota[:], P.dram["iota"]).then_inc(loaded, 16)
            sp.dma_start(raw[:, 0:4], P.dram["g_xattn"]).then_inc(loaded, 16)
            sp.dma_start(raw[:, 4:8], P.dram["g_ffn"]).then_inc(loaded, 16)
            sp.dma_start(raw[:, 8:9], P.dram["rs"]).then_inc(loaded, 16)
            sp.wait_ge(loaded, 7 * 16)

        @block.scalar
        def _(act):
            act.wait_ge(loaded, 7 * 16)
            nc.scalar.activation(P.gates[:, 0:8], raw[:, 0:8], ACT.Tanh)

        @block.vector
        def _(dve):
            dve.wait_ge(loaded, 7 * 16)
            nc.vector.tensor_scalar(P.gates[:, 8:9], raw[:, 8:9], 0.0, 0.3, ALU.max, ALU.min)
            nc.vector.memset(P.ones[:], 1.0)


def norm_stage(P, k, early):
    nc = P.nc
    with Stage(nc, f"norm{k}") as st:
        stats = st.sb("stats", [TT, NT, 6])
        mean_var = st.sb("mean_var", [TT, NT, 2])
        var_eps = st.sb("var_eps", [TT, NT])
        std = st.sb("std", [TT, NT])
        rstd = st.sb("rstd", [TT, NT])
        turned = [st.ps(f"turned{c}", [128, 512]) for c in range(KT)]
        dve_step, var_ready, std_ready = st.sem("dve_step"), st.sem("var_ready"), st.sem("std_ready")
        xn_ready, turned_done = st.sem("xn_ready"), st.sems("turned_done", KT)
        block = st.block()

        @block.sync
        def _(sp):
            early(sp)

        @block.vector
        def _(dve):
            link = in_order(dve, dve_step)
            for j in range(NT):
                last = nc.vector.bn_stats(stats[:, j, :], P.x[:, j, :])
            link(last)
            for j in range(NT):
                last = nc.vector.bn_aggr(mean_var[:, j, :], stats[:, j, :])
            link(last)
            nc.vector.tensor_scalar(var_eps[:], mean_var[:, :, 1], EPS_LN, None, ALU.add).then_inc(var_ready, 1)
            dve.wait_ge(std_ready, 1)
            link(nc.vector.reciprocal(rstd[:], std[:]))
            for j in range(NT):
                nc.vector.tensor_scalar(P.xn[:, j, :], P.x[:, j, :], mean_var[:, j, 0:1], rstd[:, j:j + 1],
                                        ALU.subtract, ALU.mult).then_inc(xn_ready, 1)
            dve.wait_ge(turned_done[0], NT)
            nc.vector.tensor_copy(P.xnT[:, 0, :], turned[0][:, 0:N_TOK])

        @block.scalar
        def _(act):
            act.wait_ge(var_ready, 1)
            nc.scalar.activation(std[:], var_eps[:], ACT.Sqrt).then_inc(std_ready, 1)
            act.wait_ge(turned_done[1], NT)
            nc.scalar.activation(P.xnT[:, 1, :], turned[1][:, 0:N_TOK], ACT.Copy)

        @block.tensor
        def _(pe):
            for j in range(NT):
                pe.wait_ge(xn_ready, j + 1)
                for c in range(KT):
                    nc.tensor.transpose(turned[c][:, j * TT:(j + 1) * TT], P.xn[:, j, c * 128:(c + 1) * 128],
                                        P.ident[0:TT, 0:TT]).then_inc(turned_done[c], 1)


def ffn_stage(P, k, E, n, F, routing, weight_e, biased=False):
    nc, dram = P.nc, P.dram
    with Stage(nc, f"ffn{k}") as st:
        router_w = st.sb("router_w", [128, KT, E])
        n_in = KT * 2 * F + 2 * biased
        w_all = st.sb("w_all", [128, 2, n_in])
        w_in = w_all[:, :, 0:KT * 2 * F].rearrange("p s (c g f) -> p s c g f", c=KT, g=2)
        w_down = st.sb("w_down", [F, 2, D])
        act_g = st.sb("act_g", [F, 2, N_TOK])
        hT = st.sb("hT", [F, 2, N_TOK])
        acc = st.sb("acc", [TT, NT, D])
        logits = st.sb("logits", [TT, NT, E])
        probs = st.sb("probs", [TT, NT, E])
        top = st.sb("top", [TT, NT, 8])
        top_at = st.sb("top_at", [TT, NT, 8], U32)
        top_at_f = st.sb("top_at_f", [TT, NT, 8])
        share = st.sb("share", [TT, NT, 2])
        tmp = st.sb("tmp", [TT, NT, E])
        rowmax = st.sb("rowmax", [TT, NT])
        rowsum = st.sb("rowsum", [TT, NT])
        rowinv = st.sb("rowinv", [TT, NT])
        w_e = st.sb("w_e", [TT, NT, E])
        w_blk = st.sb("w_blk", [TT, NT, n])
        if biased:
            b_gate, b_up = w_all[0:F, :, n_in - 2:n_in - 1], w_all[0:F, :, n_in - 1:n_in]
            b_down = st.sb("b_down", [n, D])
            w_blkT = st.sb("w_blkT", [n, N_TOK])
        small_loaded, in_loaded, down_loaded = st.sem("small_loaded"), st.sems("in_loaded", 2), st.sems("down_loaded", 2)

        def load_in(sp, b, s):
            sp.dma_start(w_all[:, s, :], dram[f"f{k}_w_in"][bass.ds(b, 1)].rearrange("o p m -> p (o m)")).then_inc(in_loaded[s], 16)

        def load_down(sp, b, s):
            sp.dma_start(w_down[:, s, :], dram[f"f{k}_w_down"][bass.ds(b, 1)].rearrange("o f d -> f (o d)")).then_inc(down_loaded[s], 16)

        def early(sp):
            sp.dma_start(router_w[:], dram[f"f{k}_router"].rearrange("(c p) e -> p c e", p=128)).then_inc(small_loaded, 16)
            if biased:
                sp.dma_start(b_down[:], dram[f"f{k}_b_down"]).then_inc(small_loaded, 16)
            for s in range(2):
                load_in(sp, s, s)
                load_down(sp, s, s)
        norm_stage(P, 2 * k + 1, early)
        gate_ps = [st.ps(f"gate{s}", [128, 512]) for s in range(2)]
        up_ps = [st.ps(f"up{s}", [128, 512]) for s in range(2)]
        down_ps = [st.ps(f"down{s}", [128, NT, D]) for s in range(2)]
        act_ready, gate_done = st.sems("act_ready", 2), st.sems("gate_done", 2)
        up_done, h_ready = st.sems("up_done", 2), st.sems("h_ready", 2)
        down_done, acc_done = st.sems("down_done", 2), st.sems("acc_done", 2)
        router_done, dve_step, logits_ready = st.sem("router_done"), st.sem("dve_step"), st.sem("logits_ready")
        exp_ready, weights_ready = st.sem("exp_ready"), st.sem("weights_ready")
        wT_done, wT_ready, bias_done, acc_ready = (st.sem("wT_done"), st.sem("wT_ready"), st.sem("bias_done"),
                                                   st.sem("acc_ready"))
        st.start_at_one(down_done, h_ready, acc_done)
        block = st.block()
        n_small = 1 + biased

        @block.sync
        def _(sp):
            with sp.Fori(0, n // 2 - 1) as i:
                for s in range(2):
                    sp.wait_ge(h_ready[s], i + 2)
                    load_in(sp, 2 * i + 2 + s, s)
                for s in range(2):
                    sp.wait_ge(down_done[s], i + 2)
                    load_down(sp, 2 * i + 2 + s, s)

        @block.tensor
        def _(pe):
            pe.wait_ge(small_loaded, 16 * n_small)
            for j in range(NT):
                for c in range(KT):
                    last = nc.tensor.matmul(down_ps[0][0:TT, j, 0:E], P.xnT[:, c, j * TT:(j + 1) * TT], router_w[:, c, :],
                                            start=(c == 0), stop=(c == KT - 1))
            last.then_inc(router_done, 1)
            if biased:
                pe.wait_ge(weights_ready, 1)
                for j in range(NT):
                    last = nc.tensor.transpose(down_ps[1][0:n, j, 0:TT], w_blk[:, j, :], P.ident[0:TT, 0:TT])
                last.then_inc(wT_done, 1)
                pe.wait_ge(wT_ready, 1)
                for j in range(NT):
                    last = nc.tensor.matmul(down_ps[0][0:TT, j, :], w_blkT[:, j * TT:(j + 1) * TT], b_down[:],
                                            start=True, stop=True)
                last.then_inc(bias_done, 1)
                pe.wait_ge(acc_ready, 1)
            else:
                pe.wait_ge(dve_step, 1)
            with pe.Fori(0, n // 2) as i:
                for s in range(2):
                    pe.wait_ge(in_loaded[s], 16 * i + 16)
                    pe.wait_ge(h_ready[s], i + 1)
                    for g, bank, done in ((0, gate_ps[s], gate_done[s]), (1, up_ps[s], up_done[s])):
                        for c in range(KT):
                            last = nc.tensor.matmul(bank[0:F, 0:N_TOK], w_in[:, s, c, g, :], P.xnT[:, c, :],
                                                    start=(c == 0), stop=(c == KT - 1))
                        last.then_inc(done, 1)
                for s in range(2):
                    pe.wait_ge(down_loaded[s], 16 * i + 16)
                    pe.wait_ge(h_ready[s], i + 2)
                    pe.wait_ge(acc_done[s], i + 1)
                    for j in range(NT):
                        last = nc.tensor.matmul(down_ps[s][0:TT, j, :], hT[:, s, j * TT:(j + 1) * TT], w_down[:, s, :],
                                                start=True, stop=True)
                    last.then_inc(down_done[s], 1)

        @block.scalar
        def _(act):
            act.wait_ge(logits_ready, 1)
            if routing == "softmax_of_top":
                nc.scalar.activation(share[:, :, 1:2], share[:, :, 0:1], ACT.Exp).then_inc(exp_ready, 1)
            elif routing == "sigmoid":
                nc.scalar.activation(probs[:], logits[:], ACT.Sigmoid).then_inc(exp_ready, 1)
            else:
                nc.scalar.activation(probs[:], logits[:], ACT.Exp).then_inc(exp_ready, 1)
            act.wait_ge(small_loaded, 16 * n_small)
            with act.Fori(0, n // 2) as i:
                for s in range(2):
                    act.wait_ge(gate_done[s], i + 1)
                    act.wait_ge(h_ready[s], i + 1)
                    if biased:
                        nc.scalar.activation(act_g[:, s, :], gate_ps[s][0:F, 0:N_TOK], ACT.Gelu,
                                             bias=b_gate[:, s]).then_inc(act_ready[s], 1)
                    else:
                        nc.scalar.activation(act_g[:, s, :], gate_ps[s][0:F, 0:N_TOK], ACT.Silu).then_inc(act_ready[s], 1)

        @block.vector
        def _(dve):
            link = in_order(dve, dve_step)
            dve.wait_ge(router_done, 1)
            link(nc.vector.tensor_copy(logits[:], down_ps[0][0:TT, :, 0:E]))
            if routing == "softmax_of_top":
                ranked = logits
                for j in range(NT):
                    link(nc.vector.max(top[:, j, :], logits[:, j, :]))
                nc.vector.tensor_tensor(share[:, :, 0:1], top[:, :, 1:2], top[:, :, 0:1], ALU.subtract).then_inc(logits_ready, 1)
                dve.wait_ge(exp_ready, 1)
                link(nc.vector.tensor_scalar(rowsum[:], share[:, :, 1], 1.0, None, ALU.add))
                link(nc.vector.reciprocal(share[:, :, 0], rowsum[:]))
                link(nc.vector.tensor_tensor(share[:, :, 1], share[:, :, 1], share[:, :, 0], ALU.mult))
            else:
                ranked = probs
                if routing == "sigmoid":
                    nc.vector.tensor_copy(tmp[:, 0, 0:1], logits[:, 0, 0:1]).then_inc(logits_ready, 1)
                    dve.wait_ge(exp_ready, 1)
                else:
                    link(nc.vector.tensor_reduce(rowmax[:], logits[:], X_AXIS, ALU.max))
                    nc.vector.tensor_tensor(logits[:], logits[:], rowmax[:].unsqueeze(2).broadcast_to([TT, NT, E]),
                                            ALU.subtract).then_inc(logits_ready, 1)
                    dve.wait_ge(exp_ready, 1)
                    link(nc.vector.tensor_reduce(rowsum[:], probs[:], X_AXIS, ALU.add))
                    link(nc.vector.reciprocal(rowinv[:], rowsum[:]))
                    link(nc.vector.tensor_tensor(probs[:], probs[:], rowinv[:].unsqueeze(2).broadcast_to([TT, NT, E]), ALU.mult))
                for j in range(NT):
                    link(nc.vector.max(top[:, j, :], probs[:, j, :]))
                if routing == "softmax":
                    link(nc.vector.tensor_copy(share[:], top[:, :, 0:2]))
                elif routing == "sigmoid":
                    link(nc.vector.tensor_reduce(rowsum[:], top[:, :, 0:2], X_AXIS, ALU.add))
                    link(nc.vector.reciprocal(rowinv[:], rowsum[:]))
                    link(nc.vector.tensor_tensor(share[:], top[:, :, 0:2], rowinv[:].unsqueeze(2).broadcast_to([TT, NT, 2]), ALU.mult))
            if routing == "top8":
                link(nc.vector.tensor_reduce(rowsum[:], top[:], X_AXIS, ALU.add))
                link(nc.vector.reciprocal(rowinv[:], rowsum[:]))
                for j in range(NT):
                    link(nc.vector.match_replace(tmp[:, j, :], top[:, j, :], probs[:, j, :], -1.0))
                link(nc.vector.tensor_tensor(tmp[:], tmp[:], probs[:], ALU.not_equal))
                link(nc.vector.tensor_tensor(tmp[:], tmp[:], probs[:], ALU.mult))
                link(nc.vector.tensor_tensor(w_e[:], tmp[:], rowinv[:].unsqueeze(2).broadcast_to([TT, NT, E]), ALU.mult))
            else:
                for j in range(NT):
                    link(nc.vector.max_index(top_at[:, j, :], top[:, j, :], ranked[:, j, :]))
                link(nc.vector.tensor_copy(top_at_f[:], top_at[:]))
                for j in range(NT):
                    for r, to in ((0, w_e), (1, tmp)):
                        link(nc.vector.tensor_scalar(to[:, j, :], P.iota[0:TT, 0:E], top_at_f[:, j, r:r + 1],
                                                     share[:, j, r:r + 1], ALU.is_equal, ALU.mult))
                link(nc.vector.tensor_tensor(w_e[:], w_e[:], tmp[:], ALU.add))
            per = sum(e == 0 for e in weight_e)
            routed = per * E
            if routed < n:
                link(nc.vector.memset(w_blk[:, :, routed:n], 1.0))
            last = nc.vector.tensor_copy(w_blk[:, :, 0:routed].rearrange("p j (e r) -> p j e r", r=per),
                                         w_e[:].unsqueeze(3).broadcast_to([TT, NT, E, per]))
            last.then_inc(weights_ready, 1)
            dve.wait_ge(weights_ready, 1)
            if biased:
                dve.wait_ge(wT_done, 1)
                nc.vector.tensor_copy(w_blkT[:].rearrange("p (j t) -> p j t", t=TT), down_ps[1][0:n, :, 0:TT]).then_inc(wT_ready, 1)
                dve.wait_ge(bias_done, 1)
                nc.vector.tensor_tensor(acc[:], P.xn[:], down_ps[0][0:TT], ALU.add).then_inc(acc_ready, 1)
            else:
                nc.vector.memset(acc[:], 0.0).then_inc(acc_ready, 1)
            dve.wait_ge(acc_ready, 1)
            with dve.Fori(0, n // 2) as i:
                for s in range(2):
                    dve.wait_ge(act_ready[s], i + 1)
                    dve.wait_ge(up_done[s], i + 1)
                    dve.wait_ge(down_done[s], i + 1)
                    if biased:
                        nc.vector.scalar_tensor_tensor(hT[:, s, :], up_ps[s][0:F, 0:N_TOK], b_up[:, s],
                                                       act_g[:, s, :], ALU.add, ALU.mult).then_inc(h_ready[s], 1)
                    else:
                        nc.vector.tensor_tensor(hT[:, s, :], act_g[:, s, :], up_ps[s][0:F, 0:N_TOK], ALU.mult)\
                            .then_inc(h_ready[s], 1)
                for s in range(2):
                    dve.wait_ge(down_done[s], i + 2)
                    dve.wait_ge(acc_done[1 - s], i + s + 1)
                    for j in range(NT):
                        last = nc.vector.scalar_tensor_tensor(acc[:, j, :], down_ps[s][0:TT, j, :],
                                                              w_blk[:, j, bass.ds(2 * i + s, 1)],
                                                              acc[:, j, :], ALU.mult, ALU.add)
                    last.then_inc(acc_done[s], 1)
            dve.wait_ge(acc_done[1], n // 2 + 1)
            nc.vector.scalar_tensor_tensor(P.x[:], acc[:], P.gates[0:TT, 4 + k:5 + k], P.x[:], ALU.mult, ALU.add)


def load_wait(engine, sem, dmas):
    engine.wait_ge(sem, 16 * dmas)


def xattn0_stage(P):
    nc, dram = P.nc, P.dram
    HH = 8
    VW = 32
    NB = 4
    with Stage(nc, "xa0") as st:
        wq, wk, wv = (st.sb(n, [128, KT, D]) for n in ("wq", "wk", "wv"))
        wo = st.sb("wo", [128, NB, D])
        den_pick = st.sb("den_pick", [128, 128])
        bq, bk = st.sb("bq", [128, 2]), st.sb("bk", [128, 2])
        bv, bo, gamma, beta = (st.sb(n, [128, D]) for n in ("bv", "bo", "gamma", "beta"))
        mask_i = st.sb("mask_i", [KP, B * KN], I32)
        keep = st.sb("keep", [KP, B * KN])
        escale, ebias = ([st.sb(f"{n}{s}", [KP, KN]) for s in range(2)] for n in ("escale", "ebias"))
        qT = st.sb("qT", [128, 2, N_TOK])
        oT = st.sb("oT", [128, NB, N_TOK])
        ctxT = [st.sb(f"ctxT{s}", [128, KT, T]) for s in range(2)]
        kT = [st.sb(f"kT{s}", [128, 2, T]) for s in range(2)]
        v = [st.sb(f"v{s}", [KP, KN, H, VW]) for s in range(2)]
        qblk = [st.sb(f"qblk{s}", [128, 2, HH, S]) for s in range(2)]
        clipped, probs = ([st.sb(f"{n}{p}", [KP, 2, HH, S]) for p in range(2)] for n in ("clipped", "probs"))
        num, den, rden, unit = (st.sb(n, [128, NB * S]) for n in ("num", "den", "rden", "unit"))
        delta = st.sb("delta", [TT, NT, D])
        stats, mean_var = st.sb("stats", [TT, NT, 6]), st.sb("mean_var", [TT, NT, 2])
        var_eps, std, rstd = st.sb("var_eps", [TT, NT]), st.sb("std", [TT, NT]), st.sb("rstd", [TT, NT])
        loaded, ctx_loaded = st.sem("loaded"), st.sems("ctx_loaded", 2)

        def load_ctx(sp, b, s):
            sp.dma_start(ctxT[s][:], dram["ctxT"][bass.ds(b, 1)].rearrange("o (c p) t -> p (o c) t", p=128)).then_inc(ctx_loaded[s], 16)

        def early(sp):
            sp.dma_start(wk[:], dram["x0_wk"].rearrange("(c p) n -> p c n", p=128)).then_inc(loaded, 16)
            load_ctx(sp, 0, 0)
            for name, t in (("wq", wq), ("wv", wv)):
                sp.dma_start(t[:], dram[f"x0_{name}"].rearrange("(c p) n -> p c n", p=128)).then_inc(loaded, 16)
            for name, t in (("wo", wo), ("bq", bq), ("bk", bk), ("bv", bv), ("bo", bo), ("gamma", gamma), ("beta", beta)):
                sp.dma_start(t[:], dram[f"x0_{name}"]).then_inc(loaded, 16)
            sp.dma_start(den_pick[:], dram["den_pick"]).then_inc(loaded, 16)
            sp.dma_start(mask_i[:], dram["mask0"]).then_inc(loaded, 16)
            load_ctx(sp, 1, 1)
        norm_stage(P, 0, early)
        RING = 3
        proj_ps = [st.ps(f"proj{r}", [128, 512]) for r in range(RING)]
        score_ps = [st.ps(f"score{p}", [128, 2, 512]) for p in range(2)]
        out_ps = st.ps("out", [128, 512])
        q_done, q_ready = st.sem("q_done"), st.sem("q_ready")
        proj_done, proj_free = st.sems("proj_done", RING), st.sems("proj_free", RING)
        qblk_ready, scale_ready, v_fill = st.sem("qblk_ready"), st.sem("scale_ready"), st.sem("v_fill")
        score_done, clip_done = st.sems("score_done", 2), st.sems("clip_done", 2)
        exp_done, pv_done = st.sems("exp_done", 2), st.sems("pv_done", 2)
        num_done, den_done, out_read, taken = (st.sem(n) for n in ("num_done", "den_done", "out_read", "taken"))
        dve_step, o_done, var_ready, std_ready = (st.sem(n) for n in ("dve_step", "o_done", "var_ready", "std_ready"))
        st.start_at_one(proj_free, clip_done, exp_done, pv_done, out_read, taken)
        block = st.block()
        N_LOADS = 12
        UNITS = 12
        RU, PER = UNITS // RING, KN // 2

        def over_batches(engine, batch):
            with engine.Fori(0, B // 2 - 1) as i:
                for s in range(2):
                    batch(2 * i + s, s, 2)
            batch(B - 2, 0, 1)
            batch(B - 1, 1, 0)

        @block.sync
        def _(sp):
            with sp.Fori(0, B // 2 - 1) as i:
                for s in range(2):
                    sp.wait_ge(proj_done[RING - 1], RU * (2 * i + s) + RU)
                    load_ctx(sp, 2 * i + s + 2, s)

        @block.tensor
        def _(pe):
            def project(b, s, u):
                if u == 0:
                    pe.wait_ge(ctx_loaded[s], 8 * (b - s) + 16)
                pe.wait_ge(proj_free[u % RING], RU * b + u // RING + 1)
                if u < 6:
                    h, c3 = u // 3, u % 3
                    for c in range(KT):
                        last = nc.tensor.matmul(proj_ps[u % RING][:, 0:KC], wk[:, c, h * 128:(h + 1) * 128],
                                                ctxT[s][:, c, c3 * KC:(c3 + 1) * KC], start=(c == 0), stop=(c == KT - 1))
                else:
                    for k in range(2):
                        n = 2 * (u - 6) + k
                        for c in range(KT):
                            last = nc.tensor.matmul(proj_ps[u % RING][0:KP, k * D:(k + 1) * D], ctxT[s][:, c, n * KP:(n + 1) * KP],
                                                    wv[:, c, :], start=(c == 0), stop=(c == KT - 1))
                last.then_inc(proj_done[u % RING], 1)

            def scores(b, s, n):
                if n == 0:
                    pe.wait_ge(qblk_ready, b + 1)
                    for r in range(RING):
                        pe.wait_ge(proj_free[r], RU * b + RU + 1)
                pe.wait_ge(clip_done[n % 2], PER * b + n // 2 + 1)
                for h in range(2):
                    last = nc.tensor.matmul(score_ps[n % 2][0:KP, h, 0:HH * S], kT[s][:, h, n * KP:(n + 1) * KP],
                                            qblk[s][:, h].rearrange("p a q -> p (a q)"), start=True, stop=True)
                last.then_inc(score_done[n % 2], 1)

            def weigh(b, s, n):
                if n == 0:
                    pe.wait_ge(out_read, b + 1)
                pe.wait_ge(exp_done[n % 2], PER * b + n // 2 + 2)
                for head in range(H):
                    g, k = head % NB, head // NB
                    last = nc.tensor.matmul(out_ps[VW * g:VW * (g + 1), k * S:(k + 1) * S], v[s][:, n, head, :],
                                            probs[n % 2][:, head // HH, head % HH, :], start=(n == 0), stop=(n == KN - 1),
                                            skip_group_check=True)
                last.then_inc(pv_done[n % 2], 1)

            def batch(b, s, more):
                for n in range(KN):
                    if n + 2 < KN:
                        scores(b, s, n + 2)
                        if more:
                            project(b + 1, 1 - s, n + 2)
                    else:
                        if more:
                            scores(b + 1, 1 - s, n + 2 - KN)
                        if more == 2:
                            project(b + 2, s, n + 2 - KN)
                    weigh(b, s, n)
                pe.wait_ge(num_done, b + 1)
                nc.tensor.matmul(out_ps[:, 256:256 + NB * S], den_pick[:], num[:], start=True, stop=True, skip_group_check=True)\
                    .then_inc(den_done, 1)

            load_wait(pe, loaded, N_LOADS)
            for h in range(2):
                for c in range(KT):
                    last = nc.tensor.matmul(score_ps[h][:, 0, 0:N_TOK], wq[:, c, h * 128:(h + 1) * 128], P.xnT[:, c, :],
                                            start=(c == 0), stop=(c == KT - 1))
                last.then_inc(q_done, 1)
            for u in range(UNITS):
                project(0, 0, u)
            pe.wait_ge(q_ready, 2)
            pe.wait_ge(v_fill, 4)
            for n in range(2):
                scores(0, 0, n)
                project(1, 1, n)
            over_batches(pe, batch)
            pe.wait_ge(taken, B + 1)
            for j in range(NT):
                for k in range(NB):
                    last = nc.tensor.matmul(proj_ps[j // 2][0:TT, (j % 2) * D:(j % 2 + 1) * D], oT[:, k, j * TT:(j + 1) * TT],
                                            wo[:, k, :], start=(k == 0), stop=(k == NB - 1))
            last.then_inc(o_done, 1)

        @block.gpsimd
        def _(pool):
            fill = in_order(pool, v_fill)
            for s in range(2):
                fill(nc.gpsimd.memset(v[s][:, :, :, HD:VW], 0.0))
                fill(nc.gpsimd.memset(v[s][:, :, :, HD:HD + 1], 1.0))

            def block_queries(b, s):
                for h in range(2):
                    last = nc.gpsimd.tensor_tensor(qblk[s][:, h], qT[:, h, bass.ds(b * S, S)].unsqueeze(1).broadcast_to([128, HH, S]),
                                                   P.head_mask[:].unsqueeze(2).broadcast_to([128, HH, S]), ALU.mult)
                last.then_inc(qblk_ready, 1)

            def batch(b, s, more):
                if more:
                    pool.wait_ge(pv_done[1], PER * b + 1)
                    block_queries(b + 1, 1 - s)
            pool.wait_ge(q_ready, 2)
            block_queries(0, 0)
            over_batches(pool, batch)

        @block.scalar
        def _(act):
            def take_keys(b, s, u):
                h, c3 = u // 3, u % 3
                act.wait_ge(proj_done[u % RING], RU * b + u // RING + 1)
                nc.scalar.activation(kT[s][:, h, c3 * KC:(c3 + 1) * KC], proj_ps[u % RING][:, 0:KC], ACT.Identity,
                                     bias=bk[:, h:h + 1]).then_inc(proj_free[u % RING], 1)

            def exponential(b, s, n):
                if n == 0:
                    act.wait_ge(scale_ready, b + 1)
                act.wait_ge(clip_done[n % 2], PER * b + n // 2 + 2)
                act.wait_ge(pv_done[n % 2], PER * b + n // 2 + 1)
                nc.scalar.activation(probs[n % 2][:], clipped[n % 2][:], ACT.Exp, bias=ebias[s][:, n:n + 1],
                                     scale=escale[s][:, n:n + 1]).then_inc(exp_done[n % 2], 1)

            def batch(b, s, more):
                for n in range(KN):
                    exponential(b, s, n)
                    if more and n < 6:
                        take_keys(b + 1, 1 - s, n)

            load_wait(act, loaded, N_LOADS)
            for h in range(2):
                act.wait_ge(q_done, h + 1)
                nc.scalar.activation(qT[:, h, :], score_ps[h][:, 0, 0:N_TOK], ACT.Identity, bias=bq[:, h:h + 1]).then_inc(q_ready, 1)
            for u in range(6):
                take_keys(0, 0, u)
            over_batches(act, batch)
            act.wait_ge(var_ready, 1)
            nc.scalar.activation(std[:], var_eps[:], ACT.Sqrt).then_inc(std_ready, 1)

        @block.vector
        def _(dve):
            def scales(b, s):
                nc.vector.tensor_scalar(escale[s][:], keep[:, bass.ds(b * KN, KN)], 0.25, None, ALU.mult)
                nc.vector.tensor_scalar(ebias[s][:], keep[:, bass.ds(b * KN, KN)], -1.0, 50.0, ALU.add, ALU.mult).then_inc(scale_ready, 1)

            def take_values(b, s, u):
                dve.wait_ge(proj_done[u % RING], RU * b + u // RING + 1)
                n = 2 * (u - 6)
                for k in range(2):
                    last = nc.vector.tensor_tensor(v[s][:, n + k, :, 0:HD], proj_ps[u % RING][0:KP, k * D:(k + 1) * D].rearrange("p (h e) -> p h e", e=HD),
                                                   bv[0:KP, :].rearrange("p (h e) -> p h e", e=HD), ALU.add)
                last.then_inc(proj_free[u % RING], 1)

            def clip(b, n):
                dve.wait_ge(score_done[n % 2], PER * b + n // 2 + 1)
                dve.wait_ge(exp_done[n % 2], PER * b + n // 2 + 1)
                nc.vector.tensor_scalar(clipped[n % 2][:].rearrange("p h a q -> p h (a q)"), score_ps[n % 2][0:KP, :, 0:HH * S], -200.0, 200.0,
                                        ALU.max, ALU.min).then_inc(clip_done[n % 2], 1)

            def take_out(b):
                count = [0]

                def done(ins):
                    count[0] += 1
                    ins.then_inc(dve_step, 1)
                    dve.wait_ge(dve_step, 2 + 5 * b + count[0])
                dve.wait_ge(pv_done[1], PER * b + PER + 1)
                dve.wait_ge(taken, b + 1)
                nc.vector.tensor_scalar(num[:], out_ps[:, 0:NB * S], 1.0, None, ALU.mult).then_inc(num_done, 1)
                dve.wait_ge(den_done, b + 1)
                nc.vector.tensor_scalar(den[:], out_ps[:, 256:256 + NB * S], 1.0, None, ALU.mult).then_inc(out_read, 1)
                dve.wait_ge(out_read, b + 2)
                done(nc.vector.reciprocal(rden[:], den[:]))
                done(nc.vector.tensor_tensor(unit[:], den[:], rden[:], ALU.mult))
                done(nc.vector.tensor_scalar(unit[:], unit[:], 1e-8, None, ALU.add))
                done(nc.vector.reciprocal(unit[:], unit[:]))
                done(nc.vector.tensor_tensor(num[:], num[:], rden[:], ALU.mult))
                nc.vector.tensor_tensor(oT[:, :, bass.ds(b * S, S)], num[:].rearrange("p (k q) -> p k q", q=S),
                                        unit[:].rearrange("p (k q) -> p k q", q=S), ALU.mult).then_inc(taken, 1)

            def batch(b, s, more):
                for n in range(KN):
                    if n + 2 < KN:
                        clip(b, n + 2)
                    elif more:
                        clip(b + 1, n + 2 - KN)
                    if more and n == 1:
                        scales(b + 1, 1 - s)
                    if more and 3 <= n < UNITS - 3:
                        take_values(b + 1, 1 - s, n + 3)
                take_out(b)

            link = in_order(dve, dve_step)
            load_wait(dve, loaded, N_LOADS)
            link(nc.vector.tensor_copy(keep[:], mask_i[:]))
            link(nc.vector.tensor_scalar(keep[:], keep[:], 0.5, None, ALU.is_gt))
            scales(0, 0)
            for u in range(6, UNITS):
                take_values(0, 0, u)
            for n in range(2):
                clip(0, n)
            over_batches(dve, batch)
            link = in_order(dve, dve_step, 2 + 5 * B)
            dve.wait_ge(o_done, 1)
            for j in range(NT):
                link(nc.vector.tensor_tensor(delta[:, j, :], proj_ps[j // 2][0:TT, (j % 2) * D:(j % 2 + 1) * D], bo[0:TT, :], ALU.add))
            link(nc.vector.tensor_scalar(delta[:], delta[:], P.gates[0:TT, 8:9], None, ALU.mult))
            for j in range(NT):
                link(nc.vector.bn_stats(stats[:, j, :], delta[:, j, :]))
            for j in range(NT):
                link(nc.vector.bn_aggr(mean_var[:, j, :], stats[:, j, :]))
            nc.vector.tensor_scalar(var_eps[:], mean_var[:, :, 1], EPS_LN, None, ALU.add).then_inc(var_ready, 1)
            dve.wait_ge(std_ready, 1)
            link(nc.vector.reciprocal(rstd[:], std[:]))
            for j in range(NT):
                link(nc.vector.tensor_scalar(delta[:, j, :], delta[:, j, :], mean_var[:, j, 0:1], rstd[:, j:j + 1],
                                             ALU.subtract, ALU.mult))
            link(nc.vector.tensor_tensor(delta[:], delta[:], gamma[0:TT, :].unsqueeze(1).broadcast_to([TT, NT, D]), ALU.mult))
            link(nc.vector.tensor_tensor(delta[:], delta[:], beta[0:TT, :].unsqueeze(1).broadcast_to([TT, NT, D]), ALU.add))
            nc.vector.scalar_tensor_tensor(P.x[:], delta[:], P.gates[0:TT, 0:1], P.x[:], ALU.mult, ALU.add)


def xattn1_stage(P):
    nc, dram = P.nc, P.dram
    G, HG, GD = 4, 4, 64
    QG = HG * S
    QT = 2 * S
    NQ = G * HG // 2
    PARTS = 6
    K_PART, Q_PART = (0, 0, 0, 1, 1, 2), (0, 1, 2, 0, 1, 0)
    CROWS = PARTS * HD
    MROWS, NROWS = 3, 13
    KA, KB = CROWS + NROWS, CROWS + NROWS - 1
    MASKED = -2.0 ** 100
    VW = 32
    parts_k = nc.dram_tensor("x1_parts_k", (B, PARTS, GD, T), BF16).ap()
    parts_q = nc.dram_tensor("x1_parts_q", (PARTS, GD, B, QG), BF16).ap()
    mask_rows_dram = nc.dram_tensor("x1_mask_rows", (B, T), BF16).ap()
    with Stage(nc, "xa1") as st:
        wq = st.sb("wq", [128, KT, HG, GD])
        wkv = st.sb("wkv", [128, KT, 2 * GD])
        wo = st.sb("wo", [128, HG, D])
        den_pick = st.sb("den_pick", [128, 128])
        ident16 = st.sb("ident16", [128, 128], BF16)
        q32 = st.sb("q32", [GD, B, HG, S])
        q_parts = st.sb("q_parts", [GD, 3, B, HG, S], BF16)
        oT = st.sb("oT", [128, HG, N_TOK])
        keep_rows, mask_rows = st.sb("keep_rows", [B, T], U8), st.sb("mask_rows", [B, T], BF16)
        keep_cols, mask_cols = st.sb("keep_cols", [KP, B * KN], U8), st.sb("mask_cols", [KP, B * KN])
        low_q, low_k = st.sb("low_q", [128, G * QG]), st.sb("low_k", [128, T])
        ctxT = [st.sb(f"ctxT{s}", [128, KT, T]) for s in range(2)]
        vT = st.sb("vT", [128, T])
        k32, k_parts = st.sb("k32", [GD, T]), st.sb("k_parts", [GD, 3, T], BF16)
        kS = [st.sb(f"kS{s}", [KA, G, T], BF16) for s in range(2)]
        qA, qB = ([st.sb(f"{n}{s}", [KA, G, HG, S], BF16) for s in range(2)] for n in ("qA", "qB"))
        v = [st.sb(f"v{s}", [KP, KN, G, VW]) for s in range(2)]
        probs = [st.sb(f"probs{p}", [KP, G * QG]) for p in range(2)]
        mask_b = [st.sb(f"mask_b{s}", [KP, KN]) for s in range(2)]
        negmax_c = st.sb("negmax_c", [QT, NQ, 3])
        negmax, m_rest = st.sb("negmax", [QT, NQ]), st.sb("m_rest", [QT, NQ])
        m_parts = st.sb("m_parts", [QT, NQ, MROWS], BF16)
        num, rden = st.sb("num", [128, QG]), st.sb("rden", [128, QG])
        loaded, ctx_loaded = st.sem("loaded"), st.sems("ctx_loaded", 2)

        def load_ctx(sp, b, s):
            sp.dma_start(ctxT[s][:], dram["ctxT"][bass.ds(b, 1)].rearrange("o (c p) t -> p (o c) t", p=128)).then_inc(ctx_loaded[s], 16)

        def early(sp):
            load_ctx(sp, 0, 0)
            sp.dma_start(wkv[:, :, 0:GD], dram["x1_wk"].rearrange("(c p) n -> p c n", p=128)).then_inc(loaded, 16)
            sp.dma_start(wkv[:, :, GD:], dram["x1_wv"].rearrange("(c p) n -> p c n", p=128)).then_inc(loaded, 16)
            sp.dma_start(wq[:], dram["x1_wq"].rearrange("(c p) (a n) -> p c a n", p=128, a=HG)).then_inc(loaded, 16)
            sp.dma_start(keep_rows[:], dram["mask1"]).then_inc(loaded, 16)
            sp.dma_start(keep_cols[:], dram["mask1_cols"]).then_inc(loaded, 16)
            sp.dma_start(low_q[CROWS:KA, :], dram["x1_q_rows"]).then_inc(loaded, 16)
            sp.dma_start(low_k[CROWS:KA, :], dram["x1_k_rows"]).then_inc(loaded, 16)
            load_ctx(sp, 1, 1)
            sp.dma_start(den_pick[:], dram["den_pick"]).then_inc(loaded, 16)
            sp.dma_start(wo[:], dram["x1_wo"]).then_inc(loaded, 16)
        norm_stage(P, 2, early)
        RING = 3
        unit_ps = [st.ps(f"unit{r}", [128, 512]) for r in range(RING)]
        score_ps = [st.ps(f"score{p}", [128, 2, 512]) for p in range(2)]
        out_ps = st.ps("out", [128, 512])
        mT_ps = unit_ps[RING - 1][CROWS:CROWS + MROWS, :].bitcast(BF16)
        ready = st.sem("ready")
        q_done, q_taken, q_part_done, q_rest_done = (st.sem(n) for n in ("q_done", "q_taken", "q_part_done", "q_rest_done"))
        q_stored, mask_stored, k_stored, mask_done = (st.sem(n) for n in ("q_stored", "mask_stored", "k_stored", "mask_done"))
        qA_loaded, qB_loaded, kS_loaded = st.sems("qA_loaded", 2), st.sems("qB_loaded", 2), st.sems("kS_loaded", 2)
        unit_done, unit_read = st.sems("unit_done", RING), st.sems("unit_read", RING)
        part_done, rest_done = st.sems("part_done", 3), st.sems("rest_done", 2)
        split_done = st.sem("split_done")
        score_done, exp_done, pv_done = st.sems("score_done", 2), st.sems("exp_done", 2), st.sems("pv_done", 2)
        num_done, den_done, out_read, dve_step, taken, o_done, ready_v, low_ready = (
            st.sem(n) for n in ("num_done", "den_done", "out_read", "dve_step", "taken", "o_done", "ready_v", "low_ready"))
        st.start_at_one(exp_done, pv_done, out_read, k_stored, taken, part_done[2])
        block = st.block()
        N_LOADS = 9
        PER = KN // 2
        V0, K0, Q0, TURN, UNITS = 0, 2, 5, 29, 30
        FIRST_K0, FIRST_V0, FIRST_K1, FIRST_Q0, FIRST_TURN, FIRST_UNITS = 0, 3, 5, 8, 32, 33

        def nth(b, u, more=2):
            if b is None:
                return u % RING, u // RING + 1
            skipped = int(more == 1 and u >= Q0)
            return u % RING, b * (UNITS // RING) + (FIRST_UNITS // RING + u // RING + 1 - skipped)

        def over_batches(engine, batch):
            with engine.Fori(0, B // 2 - 1) as i:
                for s in range(2):
                    batch(2 * i + s, s, 2)
            batch(B - 2, 0, 1)
            batch(B - 1, 1, 0)

        def per_slot(b, s):
            return 8 * (b - s) + 16

        @block.sync
        def _(sp):
            def load_queries(to, done, b):
                for g in range(G):
                    sp.dma_start(to[0:CROWS, g].rearrange("p a q -> p (a q)"),
                                 parts_q[:, g * HD:(g + 1) * HD, bass.ds(b, 1), :].rearrange("r d o n -> r d (o n)")).then_inc(done, 16)

            def store_keys(b):
                for r in range(PARTS):
                    sp.wait_ge(part_done[K_PART[r]], b + 1 + (K_PART[r] == 2))
                    sp.dma_start(parts_k[bass.ds(b, 1), r].rearrange("o d t -> (o d) t"), k_parts[:, K_PART[r], :]).then_inc(k_stored, 16)

            def load_keys(b, s):
                sp.wait_ge(k_stored, 16 * PARTS * (b + 1) + 1)
                for g in range(G):
                    sp.dma_start(kS[s][0:CROWS, g, :], parts_k[bass.ds(b, 1), :, g * HD:(g + 1) * HD, :].rearrange("o r d t -> (o r) d t"))\
                        .then_inc(kS_loaded[s], 16)
                    sp.dma_start(kS[s][KB:KA, g, :], mask_rows_dram[bass.ds(b, 1), :]).then_inc(kS_loaded[s], 16)

            sp.wait_ge(mask_done, 1)
            sp.dma_start(mask_rows_dram, mask_rows[:]).then_inc(mask_stored, 16)
            for r in range(PARTS):
                sp.wait_ge(q_part_done, Q_PART[r] + 1)
                sp.dma_start(parts_q[r], q_parts[:, Q_PART[r]].rearrange("p b a q -> p b (a q)")).then_inc(q_stored, 16)
            store_keys(0)
            sp.wait_ge(mask_stored, 16)
            sp.wait_ge(low_ready, 2 * (G + 2))
            load_keys(0, 0)
            sp.wait_ge(q_stored, 16 * PARTS)
            load_queries(qA[0], qA_loaded[0], 0)
            load_queries(qB[0], qB_loaded[0], 0)
            store_keys(1)
            load_keys(1, 1)
            load_queries(qA[1], qA_loaded[1], 1)
            load_queries(qB[1], qB_loaded[1], 1)
            r, count = nth(None, FIRST_V0 + 1)
            sp.wait_ge(unit_done[r], count)
            load_ctx(sp, 2, 0)

            def batch(b, s, more):
                if more == 2:
                    if more_ctx:
                        r, count = nth(b, V0 + 1)
                        sp.wait_ge(unit_done[r], count)
                        load_ctx(sp, b + 3, 1 - s)
                    store_keys(b + 2)
                    load_queries(qA[s], qA_loaded[s], b + 2)
                    sp.wait_ge(pv_done[1], PER * b + PER + 1)
                    load_keys(b + 2, s)
                    load_queries(qB[s], qB_loaded[s], b + 2)
            more_ctx = True
            with sp.Fori(0, B // 2 - 2) as i:
                for s in range(2):
                    batch(2 * i + s, s, 2)
            batch(B - 4, 0, 2)
            more_ctx = False
            batch(B - 3, 1, 2)

        @block.tensor
        def _(pe):
            def begin(r, count):
                if not isinstance(count, int) or count > 1:
                    pe.wait_ge(unit_read[r], count - 1)

            def project(r, count, b, s, c3):
                begin(r, count)
                if c3 == 0:
                    pe.wait_ge(ctx_loaded[s], per_slot(b, s))
                for c in range(KT):
                    last = nc.tensor.matmul(unit_ps[r][:, 0:KC], wkv[:, c, :], ctxT[s][:, c, c3 * KC:(c3 + 1) * KC],
                                            start=(c == 0), stop=(c == KT - 1))
                last.then_inc(unit_done[r], 1)

            def turn_values(r, half):
                for n in range(6):
                    t0 = (half * 6 + n) * KP
                    last = nc.tensor.transpose(unit_ps[r][0:KP, n * GD:(n + 1) * GD], vT[GD:, t0:t0 + KP], P.ident[GD:, GD:])
                last.then_inc(unit_done[r], 1)

            def first(r, count, b, s, t, c):
                begin(r, count)
                if t == 0 and c == 0:
                    pe.wait_ge(qA_loaded[s], G * per_slot(b, s))
                    pe.wait_ge(kS_loaded[s], 2 * G * per_slot(b, s))
                nc.tensor.matmul(unit_ps[r][0:QT, 0:KC], qA[s][:, t // 2, (t % 2) * 2:(t % 2 + 1) * 2, :].rearrange("p a q -> p (a q)"),
                                 kS[s][:, t // 2, c * KC:(c + 1) * KC], start=True, stop=True).then_inc(unit_done[r], 1)

            def turn(r, count, b):
                begin(r, count)
                pe.wait_ge(split_done, b + 1)
                for t in range(NQ):
                    last = nc.tensor.transpose(mT_ps[:, t * QT:(t + 1) * QT], m_parts[:, t, :], ident16[0:QT, 0:QT])
                last.then_inc(unit_done[r], 1)

            def unit(b, s, more, u):
                r, count = nth(b, u, more)
                if u < K0:
                    turn_values(r, u - V0)
                elif u < Q0:
                    if more == 2:
                        project(r, count, b + 2, s, u - K0)
                elif u < TURN:
                    first(r, count, b + 1, 1 - s, (u - Q0) // 3, (u - Q0) % 3)
                else:
                    turn(r, count, b + 1)

            def second(b, s, n, keys_came=True):
                if n == 0:
                    bank, use = nth(b, TURN)
                    pe.wait_ge(unit_read[bank], use - UNITS // RING - (not keys_came))
                    pe.wait_ge(qB_loaded[s], G * per_slot(b, s))
                pe.wait_ge(exp_done[n % 2], PER * b + n // 2 + 1)
                for g in range(G):
                    last = nc.tensor.matmul(score_ps[n % 2][0:KP, g // 2, (g % 2) * QG:(g % 2 + 1) * QG], kS[s][0:KB, g, n * KP:(n + 1) * KP],
                                            qB[s][0:KB, g].rearrange("p a q -> p (a q)"), start=True, stop=True)
                last.then_inc(score_done[n % 2], 1)

            def weigh(b, s, n):
                if n == 0:
                    for half in range(2):
                        bank, use = nth(b, V0 + half)
                        pe.wait_ge(unit_read[bank], use - UNITS // RING)
                    pe.wait_ge(out_read, b + 1)
                pe.wait_ge(exp_done[n % 2], PER * b + n // 2 + 2)
                for g in range(G):
                    last = nc.tensor.matmul(out_ps[VW * g:VW * (g + 1), 0:QG], v[s][:, n, g, :], probs[n % 2][:, g * QG:(g + 1) * QG],
                                            start=(n == 0), stop=(n == KN - 1), skip_group_check=True)
                last.then_inc(pv_done[n % 2], 1)

            def may_turn(b):
                for c3 in range(3):
                    bank, use = nth(b, K0 + c3)
                    pe.wait_ge(unit_read[bank], use - UNITS // RING)
                for half in range(2):
                    begin(*nth(b, V0 + half))

            def batch(b, s, more):
                if more:
                    may_turn(b)
                for n in range(KN):
                    if n + 1 < KN:
                        second(b, s, n + 1)
                    elif more:
                        second(b + 1, 1 - s, 0, keys_came=more == 2)
                    if more:
                        for u in range(3 * n, min(3 * n + 3, TURN)):
                            unit(b, s, more, u)
                        if n == KN - 2:
                            unit(b, s, more, TURN)
                    weigh(b, s, n)
                pe.wait_ge(num_done, b + 1)
                nc.tensor.matmul(out_ps[:, 256:256 + QG], den_pick[:], num[:], start=True, stop=True, skip_group_check=True)\
                    .then_inc(den_done, 1)

            pe.wait_ge(loaded, 16 * N_LOADS)
            for a in range(HG):
                if a >= 2:
                    pe.wait_ge(q_taken, a - 1)
                for c in range(KT):
                    last = nc.tensor.matmul(score_ps[a % 2][0:GD, 0, 0:N_TOK], wq[:, c, a, :], P.xnT[:, c, :],
                                            start=(c == 0), stop=(c == KT - 1))
                last.then_inc(q_done, 1)
            for c3 in range(3):
                project(*nth(None, FIRST_K0 + c3), 0, 0, c3)
            for c3 in range(3):
                bank, use = nth(None, FIRST_K0 + c3)
                pe.wait_ge(unit_read[bank], use)
            for half in range(2):
                begin(*nth(None, FIRST_V0 + half))
                turn_values(nth(None, FIRST_V0 + half)[0], half)
            for c3 in range(3):
                project(*nth(None, FIRST_K1 + c3), 1, 1, c3)
            pe.wait_ge(q_taken, HG)
            pe.wait_ge(ready, 1)
            for k in range(3 * NQ):
                first(*nth(None, FIRST_Q0 + k), 0, 0, k // 3, k % 3)
            turn(*nth(None, FIRST_TURN), 0)
            second(0, 0, 0)
            over_batches(pe, batch)
            pe.wait_ge(taken, B + 1)
            for j in range(NT):
                for a in range(HG):
                    last = nc.tensor.matmul(score_ps[j // 2][0:TT, 0, (j % 2) * D:(j % 2 + 1) * D], oT[:, a, j * TT:(j + 1) * TT],
                                            wo[:, a, :], start=(a == 0), stop=(a == HG - 1))
            last.then_inc(o_done, 1)

        @block.gpsimd
        def _(pool):
            for s in range(2):
                nc.gpsimd.memset(v[s][:], 0.0).then_inc(ready_v, 1)
            pool.wait_ge(ready_v, 2)
            for s in range(2):
                nc.gpsimd.memset(v[s][:, :, :, HD:HD + 1], 1.0).then_inc(ready_v, 1)

            def rest(b, x):
                pool.wait_ge(part_done[x], b + 1)
                nc.gpsimd.tensor_tensor(k32[:], k32[:], k_parts[:, x, :], ALU.subtract).then_inc(rest_done[x], 1)

            def batch(b, s, more):
                if more == 2:
                    for x in range(2):
                        rest(b + 2, x)
            for b in range(2):
                for x in range(2):
                    rest(b, x)
            over_batches(pool, batch)

        @block.scalar
        def _(act):
            def take_keys(at, b):
                for c3, (r, count) in enumerate(at):
                    act.wait_ge(unit_done[r], count)
                    if c3 == 0:
                        act.wait_ge(part_done[2], b + 1)
                    nc.scalar.activation(k32[:, c3 * KC:(c3 + 1) * KC], unit_ps[r][0:GD, 0:KC], ACT.Copy)
                    nc.scalar.activation(vT[GD:, c3 * KC:(c3 + 1) * KC], unit_ps[r][GD:, 0:KC], ACT.Copy).then_inc(unit_read[r], 1)
                for r, count in at:
                    act.wait_ge(unit_read[r], count)
                key_part(b, 0)

            def key_part(b, x):
                if x:
                    act.wait_ge(rest_done[x - 1], b + 1)
                act.wait_ge(k_stored, 16 * PARTS * b + 1)
                nc.scalar.activation(k_parts[:, x, :], k32[:], ACT.Copy).then_inc(part_done[x], 1)

            def take_values(at, s):
                for half, (r, count) in enumerate(at):
                    act.wait_ge(unit_done[r], count)
                    nc.scalar.activation(v[s][:, half * 6:(half + 1) * 6, :, 0:HD],
                                         unit_ps[r][0:KP, 0:6 * GD].rearrange("p (n g d) -> p n g d", g=G, d=HD), ACT.Copy)\
                        .then_inc(unit_read[r], 1)

            def rows(r, count, b, s):
                act.wait_ge(unit_done[r], count)
                act.wait_ge(qB_loaded[s], G * per_slot(b, s))
                nc.scalar.activation(qB[s][CROWS:CROWS + MROWS].rearrange("p g a q -> p (g a q)"), mT_ps[:, 0:G * QG], ACT.Copy)\
                    .then_inc(unit_read[r], 1)

            def exponential(b, s, n):
                act.wait_ge(score_done[n % 2], PER * b + n // 2 + 1)
                act.wait_ge(pv_done[n % 2], PER * b + n // 2 + 1)
                nc.scalar.activation(probs[n % 2][:].rearrange("p (c n) -> p c n", c=2), score_ps[n % 2][0:KP, :, 0:2 * QG], ACT.Exp,
                                     bias=mask_b[s][:, n:n + 1]).then_inc(exp_done[n % 2], 1)

            def batch(b, s, more):
                for n in range(KN):
                    exponential(b, s, n)
                    if n == 0 and more:
                        take_values([nth(b, V0 + half) for half in range(2)], 1 - s)
                    elif n == 1 and more == 2:
                        take_keys([nth(b, K0 + c3) for c3 in range(3)], b + 2)
                    elif n == 4 and more == 2:
                        key_part(b + 2, 1)
                    elif n == 7 and more == 2:
                        key_part(b + 2, 2)
                    if n == KN - 2 and more:
                        rows(*nth(b, TURN, more), b + 1, 1 - s)

            for a in range(HG):
                act.wait_ge(q_done, a + 1)
                nc.scalar.activation(q32[:, :, a, :], score_ps[a % 2][0:GD, 0, 0:N_TOK].rearrange("p (b q) -> p b q", q=S), ACT.Copy,
                                     scale=0.25).then_inc(q_taken, 1)
            take_keys([nth(None, FIRST_K0 + c3) for c3 in range(3)], 0)
            act.wait_ge(ready_v, 4)
            take_values([nth(None, FIRST_V0 + half) for half in range(2)], 0)
            key_part(0, 1)
            key_part(0, 2)
            take_keys([nth(None, FIRST_K1 + c3) for c3 in range(3)], 1)
            key_part(1, 1)
            key_part(1, 2)
            rows(*nth(None, FIRST_TURN), 0, 0)
            over_batches(act, batch)

        @block.vector
        def _(dve):
            def first_max(r, count, t, c):
                dve.wait_ge(unit_done[r], count)
                nc.vector.tensor_reduce(negmax_c[:, t, c:c + 1], unit_ps[r][0:QT, 0:KC], X_AXIS, ALU.max, negate=True).then_inc(unit_read[r], 1)

            def split(at, b, s):
                for r, count in at:
                    dve.wait_ge(unit_read[r], count)
                nc.vector.tensor_scalar(mask_b[s][:], mask_cols[:, bass.ds(b * KN, KN)], 1.0, None, ALU.mult)
                count = [0]

                def done(ins):
                    count[0] += 1
                    ins.then_inc(dve_step, 1)
                    dve.wait_ge(dve_step, 5 * b + count[0])
                done(nc.vector.tensor_reduce(negmax[:], negmax_c[:], X_AXIS, ALU.min))
                done(nc.vector.tensor_copy(m_parts[:, :, 0], negmax[:]))
                done(nc.vector.tensor_tensor(m_rest[:], negmax[:], m_parts[:, :, 0], ALU.subtract))
                done(nc.vector.tensor_copy(m_parts[:, :, 1], m_rest[:]))
                done(nc.vector.tensor_tensor(m_rest[:], m_rest[:], m_parts[:, :, 1], ALU.subtract))
                nc.vector.tensor_copy(m_parts[:, :, 2], m_rest[:]).then_inc(split_done, 1)

            def take_out(b):
                dve.wait_ge(pv_done[1], PER * b + PER + 1)
                dve.wait_ge(taken, b + 1)
                nc.vector.tensor_scalar(num[:], out_ps[:, 0:QG], 1.0, None, ALU.mult).then_inc(num_done, 1)
                dve.wait_ge(den_done, b + 1)
                nc.vector.reciprocal(rden[:], out_ps[:, 256:256 + QG]).then_inc(out_read, 1)
                dve.wait_ge(out_read, b + 2)
                nc.vector.tensor_tensor(oT[:, :, bass.ds(b * S, S)], num[:].rearrange("p (a q) -> p a q", a=HG),
                                        rden[:].rearrange("p (a q) -> p a q", a=HG), ALU.mult).then_inc(taken, 1)

            def batch(b, s, more):
                if more:
                    for k in range(3 * NQ):
                        first_max(*nth(b, Q0 + k, more), k // 3, k % 3)
                    split([nth(b, u, more) for u in range(TURN - 3, TURN)], b + 1, 1 - s)
                take_out(b)

            dve.wait_ge(loaded, 16 * N_LOADS)
            nc.vector.tensor_scalar(mask_rows[:], keep_rows[:], -MASKED, MASKED, ALU.mult, ALU.add).then_inc(mask_done, 1)
            nc.vector.tensor_scalar(mask_cols[:], keep_cols[:], -MASKED, MASKED, ALU.mult, ALU.add)
            nc.vector.tensor_copy(ident16[:], P.ident[:])
            for s in range(2):
                for g in range(G):
                    nc.vector.tensor_copy(kS[s][CROWS:KA, g, :], low_k[CROWS:KA, :]).then_inc(low_ready, 1)
                for t in (qA[s], qB[s]):
                    nc.vector.tensor_copy(t[CROWS:KA].rearrange("p g a q -> p (g a q)"), low_q[CROWS:KA, :]).then_inc(low_ready, 1)
            dve.wait_ge(q_taken, HG)
            for x in range(3):
                nc.vector.tensor_copy(q_parts[:, x], q32[:]).then_inc(q_part_done, 1)
                dve.wait_ge(q_part_done, x + 1)
                if x < 2:
                    nc.vector.tensor_tensor(q32[:], q32[:], q_parts[:, x], ALU.subtract).then_inc(q_rest_done, 1)
                    dve.wait_ge(q_rest_done, x + 1)
            nc.vector.memset(m_rest[:], 0.0).then_inc(ready, 1)
            for k in range(3 * NQ):
                first_max(*nth(None, FIRST_Q0 + k), k // 3, k % 3)
            split([nth(None, u) for u in range(FIRST_TURN - 3, FIRST_TURN)], 0, 0)
            over_batches(dve, batch)
            dve.wait_ge(o_done, 1)
            for j in range(NT):
                nc.vector.scalar_tensor_tensor(P.x[:, j, :], score_ps[j // 2][0:TT, 0, (j % 2) * D:(j % 2 + 1) * D],
                                               P.gates[0:TT, 1:2], P.x[:, j, :], ALU.mult, ALU.add)


def xattn2_stage(P):
    nc, dram = P.nc, P.dram
    with Stage(nc, "xa2") as st:
        wq, wg, wo = (st.sb(n, [128, KT, D]) for n in ("wq", "wg", "wo"))
        wkv = st.sb("wkv", [128, KT, 2 * D])
        bg = st.sb("bg", [128, 2])
        block_mask = st.sb("block_mask", [128, 128])
        fq, lq, eq = (st.sb(n, [128, 2, N_TOK]) for n in ("fq", "lq", "eq"))
        gateT, oT = st.sb("gateT", [128, 2, N_TOK]), st.sb("oT", [128, 2, N_TOK])
        ctxT = [st.sb(f"ctxT{s}", [128, KT, T]) for s in range(2)]
        RING = 3
        pos, low, ek, fk = ([st.sb(f"{n}{r}", [KP, D]) for r in range(RING)] for n in ("pos", "low", "ek", "fk"))
        vx = [st.sb(f"vx{r}", [KP, 2, 129]) for r in range(RING)]
        summary, ksum_blk = st.sb("summary", [128, 2, 128]), st.sb("ksum_blk", [128, 2, 128])
        rden = st.sb("rden", [128, 2, S])
        loaded, ctx_loaded = st.sem("loaded"), st.sems("ctx_loaded", 2)

        def load_ctx(sp, b, s):
            sp.dma_start(ctxT[s][:], dram["ctxT"][bass.ds(b, 1)].rearrange("o (c p) t -> p (o c) t", p=128)).then_inc(ctx_loaded[s], 16)

        def early(sp):
            for name, t in (("wq", wq), ("wg", wg), ("wkv", wkv), ("wo", wo)):
                sp.dma_start(t[:], dram[f"x2_{name}"].rearrange("(c p) n -> p c n", p=128)).then_inc(loaded, 16)
            sp.dma_start(bg[:], dram["x2_bg"]).then_inc(loaded, 16)
            sp.dma_start(block_mask[:], dram["block_mask"]).then_inc(loaded, 16)
            for s in range(2):
                load_ctx(sp, s, s)
        norm_stage(P, 4, early)
        kv_ps = [st.ps(f"kv{r}", [128, 512]) for r in range(RING)]
        sum_ps = [st.ps(f"sum{h}", [128, 512]) for h in range(2)]
        out_ps = st.ps("out", [128, 512])
        q_ps = [st.ps(f"q{h}", [128, 512]) for h in range(2)]
        q_done, q_low, q_exp, gate_done, gate_ready = (st.sem("q_done"), st.sem("q_low"), st.sem("q_exp"),
                                                       st.sem("gate_done"), st.sem("gate_ready"))
        kv_done, low_done, relu_done, exp_done = (st.sems(n, RING) for n in ("kv_done", "low_done", "relu_done", "exp_done"))
        fk_done, used = st.sems("fk_done", RING), st.sems("used", RING)
        v_done = st.sems("v_done", RING)
        sum_done, sum_read, out_done, out_read = st.sems("sum_done", 2), st.sem("sum_read"), st.sem("out_done"), st.sem("out_read")
        dve_step, o_done, dve_q = st.sem("dve_step"), st.sem("o_done"), st.sem("dve_q")
        st.start_at_one(sum_done, sum_read, v_done, relu_done, low_done, out_read, fk_done, exp_done, out_done)
        block = st.block()
        N_LOADS = 6
        RU = KN // RING

        @block.sync
        def _(sp):
            with sp.Fori(0, B // 2 - 1) as i:
                for s in range(2):
                    sp.wait_ge(sum_done[s], i + 2)
                    load_ctx(sp, 2 * i + 2 + s, s)

        @block.tensor
        def _(pe):
            load_wait(pe, loaded, N_LOADS)
            for w, done in ((wq, q_done), (wg, gate_done)):
                for h in range(2):
                    if w is wg:
                        pe.wait_ge(q_low, 2 * h + 2)
                    for c in range(KT):
                        last = nc.tensor.matmul(q_ps[h][:, 0:N_TOK], w[:, c, h * 128:(h + 1) * 128], P.xnT[:, c, :],
                                                start=(c == 0), stop=(c == KT - 1))
                    last.then_inc(done, 1)
            with pe.Fori(0, B // 2) as i:
                for s in range(2):
                    b = 2 * i + s
                    pe.wait_ge(ctx_loaded[s], 16 * i + 16)

                    def summarise(n):
                        r = n % RING
                        pe.wait_ge(fk_done[r], RU * b + n // RING + 2)
                        pe.wait_ge(v_done[r], RU * b + n // RING + 2)
                        if n == 0:
                            pe.wait_ge(sum_read, b + 1)
                        for h in range(2):
                            last = nc.tensor.matmul(sum_ps[h][:, 0:129], fk[r][:, h * 128:(h + 1) * 128], vx[r][:, h, :],
                                                    start=(n == 0), stop=(n == KN - 1))
                        last.then_inc(used[r] if n < KN - 1 else sum_done[s], 1)

                    for n in range(KN):
                        r = n % RING
                        pe.wait_ge(v_done[r], RU * b + n // RING + 1)
                        pe.wait_ge(relu_done[r], RU * b + n // RING + 1)
                        pe.wait_ge(low_done[r], RU * b + n // RING + 1)
                        for c in range(KT):
                            last = nc.tensor.matmul(kv_ps[r][0:KP, :], ctxT[s][:, c, n * KP:(n + 1) * KP], wkv[:, c, :],
                                                    start=(c == 0), stop=(c == KT - 1))
                        last.then_inc(kv_done[r], 1)
                        if n >= 2:
                            summarise(n - 2)
                    summarise(KN - 2)
                    summarise(KN - 1)
                    pe.wait_ge(sum_read, b + 2)
                    pe.wait_ge(out_read, b + 1)
                    pe.wait_ge(dve_q, 2)
                    for h in range(2):
                        for w, at in ((summary, 0), (ksum_blk, 1)):
                            last = nc.tensor.matmul(out_ps[:, (2 * h + at) * S:(2 * h + at + 1) * S], w[:, h, :],
                                                    fq[:, h, bass.ds(b * S, S)], start=True, stop=True)
                    last.then_inc(out_done, 1)
            pe.wait_ge(out_read, B + 1)
            for j in range(NT):
                for h in range(2):
                    last = nc.tensor.matmul(q_ps[j // 2][0:TT, (j % 2) * D:(j % 2 + 1) * D], oT[:, h, j * TT:(j + 1) * TT],
                                            wo[:, h, :], start=(h == 0), stop=(h == 1))
            last.then_inc(o_done, 1)

        @block.scalar
        def _(act):
            load_wait(act, loaded, N_LOADS)
            for h in range(2):
                act.wait_ge(q_low, 2 * h + 1)
                nc.scalar.activation(eq[:, h, :], lq[:, h, :], ACT.Exp).then_inc(q_exp, 1)
            for h in range(2):
                act.wait_ge(gate_done, h + 1)
                nc.scalar.activation(gateT[:, h, :], q_ps[h][:, 0:N_TOK], ACT.Sigmoid, bias=bg[:, h:h + 1]).then_inc(gate_ready, 1)
            with act.Fori(0, B // 2) as i:
                for s in range(2):
                    b = 2 * i + s
                    for n in range(KN):
                        r = n % RING
                        act.wait_ge(fk_done[r], RU * b + n // RING + 1)
                        act.wait_ge(v_done[r], RU * b + n // RING + 2)
                        nc.scalar.activation(pos[r][:], kv_ps[r][0:KP, 0:D], ACT.Relu).then_inc(relu_done[r], 1)
                        act.wait_ge(low_done[r], RU * b + n // RING + 2)
                        nc.scalar.activation(ek[r][:], low[r][:], ACT.Exp).then_inc(exp_done[r], 1)

        @block.vector
        def _(dve):
            for r in range(RING):
                nc.vector.memset(vx[r][:, :, 128:129], 1.0)
            for h in range(2):
                dve.wait_ge(q_done, h + 1)
                nc.vector.tensor_scalar(lq[:, h, :], q_ps[h][:, 0:N_TOK], 0.0, None, ALU.min).then_inc(q_low, 1)
                nc.vector.tensor_scalar(fq[:, h, :], q_ps[h][:, 0:N_TOK], 0.0, None, ALU.max).then_inc(q_low, 1)
            for h in range(2):
                dve.wait_ge(q_exp, h + 1)
                dve.wait_ge(q_low, 4)
                nc.vector.tensor_tensor(fq[:, h, :], fq[:, h, :], eq[:, h, :], ALU.add).then_inc(dve_q, 1)
            dve.wait_ge(loaded, 16 * N_LOADS)
            with dve.Fori(0, B // 2) as i:
                for s in range(2):
                    b = 2 * i + s
                    for n in range(KN):
                        r = n % RING
                        dve.wait_ge(kv_done[r], RU * b + n // RING + 1)
                        dve.wait_ge(exp_done[r], RU * b + n // RING + 1)
                        nc.vector.tensor_scalar(low[r][:], kv_ps[r][0:KP, 0:D], 0.0, None, ALU.min).then_inc(low_done[r], 1)
                        if n < RING:
                            dve.wait_ge(sum_done[1 - s], i + s + 1)
                        else:
                            dve.wait_ge(used[r], (RU - (r == RING - 1)) * b + n // RING)
                        nc.vector.tensor_copy(vx[r][:, :, 0:128], kv_ps[r][0:KP, D:2 * D].rearrange("p (h d) -> p h d", h=2))\
                            .then_inc(v_done[r], 1)
                        dve.wait_ge(relu_done[r], RU * b + n // RING + 2)
                        dve.wait_ge(exp_done[r], RU * b + n // RING + 2)
                        nc.vector.tensor_tensor(fk[r][:], pos[r][:], ek[r][:], ALU.add).then_inc(fk_done[r], 1)
                    dve.wait_ge(sum_done[s], i + 2)
                    dve.wait_ge(out_done, b + 1)
                    for h in range(2):
                        nc.vector.tensor_tensor(summary[:, h, :], sum_ps[h][:, 0:128], block_mask[:], ALU.mult)
                        last = nc.vector.tensor_scalar(ksum_blk[:, h, :], block_mask[:], sum_ps[h][:, 128:129], None, ALU.mult)
                    last.then_inc(sum_read, 1)
                    dve.wait_ge(out_done, b + 2)
                    view = out_ps[:, 0:4 * S].rearrange("p (h w q) -> p h w q", h=2, w=2)
                    nc.vector.tensor_scalar(rden[:], view[:, :, 1, :], 1e-6, None, ALU.add).then_inc(dve_step, 1)
                    dve.wait_ge(dve_step, 3 * b + 1)
                    nc.vector.reciprocal(rden[:], rden[:]).then_inc(dve_step, 1)
                    dve.wait_ge(dve_step, 3 * b + 2)
                    nc.vector.tensor_tensor(rden[:], view[:, :, 0, :], rden[:], ALU.mult).then_inc(dve_step, 1)
                    dve.wait_ge(dve_step, 3 * b + 3)
                    dve.wait_ge(gate_ready, 2)
                    nc.vector.tensor_tensor(oT[:, :, bass.ds(b * S, S)], rden[:], gateT[:, :, bass.ds(b * S, S)], ALU.mult)\
                        .then_inc(out_read, 1)
            dve.wait_ge(o_done, 1)
            for j in range(NT):
                nc.vector.scalar_tensor_tensor(P.x[:, j, :], q_ps[j // 2][0:TT, (j % 2) * D:(j % 2 + 1) * D],
                                               P.gates[0:TT, 2:3], P.x[:, j, :], ALU.mult, ALU.add)


ROUND = 12582912.0


def xattn3_stage(P):
    nc = P.nc
    P.kT_dram = nc.dram_tensor("k_parts", (3, D, B, T), BF16).ap()
    P.qT_dram = nc.dram_tensor("q_parts", (3, D, N_TOK), BF16).ap()
    with Stage(nc, "xa3") as keep:
        values = keep.sb("values", [128, B * KN * D])
        P.v32 = values[0:KP].rearrange("p (n d) -> p n d", d=D)
        halves = values[0:KP].bitcast(BF16).rearrange("p (a n) -> p a n", a=4)
        P.v8 = values[0:KP].bitcast(BF16)[:, 0:B * KN * D].rearrange("p (n d) -> p n d", d=D)
        P.vpad = [halves[:, 2 + s, :].rearrange("p (n d) -> p n d", d=128) for s in range(2)]
        P.v_scale = keep.sb("v_scale", [128, 2])
        P.oT = keep.sb("oT", [128, 2, N_TOK])
        P.rden = keep.sb("rden", [TT, NT, H])
        xattn3_keys(P)
        xattn3_queries(P)
        xattn3_attend(P)
        xattn3_out(P)


def xattn3_keys(P):
    nc, dram = P.nc, P.dram
    KE = KP + 1
    with Stage(nc, "xa3k") as st:
        wkv, bkv = st.sb("wkv", [128, KT, 2 * D]), st.sb("bkv", [128, 2 * D])
        ident16 = st.sb("ident16", [128, 128], BF16)
        ctxT = [st.sb(f"ctxT{s}", [128, KT, T]) for s in range(2)]
        kb = [st.sb(f"kb{s}", [KP, KN, D]) for s in range(2)]
        ints = st.sb("ints", [KP, KN, D])
        vmax, row = st.sb("vmax", [KP, D]), st.sb("row", [KP, D])
        vinv = st.sb("vinv", [128, 2])
        vdiag = bkv[:, 0:D].rearrange("p (h n) -> p h n", h=2)
        scale, inv = ([st.sb(f"{n}{s}", [KP, KN, H]) for s in range(2)] for n in ("scale", "inv"))
        part = [st.sb(f"part{x}", [KP, KN, D], BF16) for x in range(3)]
        turned = [st.sb(f"turned{h}", [128, T], BF16) for h in range(2)]
        loaded, ctx_loaded = st.sem("loaded"), st.sems("ctx_loaded", 2)

        def load_ctx(sp, b, s):
            sp.dma_start(ctxT[s][:], dram["ctxT"][bass.ds(b, 1)].rearrange("o (c p) t -> p (o c) t", p=128)).then_inc(ctx_loaded[s], 16)

        def early(sp):
            sp.dma_start(wkv[:], dram["x3_wkv"].rearrange("(c p) n -> p c n", p=128)).then_inc(loaded, 16)
            sp.dma_start(bkv[:], dram["x3_bkv"]).then_inc(loaded, 16)
            for s in range(2):
                load_ctx(sp, s, s)
        norm_stage(P, 6, early)
        RING = 3
        RU = KN // RING
        kv_ps = [st.ps(f"kv{r}", [128, 512]) for r in range(RING)]
        turn_ps = [st.ps(f"turn{h}", [128, 2, 1024], BF16) for h in range(2)]
        vscale_ps = st.ps("vscale", [128, 512])
        vt_done, diag_done, row_done = (st.sem(n) for n in ("vt_done", "diag_done", "row_done"))
        ident_ready = st.sem("ident_ready")
        kv_done, kv_read = st.sems("kv_done", RING), st.sems("kv_read", RING)
        dve_step, ints_ready, khat_done = st.sem("dve_step"), st.sem("ints_ready"), st.sem("khat_done")
        part_done, rest_done = st.sems("part_done", 3), st.sems("rest_done", 2)
        turn_done, copied, stored = st.sems("turn_done", 2), st.sems("copied", 2), st.sems("stored", 2)
        st.start_at_one(kv_read, copied, part_done[2], stored)
        block = st.block()
        LARGEST_DONE = 1 + 6 * B

        def by_head(t):
            return t.rearrange("p n (h e) -> p (n h) e", e=HD)

        def wide(t):
            return t.rearrange("p n h -> p (n h)").unsqueeze(2).broadcast_to([KP, KN * H, HD])

        def steps(engine, batch):
            with engine.Fori(0, B // 2 - 1) as i:
                for s in range(2):
                    batch(2 * i + s, s, 2)
            batch(B - 2, 0, 1)
            batch(B - 1, 1, 0)

        @block.sync
        def _(sp):
            def store(b):
                for x in range(3):
                    for h in range(2):
                        sp.wait_ge(copied[h], 3 * b + x + 2)
                        sp.dma_start(P.kT_dram[x, h * 128:(h + 1) * 128, bass.ds(b, 1), :].rearrange("p o t -> p (o t)"), turned[h][:])\
                            .then_inc(stored[h], 16)
            with sp.Fori(0, B // 2 - 1) as i:
                for s in range(2):
                    sp.wait_ge(kv_done[RING - 1], RU * (2 * i + s) + RU)
                    load_ctx(sp, 2 * i + s + 2, s)
                    store(2 * i + s)
            for b in range(B - 2, B):
                store(b)
            for h in range(2):
                sp.wait_ge(stored[h], 16 * 3 * B + 1)

        @block.tensor
        def _(pe):
            def project(b, s, n):
                if n == 0:
                    pe.wait_ge(ctx_loaded[s], 8 * (b - s) + 16)
                pe.wait_ge(kv_read[n % RING], RU * b + n // RING + 1)
                for c in range(KT):
                    last = nc.tensor.matmul(kv_ps[n % RING][0:KP, :], ctxT[s][:, c, n * KP:(n + 1) * KP], wkv[:, c, :],
                                            start=(c == 0), stop=(c == KT - 1))
                last.then_inc(kv_done[n % RING], 1)

            def turn(b, x):
                pe.wait_ge(part_done[x], b + (2 if x == 2 else 1))
                for h in range(2):
                    pe.wait_ge(copied[h], 3 * b + x + 1)
                    for n in range(KN):
                        last = nc.tensor.transpose(turn_ps[h][:, n // 6, (n % 6) * KE:(n % 6) * KE + KP],
                                                   part[x][:, n, h * 128:(h + 1) * 128], ident16[0:KP, 0:KP])
                    last.then_inc(turn_done[h], 1)

            def batch(b, s, more):
                turns = {4: 0, 8: 1, 11: 2}
                if not more:
                    pe.wait_ge(dve_step, LARGEST_DONE)
                    for h in range(2):
                        last = nc.tensor.transpose(vscale_ps[:, h * KP:(h + 1) * KP], vmax[:, h * 128:(h + 1) * 128], P.ident[0:KP, 0:KP])
                    last.then_inc(vt_done, 1)
                for n in range(KN):
                    if n + RING < KN:
                        if more:
                            project(b + 1, 1 - s, n + RING)
                    elif more == 2:
                        project(b + 2, s, n + RING - KN)
                    if n in turns:
                        turn(b, turns[n])
                    if n == 6 and not more:
                        pe.wait_ge(diag_done, 1)
                        for h in range(2):
                            last = nc.tensor.matmul(vscale_ps[0:KP, 256 + h * 128:256 + (h + 1) * 128], P.ones[:, 0:KP], vdiag[:, h, :],
                                                    start=True, stop=True)
                        last.then_inc(row_done, 1)

            load_wait(pe, loaded, 2)
            pe.wait_ge(ident_ready, 1)
            for n in range(KN):
                project(0, 0, n)
            for n in range(RING):
                project(1, 1, n)
            steps(pe, batch)

        @block.gpsimd
        def _(pool):
            def khat(b, s):
                pool.wait_ge(ints_ready, b + 1)
                nc.gpsimd.tensor_tensor(by_head(kb[s][:]), by_head(ints[:]), wide(scale[s][:]), ALU.mult).then_inc(khat_done, 1)

            def batch(b, s, more):
                pool.wait_ge(part_done[1], b + 1)
                nc.gpsimd.tensor_tensor(kb[s][:], kb[s][:], part[1][:], ALU.subtract).then_inc(rest_done[1], 1)
                if more:
                    khat(b + 1, 1 - s)
            khat(0, 0)
            steps(pool, batch)

        @block.scalar
        def _(act):
            def batch(b, s, more):
                for x, source in enumerate((khat_done, rest_done[0], rest_done[1])):
                    act.wait_ge(source, b + 1)
                    nc.scalar.activation(part[x][:], kb[s][:], ACT.Copy).then_inc(part_done[x], 1)
                    for h in range(2):
                        act.wait_ge(turn_done[h], 3 * b + x + 1)
                        act.wait_ge(stored[h], 16 * (3 * b + x) + 1)
                        nc.scalar.activation(turned[h][:].rearrange("p (a n t) -> p a n t", a=2, n=6),
                                             turn_ps[h][:, :, 0:6 * KE].rearrange("p a (n t) -> p a n t", t=KE)[:, :, :, 0:KP], ACT.Copy)\
                            .then_inc(copied[h], 1)
            steps(act, batch)

        @block.vector
        def _(dve):
            def read(b, s, n):
                dve.wait_ge(kv_done[n % RING], RU * b + n // RING + 1)
                nc.vector.tensor_tensor(kb[s][:, n, :], kv_ps[n % RING][0:KP, 0:D], bkv[0:KP, 0:D], ALU.add)
                nc.vector.tensor_tensor(P.v32[:, bass.ds(b * KN + n, 1), :].rearrange("p o d -> p (o d)"),
                                        kv_ps[n % RING][0:KP, D:2 * D], bkv[0:KP, D:2 * D], ALU.add)\
                    .then_inc(kv_read[n % RING], 1)

            def steps_from(start):
                count = [0]

                def done(ins):
                    count[0] += 1
                    ins.then_inc(dve_step, 1)
                    dve.wait_ge(dve_step, start + count[0])
                return done

            def quantise(b, s, after_another):
                dve.wait_ge(kv_read[RING - 1], RU * b + RU + 1)
                done = steps_from(6 * b + 1)
                done(nc.vector.tensor_reduce(scale[s][:].rearrange("p n h -> p (n h)"), by_head(kb[s][:]), X_AXIS, ALU.max,
                                             apply_absolute_value=True))
                done(nc.vector.tensor_scalar(scale[s][:], scale[s][:], 1.0 / 127.0, 1e-8, ALU.mult, ALU.max))
                done(nc.vector.reciprocal(inv[s][:], scale[s][:]))
                if after_another:
                    dve.wait_ge(khat_done, b)
                done(nc.vector.tensor_tensor(by_head(ints[:]), by_head(kb[s][:]), wide(inv[s][:]), ALU.mult))
                nc.vector.tensor_scalar(ints[:], ints[:], ROUND, -ROUND, ALU.add, ALU.add).then_inc(ints_ready, 1)

            def largest(b):
                done = steps_from(6 * b + 5)
                done(nc.vector.tensor_reduce(row[:], P.v32[:, bass.ds(b * KN, KN), :].rearrange("p n d -> p d n"), X_AXIS, ALU.max,
                                             apply_absolute_value=True))
                done(nc.vector.tensor_tensor(vmax[:], vmax[:], row[:], ALU.max))

            def batch(b, s, more):
                if more:
                    dve.wait_ge(part_done[2], b + 1)
                for n in range(KN):
                    if more:
                        read(b + 1, 1 - s, n)
                    if n == 3:
                        largest(b)
                    if n == 6:
                        dve.wait_ge(part_done[0], b + 1)
                        nc.vector.tensor_tensor(kb[s][:], kb[s][:], part[0][:], ALU.subtract).then_inc(rest_done[0], 1)
                if more:
                    quantise(b + 1, 1 - s, True)

            dve.wait_ge(loaded, 32)
            nc.vector.tensor_copy(ident16[:], P.ident[:]).then_inc(ident_ready, 1)
            nc.vector.memset(vmax[:], 0.0).then_inc(dve_step, 1)
            for n in range(KN):
                read(0, 0, n)
            quantise(0, 0, False)
            steps(dve, batch)
            done = steps_from(LARGEST_DONE)
            dve.wait_ge(vt_done, 1)
            done(nc.vector.tensor_reduce(P.v_scale[:], vscale_ps[:, 0:2 * KP].rearrange("p (h t) -> p h t", h=2), X_AXIS, ALU.max))
            done(nc.vector.tensor_scalar(P.v_scale[:], P.v_scale[:], 1.0 / 127.0, 1e-8, ALU.mult, ALU.max))
            done(nc.vector.reciprocal(vinv[:], P.v_scale[:]))
            for h in range(2):
                last = nc.vector.tensor_scalar(vdiag[:, h, :], P.ident[:], vinv[:, h:h + 1], None, ALU.mult)
            last.then_inc(diag_done, 1)
            dve.wait_ge(row_done, 1)
            done(nc.vector.tensor_copy(row[:], vscale_ps[0:KP, 256:256 + D]))
            dve.wait_ge(khat_done, B)
            for b in range(B):
                done(nc.vector.tensor_tensor(ints[:], P.v32[:, b * KN:(b + 1) * KN, :], row[:].unsqueeze(1).broadcast_to([KP, KN, D]), ALU.mult))
                done(nc.vector.tensor_scalar(P.v8[:, b * KN:(b + 1) * KN, :], ints[:], ROUND, -ROUND, ALU.add, ALU.add))


def xattn3_queries(P):
    nc, dram = P.nc, P.dram
    with Stage(nc, "xa3q") as st:
        wq, bq = st.sb("wq", [128, KT, D]), st.sb("bq", [128, D])
        q, qi, = st.sb("q", [TT, NT, D]), st.sb("qi", [TT, NT, D])
        scale, inv = st.sb("scale", [TT, NT, H]), st.sb("inv", [TT, NT, H])
        part = [st.sb(f"part{x}", [TT, NT, D], BF16) for x in range(3)]
        ident16 = st.sb("ident16", [128, 128], BF16)
        partT = st.sb("partT", [128, 3, 2, N_TOK], BF16)
        q_ps = st.ps("q_ps", [128, NT, D])
        turn_ps = [st.ps(f"turn{r}", [128, 1024], BF16) for r in range(2)]
        loaded, q_done, dve_step = st.sem("loaded"), st.sem("q_done"), st.sem("dve_step")
        parts_done, turn_done, copied, stored = st.sem("parts_done"), st.sem("turn_done"), st.sem("copied"), st.sem("stored")
        block = st.block()

        @block.sync
        def _(sp):
            sp.dma_start(wq[:], dram["x3_wq"].rearrange("(c p) n -> p c n", p=128)).then_inc(loaded, 16)
            sp.dma_start(bq[:], dram["x3_bq"]).then_inc(loaded, 16)
            for x in range(3):
                sp.wait_ge(copied, 2 * x + 2)
                sp.dma_start(P.qT_dram[x].rearrange("(h p) t -> p h t", p=128), partT[:, x]).then_inc(stored, 16)
            sp.wait_ge(stored, 48)

        @block.tensor
        def _(pe):
            load_wait(pe, loaded, 2)
            for j in range(NT):
                for c in range(KT):
                    last = nc.tensor.matmul(q_ps[0:TT, j, :], P.xnT[:, c, j * TT:(j + 1) * TT], wq[:, c, :],
                                            start=(c == 0), stop=(c == KT - 1))
            last.then_inc(q_done, 1)
            pe.wait_ge(parts_done, 1)
            for x in range(3):
                for h in range(2):
                    k = 2 * x + h
                    if k >= 2:
                        pe.wait_ge(copied, k - 1)
                    for j in range(NT):
                        last = nc.tensor.transpose(turn_ps[k % 2][:, j * TT:(j + 1) * TT], part[x][:, j, h * 128:(h + 1) * 128],
                                                   ident16[0:TT, 0:TT])
                    last.then_inc(turn_done, 1)

        @block.scalar
        def _(act):
            for k in range(6):
                act.wait_ge(turn_done, k + 1)
                nc.scalar.activation(partT[:, k // 2, k % 2, :], turn_ps[k % 2][:, 0:N_TOK], ACT.Copy).then_inc(copied, 1)

        @block.vector
        def _(dve):
            link = in_order(dve, dve_step)
            load_wait(dve, loaded, 2)
            nc.vector.tensor_copy(ident16[:], P.ident[:])
            dve.wait_ge(q_done, 1)
            link(nc.vector.tensor_tensor(q[:], q_ps[0:TT], bq[0:TT, :].unsqueeze(1).broadcast_to([TT, NT, D]), ALU.add))
            link(nc.vector.tensor_scalar(q[:], q[:], 0.25, None, ALU.mult))

            def groups(t):
                return t.rearrange("p j (h e) -> p (j h) e", e=HD)

            def wide(t):
                return t.rearrange("p j h -> p (j h)").unsqueeze(2).broadcast_to([TT, NT * H, HD])
            link(nc.vector.tensor_reduce(scale[:].rearrange("p j h -> p (j h)"), groups(q[:]), X_AXIS, ALU.max, apply_absolute_value=True))
            link(nc.vector.tensor_scalar(scale[:], scale[:], 1.0 / 127.0, 1e-8, ALU.mult, ALU.max))
            link(nc.vector.reciprocal(inv[:], scale[:]))
            link(nc.vector.tensor_tensor(groups(qi[:]), groups(q[:]), wide(inv[:]), ALU.mult))
            link(nc.vector.tensor_scalar(qi[:], qi[:], ROUND, -ROUND, ALU.add, ALU.add))
            link(nc.vector.tensor_tensor(groups(q[:]), groups(qi[:]), wide(scale[:]), ALU.mult))
            for x in range(2):
                link(nc.vector.tensor_copy(part[x][:], q[:]))
                link(nc.vector.tensor_tensor(q[:], q[:], part[x][:], ALU.subtract))
            nc.vector.tensor_copy(part[2][:], q[:]).then_inc(parts_done, 1)


def attend_order(*streams):
    return [(name, k) for _, name, k in sorted((first + k * step, name, k) for name, count, first, step in streams for k in range(count))]


def xattn3_attend(P):
    nc = P.nc
    NK = B * KN
    CHUNK = 2 * KC
    NC = B * T // CHUNK
    NA = NT * NC
    NG = NK // 3
    PER_A, PER_G = NA // 2, NG // 2
    QUARTERS = 4
    GQ = NG // QUARTERS
    QROWS, MROWS = 6 * HD, 3
    K_PART, Q_PART = (0, 0, 0, 1, 1, 2), (0, 1, 2, 0, 1, 0)
    AHEAD, PE_AHEAD = 4, 6
    A_STEP = NG / NA
    PE_ORDER = [("first", NA, 0.9, A_STEP), ("keys", NG, 1.25, 1.0), ("weigh", NG, 2.1, 1.0), ("turn", 1, 31.24, 1.0)]
    ACT_ORDER = [("first", NA, 0.4, A_STEP), ("exp", NG, 0.0, 1.0), ("rows", 1, 31.7, 1.0), ("corr", 1, 30.1, 1.0)]
    DVE_ORDER = [("first", NA, -0.2, A_STEP), ("round", NG, 0.85, 1.0), ("split", 1, 29.6, 1.0), ("den", 1, 31.6, 1.0)]
    with Stage(nc, "xa3a") as st:
        kS = [st.sb(f"kS{s}", [128, B * T], BF16) for s in range(2)]
        qA = [st.sb(f"qA{s}", [128, N_TOK], BF16) for s in range(2)]
        qB = [st.sb(f"qB{s}", [128, N_TOK], BF16) for s in range(2)]
        vpad = P.vpad
        zeros, ones16 = st.sb("zeros", [KP, N_TOK], BF16), st.sb("ones16", [KP, HD], BF16)
        ident16 = st.sb("ident16", [128, 128], BF16)
        e = [st.sb(f"e{r}", [KP, 3, N_TOK]) for r in range(2)]
        r8 = [st.sb(f"r8{r}", [KP, 3, N_TOK], BF16) for r in range(2)]
        negmax, esum = ([st.sb(f"{n}{s}", [TT, NT, NC]) for s in range(2)] for n in ("negmax", "esum"))
        diff, corr = st.sb("diff", [TT, NT, NC]), st.sb("corr", [TT, NT, NC])
        negm, m_rest = st.sb("negm", [TT, NT]), st.sb("m_rest", [TT, NT])
        m_parts = st.sb("m_parts", [TT, NT, MROWS], BF16)
        den, rden_h = st.sb("den", [TT, NT]), st.sb("rden_h", [TT, NT])
        ln255 = st.sb("ln255", [128, 1])
        first_ps = [st.ps(f"first{p}", [128, 2, 512]) for p in range(2)]
        keys_ps = st.ps("keys", [128, 3, 512])
        out_ps = st.ps("out", [128, 512])
        mT_ps = keys_ps[QROWS:QROWS + MROWS, 0, :].bitcast(BF16)
        prep, ones_rows, vpad_ready = st.sem("prep"), st.sem("ones_rows"), st.sems("vpad_ready", 2)
        qA_loaded, qB_loaded = st.sems("qA_loaded", 2), st.sems("qB_loaded", 2)
        k_loaded = [st.sems(f"k_loaded{s}_", QUARTERS) for s in range(2)]
        first_scored, first_summed, max_done = st.sems("first_scored", 2), st.sems("first_summed", 2), st.sem("max_done")
        keys_scored, keys_exp = st.sem("keys_scored"), st.sem("keys_exp")
        split_done, mT_done, m_ready = st.sem("split_done"), st.sem("mT_done"), st.sem("m_ready")
        diff_done, corr_done = st.sem("diff_done"), st.sem("corr_done")
        round_done, pv_done = st.sems("round_done", 2), st.sems("pv_done", 2)
        dve_step, half_done, half_read = st.sem("dve_step"), st.sem("half_done"), st.sem("half_read")
        pool_step = st.sem("pool_step")
        st.start_at_one(first_summed, keys_exp, round_done, pv_done)
        block = st.block()

        @block.sync
        def _(sp):
            def load_queries(t, loaded, row):
                for g in range(6):
                    sp.dma_start(t[g * HD:(g + 1) * HD, :], P.qT_dram[Q_PART[g], bass.ds(row, HD), :]).then_inc(loaded, 16)

            def load_keys(s, quarter, row):
                b0, nb = quarter * B // QUARTERS, B // QUARTERS
                for g in range(6):
                    sp.dma_start(kS[s][g * HD:(g + 1) * HD, b0 * T:(b0 + nb) * T].rearrange("p (b t) -> p b t", b=nb),
                                 P.kT_dram[K_PART[g], bass.ds(row, HD), b0:b0 + nb, :]).then_inc(k_loaded[s][quarter], 16)
            for s in range(2):
                load_queries(qA[s], qA_loaded[s], s * HD)
                for quarter in range(QUARTERS):
                    load_keys(s, quarter, s * HD)
                load_queries(qB[s], qB_loaded[s], s * HD)
            with sp.Fori(0, H // 2 - 1) as i:
                for s in range(2):
                    h = 2 * i + s
                    sp.wait_ge(first_scored[1], PER_A * h + PER_A)
                    load_queries(qA[s], qA_loaded[s], (h + 2) * HD)
                    for quarter in range(QUARTERS):
                        sp.wait_ge(keys_scored, NG * h + GQ * (quarter + 1))
                        load_keys(s, quarter, (h + 2) * HD)
                    load_queries(qB[s], qB_loaded[s], (h + 2) * HD)

        @block.gpsimd
        def _(pool):
            link = in_order(pool, pool_step)
            ones_wide = ones16[:].unsqueeze(1).broadcast_to([KP, NK, HD])
            fill = in_order(pool, ones_rows)
            fill(nc.gpsimd.memset(kS[0][QROWS:, B * T // 2:], 1.0))
            fill(nc.gpsimd.memset(kS[1][QROWS:, :], 1.0))
            link(nc.gpsimd.memset(ones16[:], 1.0))
            for s in range(2):
                link(nc.gpsimd.memset(vpad[s], 0.0))
            for s in range(2):
                nc.gpsimd.tensor_tensor(vpad[s][:, :, s * HD:(s + 1) * HD], P.v8[:, :, s * HD:(s + 1) * HD], ones_wide, ALU.mult)\
                    .then_inc(vpad_ready[s], 1)
            with pool.Fori(0, H // 2 - 1) as i:
                for s in range(2):
                    h = 2 * i + s
                    pool.wait_ge(pv_done[1], PER_G * h + PER_G + 1)
                    nc.gpsimd.tensor_tensor(vpad[s][:, :, bass.ds(i % 4 * (2 * HD) + s * HD, HD)], P.v8[:, :, 0:HD], P.v8[:, :, 0:HD],
                                            ALU.subtract).then_inc(pool_step, 1)
                    pool.wait_ge(pool_step, 3 + h + 1)
                    nc.gpsimd.tensor_tensor(vpad[s][:, :, bass.ds((i + 1) % 4 * (2 * HD) + s * HD, HD)], P.v8[:, :, bass.ds((h + 2) * HD, HD)],
                                            ones_wide, ALU.mult).then_inc(vpad_ready[s], 1)

        @block.tensor
        def _(pe):
            def first(h, s, hs, a):
                p, c, j = a % 2, a // NT, a % NT
                if a == 0:
                    pe.wait_ge(qA_loaded[s], 96 * hs + 96)
                if a % (NA // QUARTERS) == 0:
                    pe.wait_ge(k_loaded[s][a // (NA // QUARTERS)], 96 * hs + 96)
                pe.wait_ge(first_summed[p], PER_A * h + a // 2 + 1)
                for k in range(2):
                    t0 = c * CHUNK + k * KC
                    last = nc.tensor.matmul(first_ps[p][0:TT, k, 0:KC], qA[s][:, j * TT:(j + 1) * TT],
                                            kS[s][:, t0:t0 + KC], start=True, stop=True)
                last.then_inc(first_scored[p], 1)

            def turn(h):
                pe.wait_ge(split_done, h + 1)
                pe.wait_ge(keys_exp, NG * h + 1)
                for j in range(NT):
                    last = nc.tensor.transpose(mT_ps[:, j * TT:(j + 1) * TT], m_parts[:, j, :], ident16[0:TT, 0:TT])
                last.then_inc(mT_done, 1)

            def keys(h, s, hs, g):
                if g == 0:
                    pe.wait_ge(m_ready, h + 1)
                    pe.wait_ge(qB_loaded[s], 96 * hs + 96)
                pe.wait_ge(keys_exp, NG * h + g + 1)
                for k in range(3):
                    t0 = (3 * g + k) * KP
                    last = nc.tensor.matmul(keys_ps[0:KP, k, 0:N_TOK], kS[s][:, t0:t0 + KP], qB[s][:], start=True, stop=True)
                last.then_inc(keys_scored, 1)

            def weigh(h, s, hs, g):
                if g == 0:
                    pe.wait_ge(vpad_ready[s], hs + 1)
                pe.wait_ge(round_done[g % 2], PER_G * h + g // 2 + 2)
                for k in range(3):
                    last = nc.tensor.matmul(out_ps[:, 0:N_TOK], vpad[s][:, 3 * g + k, :], r8[g % 2][:, k, :],
                                            start=False, stop=False, skip_group_check=True)
                last.then_inc(pv_done[g % 2], 1)

            def head(i, s, more=2):
                h = 2 * i + s
                following, then = (h + 1, 1 - s, i + s), (h + 2, s, i + 1)
                for what, k in attend_order(*PE_ORDER):
                    if what == "first" and k + PE_AHEAD < NA and more:
                        first(*following, k + PE_AHEAD)
                    elif what == "first" and k + PE_AHEAD >= NA and more == 2:
                        first(*then, k + PE_AHEAD - NA)
                    elif what == "turn" and more:
                        turn(h + 1)
                    elif what == "keys" and k + 2 < NG:
                        keys(h, s, i, k + 2)
                    elif what == "keys" and more:
                        keys(*following, k + 2 - NG)
                    elif what == "weigh":
                        weigh(h, s, i, k)

            pe.wait_ge(prep, 1)
            pe.wait_ge(ones_rows, 1)
            for a in range(NA):
                first(0, 0, 0, a)
            pe.wait_ge(ones_rows, 2)
            for a in range(AHEAD):
                first(1, 1, 0, a)
                if a == 1:
                    turn(0)
            keys(0, 0, 0, 0)
            for a in range(AHEAD, AHEAD + 2):
                first(1, 1, 0, a)
            keys(0, 0, 0, 1)
            for a in range(AHEAD + 2, PE_AHEAD):
                first(1, 1, 0, a)
            for half in range(2):
                if half:
                    pe.wait_ge(half_read, 1)
                nc.tensor.matmul(out_ps[:, 0:N_TOK], zeros[:, 0:128], zeros[:], start=True, stop=False, skip_group_check=True)
                with pe.Fori(4 * half, 4 + 3 * half) as i:
                    for s in range(2):
                        head(i, s)
                if half:
                    head(H // 2 - 1, 0, more=1)
                    head(H // 2 - 1, 1, more=0)
                nc.tensor.matmul(out_ps[:, 0:N_TOK], zeros[:, 0:128], zeros[:], start=False, stop=True, skip_group_check=True)\
                    .then_inc(half_done, 1)

        @block.scalar
        def _(act):
            def first(h, s, a):
                p, c, j = a % 2, a // NT, a % NT
                act.wait_ge(max_done, NA * h + a + 1)
                nc.scalar.activation(first_ps[p][0:TT, :, 0:KC], first_ps[p][0:TT, :, 0:KC], ACT.Exp,
                                     bias=negmax[s][:, j, c:c + 1], accum_out=esum[s][:, j, c:c + 1]).then_inc(first_summed[p], 1)

            def rows(h, s):
                act.wait_ge(mT_done, h + 1)
                nc.scalar.activation(qB[s][QROWS:QROWS + MROWS, :], mT_ps[:, 0:N_TOK], ACT.Copy).then_inc(m_ready, 1)

            def correction(h):
                act.wait_ge(diff_done, h + 1)
                nc.scalar.activation(corr[:], diff[:], ACT.Exp).then_inc(corr_done, 1)

            def exponential(h, g):
                act.wait_ge(keys_scored, NG * h + g + 1)
                act.wait_ge(round_done[g % 2], PER_G * h + g // 2 + 1)
                nc.scalar.activation(e[g % 2][:], keys_ps[0:KP, :, 0:N_TOK], ACT.Exp, bias=ln255[0:KP, :]).then_inc(keys_exp, 1)

            def head(i, s, more=2):
                h = 2 * i + s
                for what, k in attend_order(*ACT_ORDER):
                    if what == "exp":
                        exponential(h, k)
                    elif what == "first" and k + AHEAD < NA and more:
                        first(h + 1, 1 - s, k + AHEAD)
                    elif what == "first" and k + AHEAD >= NA and more == 2:
                        first(h + 2, s, k + AHEAD - NA)
                    elif what == "rows" and more:
                        rows(h + 1, 1 - s)
                    elif what == "corr" and more:
                        correction(h + 1)

            act.wait_ge(prep, 1)
            for a in range(NA):
                first(0, 0, a)
            for a in range(AHEAD):
                first(1, 1, a)
                if a == 0:
                    rows(0, 0)
                    correction(0)
            for half in range(2):
                with act.Fori(4 * half, 4 + 3 * half) as i:
                    for s in range(2):
                        head(i, s)
                if half:
                    head(H // 2 - 1, 0, more=1)
                    head(H // 2 - 1, 1, more=0)

        @block.vector
        def _(dve):
            def first(h, s, a):
                p, c, j = a % 2, a // NT, a % NT
                dve.wait_ge(first_scored[p], PER_A * h + a // 2 + 1)
                nc.vector.tensor_reduce(negmax[s][:, j, c:c + 1], first_ps[p][0:TT, :, 0:KC], XY_AXES, ALU.max, negate=True)\
                    .then_inc(max_done, 1)

            def split(h, s):
                steps = [0]

                def done(ins):
                    steps[0] += 1
                    ins.then_inc(dve_step, 1)
                    dve.wait_ge(dve_step, 8 * h + steps[0])
                dve.wait_ge(max_done, NA * h + NA)
                done(nc.vector.tensor_reduce(negm[:], negmax[s][:], X_AXIS, ALU.min))
                done(nc.vector.tensor_copy(m_parts[:, :, 0], negm[:]))
                done(nc.vector.tensor_tensor(m_rest[:], negm[:], m_parts[:, :, 0], ALU.subtract))
                done(nc.vector.tensor_copy(m_parts[:, :, 1], m_rest[:]))
                done(nc.vector.tensor_tensor(m_rest[:], m_rest[:], m_parts[:, :, 1], ALU.subtract))
                nc.vector.tensor_copy(m_parts[:, :, 2], m_rest[:]).then_inc(split_done, 1)
                nc.vector.tensor_tensor(diff[:], negm[:].unsqueeze(2).broadcast_to([TT, NT, NC]), negmax[s][:], ALU.subtract)\
                    .then_inc(diff_done, 1)

            def denominators(h, s):
                steps = [5]

                def done(ins):
                    steps[0] += 1
                    ins.then_inc(dve_step, 1)
                    dve.wait_ge(dve_step, 8 * h + steps[0])
                dve.wait_ge(corr_done, h + 1)
                done(nc.vector.tensor_tensor(corr[:], corr[:], esum[s][:], ALU.mult))
                done(nc.vector.tensor_reduce(den[:], corr[:], X_AXIS, ALU.add))
                done(nc.vector.reciprocal(rden_h[:], den[:]))
                nc.vector.tensor_scalar(P.rden[:, :, bass.ds(h, 1)].rearrange("p j o -> p (j o)"), rden_h[:], 1.0 / 255.0, None, ALU.mult)

            def rounded(h, g):
                dve.wait_ge(keys_exp, NG * h + g + 2)
                dve.wait_ge(pv_done[g % 2], PER_G * h + g // 2 + 1)
                nc.vector.tensor_scalar(r8[g % 2][:], e[g % 2][:], ROUND, -ROUND, ALU.add, ALU.add).then_inc(round_done[g % 2], 1)

            def head(i, s, more=2):
                h = 2 * i + s
                for what, k in attend_order(*DVE_ORDER):
                    if what == "round":
                        rounded(h, k)
                    elif what == "first" and k + AHEAD < NA and more:
                        first(h + 1, 1 - s, k + AHEAD)
                    elif what == "first" and k + AHEAD >= NA and more == 2:
                        first(h + 2, s, k + AHEAD - NA)
                    elif what == "split" and more:
                        split(h + 1, 1 - s)
                    elif what == "den" and more:
                        denominators(h + 1, 1 - s)

            nc.vector.memset(kS[0][QROWS:, :B * T // 2], 1.0)
            for s in range(2):
                nc.vector.memset(qA[s][QROWS:, :], 0.0)
                nc.vector.memset(qB[s][QROWS:, :], 0.0)
            nc.vector.memset(zeros[:], 0.0)
            nc.vector.memset(ln255[:], math.log(255.0))
            nc.vector.tensor_copy(ident16[:], P.ident[:]).then_inc(prep, 1)
            for a in range(NA):
                first(0, 0, a)
            split(0, 0)
            for a in range(AHEAD):
                first(1, 1, a)
            denominators(0, 0)
            for half in range(2):
                with dve.Fori(4 * half, 4 + 3 * half) as i:
                    for s in range(2):
                        head(i, s)
                if half:
                    head(H // 2 - 1, 0, more=1)
                    head(H // 2 - 1, 1, more=0)
                dve.wait_ge(half_done, half + 1)
                nc.vector.tensor_scalar(P.oT[:, half, :], out_ps[:, 0:N_TOK], P.v_scale[:, half:half + 1], None, ALU.mult).then_inc(half_read, 1)


def xattn3_out(P):
    nc, dram = P.nc, P.dram
    with Stage(nc, "xa3o") as st:
        wp, bp = st.sb("wp", [128, 2, D]), st.sb("bp", [128, D])
        wide = st.sb("wide", [TT, NT, D])
        delta = st.sb("delta", [TT, NT, D])
        turn_ps = [st.ps(f"turn{h}", [128, 512]) for h in range(2)]
        o_ps = st.ps("o", [128, NT, D])
        loaded, wide_done, turn_done, oT_ready, o_done = (
            st.sem(n) for n in ("loaded", "wide_done", "turn_done", "oT_ready", "o_done"))
        dve_step = st.sem("dve_step")
        block = st.block()

        @block.sync
        def _(sp):
            sp.dma_start(wp[:], dram["x3_wp"].rearrange("(c p) n -> p c n", p=128)).then_inc(loaded, 16)
            sp.dma_start(bp[:], dram["x3_bp"]).then_inc(loaded, 16)

        @block.tensor
        def _(pe):
            pe.wait_ge(wide_done, 1)
            for h in range(2):
                for j in range(NT):
                    last = nc.tensor.transpose(turn_ps[h][:, j * TT:(j + 1) * TT], wide[:, j, h * 128:(h + 1) * 128],
                                               P.ident[0:TT, 0:TT])
                last.then_inc(turn_done, 1)
            load_wait(pe, loaded, 2)
            pe.wait_ge(oT_ready, 2)
            for j in range(NT):
                for h in range(2):
                    last = nc.tensor.matmul(o_ps[0:TT, j, :], P.oT[:, h, j * TT:(j + 1) * TT], wp[:, h, :],
                                            start=(h == 0), stop=(h == 1))
            last.then_inc(o_done, 1)

        @block.vector
        def _(dve):
            link = in_order(dve, dve_step)
            nc.vector.tensor_copy(wide[:].rearrange("p j (h e) -> p (j h) e", e=HD),
                                  P.rden[:].rearrange("p j h -> p (j h)").unsqueeze(2).broadcast_to([TT, NT * H, HD])).then_inc(wide_done, 1)
            for h in range(2):
                dve.wait_ge(turn_done, h + 1)
                nc.vector.tensor_tensor(P.oT[:, h, :], P.oT[:, h, :], turn_ps[h][:, 0:N_TOK], ALU.mult).then_inc(oT_ready, 1)
            dve.wait_ge(o_done, 1)
            link(nc.vector.tensor_tensor(delta[:], o_ps[0:TT], bp[0:TT, :].unsqueeze(1).broadcast_to([TT, NT, D]), ALU.add))
            nc.vector.scalar_tensor_tensor(P.x[:], delta[:], P.gates[0:TT, 3:4], P.x[:], ALU.mult, ALU.add)


def finish_stage(P):
    with Stage(P.nc, "finish") as st:
        stored = st.sem("stored")
        block = st.block()

        @block.sync
        def _(sp):
            sp.dma_start(P.out.rearrange("(j p) d -> p j d", p=TT), P.x[:]).then_inc(stored, 16)
            sp.wait_ge(stored, 16)


def build_program(nc, dram, out):
    P = Program(nc, dram, out)
    with ExitStack() as stack:
        def sb(name, shape, dt=FP32):
            return stack.enter_context(nc.sbuf_tensor("s_" + name, shape, dt))
        P.x, P.xn = sb("x", [TT, NT, D]), sb("xn", [TT, NT, D])
        P.xnT = sb("xnT", [128, KT, N_TOK])
        P.ident, P.ones = sb("ident", [128, 128]), sb("ones", [128, 128])
        P.head_mask, P.iota = sb("head_mask", [128, 8]), sb("iota", [128, 32])
        P.gates = sb("gates", [128, 9])
        setup_stage(P)
        stages = [
            lambda: xattn0_stage(P),
            lambda: ffn_stage(P, 0, 8, 8, 96, "softmax_of_top", list(range(8))),
            lambda: xattn1_stage(P),
            lambda: ffn_stage(P, 1, 32, 32, 96, "top8", list(range(32))),
            lambda: xattn2_stage(P),
            lambda: ffn_stage(P, 2, 8, 20, 88, "softmax", [e for e in range(8) for _ in range(2)] + [None] * 4),
            lambda: xattn3_stage(P),
            lambda: ffn_stage(P, 3, 16, 18, 128, "sigmoid", list(range(16)) + [None] * 2, biased=True),
        ]
        for k, stage in enumerate(stages):
            if k not in STAGES:
                continue
            stage()
        finish_stage(P)


STAGES = range(8)


def laid_out(i):
    A = np.ascontiguousarray
    d = {}
    i = {k: np.asarray(v) for k, v in i.items()}

    def rows(a):
        return np.broadcast_to(a, (128, a.size))

    def halves(a):
        return a.reshape(2, 128).T
    p = np.arange(128)
    d["x"] = i["x"].reshape(N_TOK, D)
    d["ctxT"] = i["ctx_2048"].transpose(0, 2, 1)
    d["ident"] = np.eye(128, dtype=np.float32)
    d["head_mask"] = (p[:, None] // HD == np.arange(8)[None]).astype(np.float32)
    d["iota"] = np.broadcast_to(np.arange(32, dtype=np.float32), (128, 32))
    d["g_xattn"], d["g_ffn"] = rows(i["g_xattn"]), rows(i["g_ffn"])
    d["rs"] = rows(i["L0_xattn_residual_scale"].reshape(1))
    for n, s in (("wq", "Wq"), ("wk", "Wk"), ("wv", "Wv")):
        d[f"x0_{n}"] = i[f"L0_xattn_{s}"].T
    wo = np.zeros((4, 32, 4, D), np.float32)
    wo[:, 0:HD] = i["L0_xattn_Wo"].T.reshape(4, 4, HD, D).transpose(1, 2, 0, 3)
    d["x0_wo"] = wo.reshape(128, 4, D)
    d["den_pick"] = (p[:, None] == p[None] // 32 * 32 + HD).astype(np.float32)
    d["x0_bq"], d["x0_bk"] = halves(i["L0_xattn_bq"]), halves(i["L0_xattn_bk"])
    for n, s in (("bv", "bv"), ("bo", "bo"), ("gamma", "ln_gamma"), ("beta", "ln_beta")):
        d[f"x0_{n}"] = rows(i[f"L0_xattn_{s}"])
    d["mask0"] = i["mask_BxS2_ik0"].reshape(B * KN, KP).T

    def gate_up(g, u):
        a = np.stack([g, u], 2)
        return a.reshape(a.shape[0], KT, 128, 2, a.shape[-1]).transpose(0, 2, 1, 3, 4).reshape(a.shape[0], 128, -1)

    def tr(a):
        return a.transpose(0, 2, 1)
    d["f0_router"] = i["L0_ffn_w_gate_router"].T
    d["f0_w_in"] = gate_up(tr(i["L0_ffn_w_gate_proj"]), tr(i["L0_ffn_w_up_proj"]))
    d["f0_w_down"] = tr(i["L0_ffn_w_down_proj"])
    d["f1_router"] = i["L1_ffn_gate_w"].T
    d["f1_w_in"] = gate_up(tr(i["L1_ffn_Wg"]), tr(i["L1_ffn_Wu"]))
    d["f1_w_down"] = tr(i["L1_ffn_Wd"])

    def blocks(a, f):
        e, dd, w = a.shape
        return a.reshape(e, dd, w // f, f).transpose(0, 2, 1, 3).reshape(e * w // f, dd, f)
    F = 88
    g = np.concatenate([blocks(i["L2_ffn_We_gate"], F), blocks(i["L2_ffn_Ws_gate"][None], F)])
    u = np.concatenate([blocks(i["L2_ffn_We_up"], F), blocks(i["L2_ffn_Ws_up"][None], F)])
    d["f2_router"] = i["L2_ffn_W_router"]
    d["f2_w_in"] = gate_up(g, u)
    d["f2_w_down"] = np.concatenate([i["L2_ffn_We_down"].reshape(-1, F, D), i["L2_ffn_Ws_down"].reshape(-1, F, D)])
    c3 = lambda r, s: np.concatenate([i[f"L3_ffn_{r}"], i[f"L3_ffn_{s}"]])
    d["f3_router"] = i["L3_ffn_wa"]
    d["f3_w_in"] = np.concatenate([gate_up(c3("rg", "sg"), c3("rw1", "sw1")), c3("rgb", "sgb")[:, :, None],
                                   c3("rb1", "sb1")[:, :, None]], 2)
    d["f3_w_down"] = c3("rw2", "sw2")
    d["f3_b_down"] = c3("rb2", "sb2")
    wq = i["L1_xattn_Wq"].reshape(D, 4, 4, HD).transpose(0, 2, 1, 3)
    d["x1_wq"] = wq.reshape(D, D)
    d["x1_wk"], d["x1_wv"] = i["L1_xattn_Wk"], i["L1_xattn_Wv"]
    wo = np.zeros((4, 32, 4, D), np.float32)
    wo[:, 0:HD] = i["L1_xattn_Wo"].reshape(4, 4, HD, D).transpose(0, 2, 1, 3)
    d["x1_wo"] = wo.reshape(128, 4, D)
    d["mask1"] = i["mask_BxS2_bf1"].view(np.uint8)
    d["mask1_cols"] = d["mask1"].reshape(B * KN, KP).T
    slope = (np.float32(2.0 ** -0.5) ** np.arange(1, H + 1, dtype=np.float32)).astype(np.float32)

    def bf16_parts(a):
        parts = []
        for _ in range(3):
            bits = a.view(np.uint32)
            parts.append(((bits + 0x7fff + (bits >> 16 & 1)) & np.uint32(0xffff0000)).view(np.float32))
            a = a - parts[-1]
        return np.stack(parts)
    q_rows = np.zeros((13, H, S), np.float32)
    q_rows[3:6] = q_rows[6:9] = bf16_parts(slope)[:, :, None]
    q_rows[9:12] = bf16_parts(-slope[:, None] * np.arange(S, dtype=np.float32))
    q_rows[12] = 1
    d["x1_q_rows"] = q_rows.reshape(13, H * S)
    position = np.arange(T, dtype=np.float32)
    k_rows = np.zeros((13, T), np.float32)
    k_rows[0:3] = k_rows[9:12] = 1
    k_rows[3:6], k_rows[6:9] = position - position % 8, position % 8
    d["x1_k_rows"] = k_rows
    d["x2_wq"], d["x2_wg"], d["x2_wkv"], d["x2_wo"] = (i[f"L2_xattn_{s}"].T for s in ("Wq", "Wg", "Wkv", "Wo"))
    d["x2_bg"] = halves(i["L2_xattn_bg"])
    d["block_mask"] = (p[:, None] // HD == p[None] // HD).astype(np.float32)
    d["x3_wq"], d["x3_wp"] = i["L3_xattn_Wq"], i["L3_xattn_Wp"]
    d["x3_wkv"] = i["L3_xattn_Wkv"]
    d["x3_bq"], d["x3_bp"], d["x3_bkv"] = rows(i["L3_xattn_bq"]), rows(i["L3_xattn_bp"]), rows(i["L3_xattn_bkv"])
    return {k: A(v) for k, v in d.items()}


def kernel(**inputs):
    import concourse.bacc as bacc
    from concourse.bass_utils import run_bass_kernel_spmd

    nc = bacc.Bacc("TRN2", target_bir_lowering=False, num_devices=1)
    arrays = laid_out(inputs)
    dram = {k: nc.dram_tensor("in_" + k, a.shape, mybir.dt.from_np(a.dtype), kind="ExternalInput").ap() for k, a in arrays.items()}
    out = nc.dram_tensor("out", (N_TOK, D), FP32, kind="ExternalOutput").ap()
    build_program(nc, dram, out)
    got = run_bass_kernel_spmd(nc, [{"in_" + k: a for k, a in arrays.items()}], core_ids=[0])
    return got.results[0]["out"].reshape(B, S, D)
```
